# Optimizing a Trainium2 kernel written in Bass

```python
import numpy as np
import jax
import jax.numpy as jnp

def _softmax(x, axis=-1):
    return jax.nn.softmax(x, axis=axis)

def _gelu(x):
    return jax.nn.gelu(x, approximate=True)

def _silu(x):
    return jax.nn.silu(x)

def _sigmoid(x):
    return jax.nn.sigmoid(x)

def _layernorm(x, axis=-1, eps=1e-05):
    m = jnp.mean(x, axis=axis, keepdims=True)
    v = jnp.var(x, axis=axis, keepdims=True)
    return (x - m) / jnp.sqrt(v + eps)

def _scatter_add(tgt, idx, src, axis=0):
    return tgt.at[idx].add(src)

def _segment_sum(src, seg, n):
    return jax.ops.segment_sum(src, seg, n)
kernel_name = 'mk_cond_resid_d4_seqx_r4_44df15'

def setup_inputs(seed: int=0):
    np.random.seed(seed)
    _w = jnp.asarray

    def _rec_inputs():
        import jax
        import jax.numpy as jnp
        _rk = jax.random.key(seed)
        x = -7.109e-05 + 0.9999 * jax.random.normal(jax.random.fold_in(_rk, 1), (8, 512, 256), jnp.float32)
        _lenS = 512 - jax.random.randint(jax.random.fold_in(_rk, 7), (8,), 0, max(1, 512 // 4) + 1, jnp.int32)
        _lenS2 = 512 - jax.random.randint(jax.random.fold_in(_rk, 8), (8,), 0, max(1, 512 // 4) + 1, jnp.int32)
        cond_1024 = -0.00356592 + 0.997978 * jax.random.normal(jax.random.fold_in(_rk, 11), (8, 256), jnp.float32)
        return (x, cond_1024)
    x, cond_1024 = _rec_inputs()

    def _L0_cond_setup():
        import jax, jax.numpy as jnp
        import numpy as np
        N, T, D, H = (128, 128, 256, 256)
        key = jax.random.key(seed)
        k1, k2, k3, k4 = jax.random.split(key, 4)
        x = jax.random.normal(k1, (N, T, D), dtype=jnp.float32)
        h0 = jax.random.normal(k2, (N, H), dtype=jnp.float32)
        Wx = jax.random.normal(k3, (D, H), dtype=jnp.float32) / np.sqrt(D)
        Wh = jax.random.normal(k4, (H, H), dtype=jnp.float32) / np.sqrt(H)
        b = jnp.zeros((H,), dtype=jnp.float32)
        return {'x': x, 'h0': h0, 'Wx': Wx, 'Wh': Wh, 'b': b}
    _L0_cond_all = _L0_cond_setup()
    _L0_cond_in = {k: v for k, v in _L0_cond_all.items() if k in ('Wx', 'Wh', 'b')}
    del _L0_cond_all

    def _L1_cond_setup():
        import jax, jax.numpy as jnp
        import numpy as np
        N, T, D, H = (64, 128, 256, 256)

        def lstm_scan(x, h0, Wx, Wh, b):
            xW = jnp.einsum('ntd,dg->ntg', x, Wx) + b
            Hdim = h0.shape[1]
            c0 = jnp.zeros_like(h0)

            def step(carry, xw_t):
                prev_h, prev_c = carry
                a = xw_t + prev_h @ Wh
                i = jax.nn.sigmoid(a[:, :Hdim])
                f = jax.nn.sigmoid(a[:, Hdim:2 * Hdim])
                o = jax.nn.sigmoid(a[:, 2 * Hdim:3 * Hdim])
                g = jnp.tanh(a[:, 3 * Hdim:])
                next_c = f * prev_c + i * g
                next_h = o * jnp.tanh(next_c)
                return ((next_h, next_c), next_h)
            _, hs = jax.lax.scan(step, (h0, c0), jnp.swapaxes(xW, 0, 1))
            return jnp.swapaxes(hs, 0, 1)
        key = jax.random.key(seed)
        k1, k2, k3, k4 = jax.random.split(key, 4)
        x = jax.random.normal(k1, (N, T, D), dtype=jnp.float32)
        h0 = jax.random.normal(k2, (N, H), dtype=jnp.float32)
        Wx = jax.random.normal(k3, (D, 4 * H), dtype=jnp.float32) / np.sqrt(D)
        Wh = jax.random.normal(k4, (H, 4 * H), dtype=jnp.float32) / np.sqrt(H)
        b = jnp.zeros((4 * H,), dtype=jnp.float32)
        return {'x': x, 'h0': h0, 'Wx': Wx, 'Wh': Wh, 'b': b}
    _L1_cond_all = _L1_cond_setup()
    _L1_cond_in = {k: v for k, v in _L1_cond_all.items() if k in ('Wx', 'Wh', 'b')}
    del _L1_cond_all

    def _L2_cond_setup():
        import math
        import jax, jax.numpy as jnp
        import numpy as np
        EPS = 1e-07
        MAX_TANH_ARG = 1.0 - 1e-05

        def _norm(x):
            return jnp.sqrt(jnp.sum(x * x, axis=-1, keepdims=True)).clip(EPS)

        def logmap0(x):
            n = _norm(x)
            return jnp.arctanh(jnp.clip(n, EPS, MAX_TANH_ARG)) * x / n

        def expmap0(v):
            n = _norm(v)
            return jnp.tanh(n) * v / n

        def mobius_add(x, y):
            x2 = jnp.sum(x * x, -1, keepdims=True)
            y2 = jnp.sum(y * y, -1, keepdims=True)
            xy = jnp.sum(x * y, -1, keepdims=True)
            num = (1 + 2 * xy + y2) * x + (1 - x2) * y
            den = (1 + 2 * xy + x2 * y2).clip(EPS)
            return num / den

        def plin(x, w, b):
            return expmap0(logmap0(x) @ w + b)

        def layer_norm(x, eps=1e-06):
            m = x.mean(-1, keepdims=True)
            v = ((x - m) ** 2).mean(-1, keepdims=True)
            return (x - m) / jnp.sqrt(v + eps)

        def _beta(a, b):
            return math.exp(math.lgamma(a) + math.lgamma(b) - math.lgamma(a + b))
        D, H, FF = (256, 16, 1024)
        HD = D // H
        BETA_N = _beta(D / 2, 0.5)
        BETA_H = _beta(HD / 2, 0.5)

        def _to_heads(p):
            B, S, _ = p.shape
            t = logmap0(p).reshape(B, S, H, HD) * (BETA_H / BETA_N)
            return expmap0(jnp.transpose(t, (0, 2, 1, 3)))

        def _from_heads(ph):
            B, _, S, _ = ph.shape
            t = logmap0(ph) * (BETA_N / BETA_H)
            t = jnp.transpose(t, (0, 2, 1, 3)).reshape(B, S, D)
            return expmap0(t)
        key = jax.random.key(seed)
        ks = jax.random.split(key, 20)
        B, S = (4, 256)
        x = expmap0(0.02 * jax.random.normal(ks[0], (B, S, D), jnp.float32))
        t_emb = jax.random.normal(ks[1], (B, 1, D), jnp.float32)
        g = lambda k, sh: 0.02 * jax.random.normal(k, sh, jnp.float32)
        return {'x': x, 't_emb': t_emb, 'w_q': g(ks[2], (D, D)), 'b_q': jnp.zeros((D,), jnp.float32), 'w_k': g(ks[3], (D, D)), 'b_k': jnp.zeros((D,), jnp.float32), 'w_v': g(ks[4], (D, D)), 'b_v': jnp.zeros((D,), jnp.float32), 'w_o': g(ks[5], (D, D)), 'b_o': jnp.zeros((D,), jnp.float32), 'w_f1': g(ks[6], (D, FF)), 'b_f1': jnp.zeros((FF,), jnp.float32), 'w_f2': g(ks[7], (FF, D)), 'b_f2': jnp.zeros((D,), jnp.float32), 'w_ada': g(ks[8], (D, 6 * D)), 'b_ada': jnp.zeros((6 * D,), jnp.float32)}
    _L2_cond_all = _L2_cond_setup()
    _L2_cond_in = {k: v for k, v in _L2_cond_all.items() if k in ('w_q', 'b_q', 'w_k', 'b_k', 'w_v', 'b_v', 'w_o', 'b_o', 'w_f1', 'b_f1', 'w_f2', 'b_f2', 'w_ada', 'b_ada')}
    del _L2_cond_all

    def _L3_cond_setup():
        import jax, jax.numpy as jnp
        import numpy as np
        NUM_EXPERTS = 4
        TOP_K = 2
        key = jax.random.key(seed)
        ks = jax.random.split(key, 16)
        B, L, D, E, H = (8, 192, 256, NUM_EXPERTS, 1024)
        s = 0.02
        return {'context_c': jax.random.normal(ks[0], (B, L, D), jnp.float32), 'time_cond': jax.random.normal(ks[1], (B, D), jnp.float32), 'gate_w': jax.random.normal(ks[2], (3 * D, E), jnp.float32) * s, 'gate_b': jnp.zeros((E,), jnp.float32), 'time_w': jax.random.normal(ks[3], (D, 2 * E), jnp.float32) * s, 'time_b': jnp.zeros((2 * E,), jnp.float32), 'ew1': jax.random.normal(ks[4], (E, D, H), jnp.float32) * s, 'eb1': jnp.zeros((E, H), jnp.float32), 'ew2': jax.random.normal(ks[5], (E, H, D), jnp.float32) * s, 'eb2': jnp.zeros((E, D), jnp.float32), 'sw1': jax.random.normal(ks[6], (D, H), jnp.float32) * s, 'sb1': jnp.zeros((H,), jnp.float32), 'sw2': jax.random.normal(ks[7], (H, D), jnp.float32) * s, 'sb2': jnp.zeros((D,), jnp.float32)}
    _L3_cond_all = _L3_cond_setup()
    _L3_cond_in = {k: v for k, v in _L3_cond_all.items() if k in ('gate_w', 'gate_b', 'time_w', 'time_b', 'ew1', 'eb1', 'ew2', 'eb2', 'sw1', 'sb1', 'sw2', 'sb2')}
    del _L3_cond_all
    return {'x': x, 'cond_1024': cond_1024, 'L0_cond_Wx': _L0_cond_in['Wx'], 'L0_cond_Wh': _L0_cond_in['Wh'], 'L0_cond_b': _L0_cond_in['b'], 'L1_cond_Wx': _L1_cond_in['Wx'], 'L1_cond_Wh': _L1_cond_in['Wh'], 'L1_cond_b': _L1_cond_in['b'], 'L2_cond_w_q': _L2_cond_in['w_q'], 'L2_cond_b_q': _L2_cond_in['b_q'], 'L2_cond_w_k': _L2_cond_in['w_k'], 'L2_cond_b_k': _L2_cond_in['b_k'], 'L2_cond_w_v': _L2_cond_in['w_v'], 'L2_cond_b_v': _L2_cond_in['b_v'], 'L2_cond_w_o': _L2_cond_in['w_o'], 'L2_cond_b_o': _L2_cond_in['b_o'], 'L2_cond_w_f1': _L2_cond_in['w_f1'], 'L2_cond_b_f1': _L2_cond_in['b_f1'], 'L2_cond_w_f2': _L2_cond_in['w_f2'], 'L2_cond_b_f2': _L2_cond_in['b_f2'], 'L2_cond_w_ada': _L2_cond_in['w_ada'], 'L2_cond_b_ada': _L2_cond_in['b_ada'], 'L3_cond_gate_w': _L3_cond_in['gate_w'], 'L3_cond_gate_b': _L3_cond_in['gate_b'], 'L3_cond_time_w': _L3_cond_in['time_w'], 'L3_cond_time_b': _L3_cond_in['time_b'], 'L3_cond_ew1': _L3_cond_in['ew1'], 'L3_cond_eb1': _L3_cond_in['eb1'], 'L3_cond_ew2': _L3_cond_in['ew2'], 'L3_cond_eb2': _L3_cond_in['eb2'], 'L3_cond_sw1': _L3_cond_in['sw1'], 'L3_cond_sb1': _L3_cond_in['sb1'], 'L3_cond_sw2': _L3_cond_in['sw2'], 'L3_cond_sb2': _L3_cond_in['sb2']}

def reference(x, cond_1024, L0_cond_Wx, L0_cond_Wh, L0_cond_b, L1_cond_Wx, L1_cond_Wh, L1_cond_b, L2_cond_w_q, L2_cond_b_q, L2_cond_w_k, L2_cond_b_k, L2_cond_w_v, L2_cond_b_v, L2_cond_w_o, L2_cond_b_o, L2_cond_w_f1, L2_cond_b_f1, L2_cond_w_f2, L2_cond_b_f2, L2_cond_w_ada, L2_cond_b_ada, L3_cond_gate_w, L3_cond_gate_b, L3_cond_time_w, L3_cond_time_b, L3_cond_ew1, L3_cond_eb1, L3_cond_ew2, L3_cond_eb2, L3_cond_sw1, L3_cond_sb1, L3_cond_sw2, L3_cond_sb2):
    import jax
    import jax.numpy as jnp

    def _L0_cond_ref(x, h0, Wx, Wh, b):
        import jax, jax.numpy as jnp
        import numpy as np
        N, T, D, H = (128, 128, 256, 256)
        xp = jnp.einsum('ntd,dh->nth', x, Wx) + b

        def step(prev_h, xp_t):
            next_h = jnp.tanh(xp_t + prev_h @ Wh)
            return (next_h, next_h)
        _, hs = jax.lax.scan(step, h0, jnp.swapaxes(xp, 0, 1))
        return jnp.swapaxes(hs, 0, 1)

    def _L1_cond_ref(x, h0, Wx, Wh, b):
        import jax, jax.numpy as jnp
        import numpy as np
        N, T, D, H = (64, 128, 256, 256)

        def lstm_scan(x, h0, Wx, Wh, b):
            xW = jnp.einsum('ntd,dg->ntg', x, Wx) + b
            Hdim = h0.shape[1]
            c0 = jnp.zeros_like(h0)

            def step(carry, xw_t):
                prev_h, prev_c = carry
                a = xw_t + prev_h @ Wh
                i = jax.nn.sigmoid(a[:, :Hdim])
                f = jax.nn.sigmoid(a[:, Hdim:2 * Hdim])
                o = jax.nn.sigmoid(a[:, 2 * Hdim:3 * Hdim])
                g = jnp.tanh(a[:, 3 * Hdim:])
                next_c = f * prev_c + i * g
                next_h = o * jnp.tanh(next_c)
                return ((next_h, next_c), next_h)
            _, hs = jax.lax.scan(step, (h0, c0), jnp.swapaxes(xW, 0, 1))
            return jnp.swapaxes(hs, 0, 1)
        return lstm_scan(x, h0, Wx, Wh, b)

    def _L2_cond_ref(x, t_emb, w_q, b_q, w_k, b_k, w_v, b_v, w_o, b_o, w_f1, b_f1, w_f2, b_f2, w_ada, b_ada):
        import math
        import jax, jax.numpy as jnp
        import numpy as np
        EPS = 1e-07
        MAX_TANH_ARG = 1.0 - 1e-05

        def _norm(x):
            return jnp.sqrt(jnp.sum(x * x, axis=-1, keepdims=True)).clip(EPS)

        def logmap0(x):
            n = _norm(x)
            return jnp.arctanh(jnp.clip(n, EPS, MAX_TANH_ARG)) * x / n

        def expmap0(v):
            n = _norm(v)
            return jnp.tanh(n) * v / n

        def mobius_add(x, y):
            x2 = jnp.sum(x * x, -1, keepdims=True)
            y2 = jnp.sum(y * y, -1, keepdims=True)
            xy = jnp.sum(x * y, -1, keepdims=True)
            num = (1 + 2 * xy + y2) * x + (1 - x2) * y
            den = (1 + 2 * xy + x2 * y2).clip(EPS)
            return num / den

        def plin(x, w, b):
            return expmap0(logmap0(x) @ w + b)

        def layer_norm(x, eps=1e-06):
            m = x.mean(-1, keepdims=True)
            v = ((x - m) ** 2).mean(-1, keepdims=True)
            return (x - m) / jnp.sqrt(v + eps)

        def _beta(a, b):
            return math.exp(math.lgamma(a) + math.lgamma(b) - math.lgamma(a + b))
        D, H, FF = (256, 16, 1024)
        HD = D // H
        BETA_N = _beta(D / 2, 0.5)
        BETA_H = _beta(HD / 2, 0.5)

        def _to_heads(p):
            B, S, _ = p.shape
            t = logmap0(p).reshape(B, S, H, HD) * (BETA_H / BETA_N)
            return expmap0(jnp.transpose(t, (0, 2, 1, 3)))

        def _from_heads(ph):
            B, _, S, _ = ph.shape
            t = logmap0(ph) * (BETA_N / BETA_H)
            t = jnp.transpose(t, (0, 2, 1, 3)).reshape(B, S, D)
            return expmap0(t)
        ada = t_emb @ w_ada + b_ada
        sh_msa, sc_msa, g_msa, sh_mlp, sc_mlp, g_mlp = jnp.split(ada, 6, axis=-1)
        residual = x
        xn = layer_norm(logmap0(x))
        xm = expmap0(xn * (1 + sc_msa) + sh_msa)
        q = _to_heads(plin(xm, w_q, b_q))
        k = _to_heads(plin(xm, w_k, b_k))
        v = _to_heads(plin(xm, w_v, b_v))
        qt, kt, vt = (logmap0(q), logmap0(k), logmap0(v))
        scores = jnp.einsum('bhqd,bhkd->bhqk', qt, kt) / math.sqrt(HD)
        attn = jax.nn.softmax(scores, axis=-1)
        out_h = expmap0(jnp.einsum('bhqk,bhkd->bhqd', attn, vt))
        attn_out = plin(_from_heads(out_h), w_o, b_o)
        attn_t = g_msa * logmap0(attn_out)
        x = mobius_add(residual, expmap0(attn_t))
        residual = x
        xn = layer_norm(logmap0(x))
        xm = expmap0(xn * (1 + sc_mlp) + sh_mlp)
        ff = plin(plin(xm, w_f1, b_f1), w_f2, b_f2)
        ff_t = g_mlp * logmap0(ff)
        return mobius_add(residual, expmap0(ff_t))

    def _L3_cond_ref(context_c, time_cond, gate_w, gate_b, time_w, time_b, ew1, eb1, ew2, eb2, sw1, sb1, sw2, sb2):
        import jax, jax.numpy as jnp
        import numpy as np
        NUM_EXPERTS = 4
        TOP_K = 2
        B, L, D = context_c.shape
        E, K = (NUM_EXPERTS, TOP_K)
        L_head = L_wrist = L // 3
        head = context_c[:, :L_head]
        wrist = context_c[:, L_head:L_head + L_wrist]
        proprio = context_c[:, L_head + L_wrist:]
        full_agg = context_c.mean(axis=1)
        hp_agg = jnp.concatenate([head, proprio], axis=1).mean(axis=1)
        wp_agg = jnp.concatenate([wrist, proprio], axis=1).mean(axis=1)
        gate_in = jnp.concatenate([full_agg, hp_agg, wp_agg], axis=-1)
        gate_logits = gate_in @ gate_w + gate_b
        mod = jax.nn.silu(time_cond) @ time_w + time_b
        scale, shift = jnp.split(mod, 2, axis=-1)
        gate_logits = gate_logits * (1.0 + scale) + shift
        gate_scores = jax.nn.softmax(gate_logits, axis=-1)
        topk_w, topk_i = jax.lax.top_k(gate_scores, K)
        topk_w = topk_w / (topk_w.sum(axis=-1, keepdims=True) + 1e-08)
        onehot = (topk_i[..., None] == jnp.arange(E)[None, None, :]).astype(context_c.dtype)
        w_be = jnp.sum(topk_w[..., None] * onehot, axis=1)
        mask = np.ones((E, L), dtype=np.float32)
        mask[1, L_head:L_head + L_wrist] = 0.0
        mask[2, :L_head] = 0.0
        mask = jnp.asarray(mask)
        out = jnp.zeros_like(context_c)
        for e in range(E):
            h = jax.nn.gelu(context_c @ ew1[e] + eb1[e], approximate=True)
            y = h @ ew2[e] + eb2[e]
            out = out + w_be[:, e][:, None, None] * mask[e][None, :, None] * y
        shared = jax.nn.gelu(context_c @ sw1 + sb1, approximate=True) @ sw2 + sb2
        return out + shared
    x = x + _L0_cond_ref(x, cond_1024, L0_cond_Wx, L0_cond_Wh, L0_cond_b)
    x = x + _L1_cond_ref(x, cond_1024, L1_cond_Wx, L1_cond_Wh, L1_cond_b)
    x = x + _L2_cond_ref(x, cond_1024[:, None, :], L2_cond_w_q, L2_cond_b_q, L2_cond_w_k, L2_cond_b_k, L2_cond_w_v, L2_cond_b_v, L2_cond_w_o, L2_cond_b_o, L2_cond_w_f1, L2_cond_b_f1, L2_cond_w_f2, L2_cond_b_f2, L2_cond_w_ada, L2_cond_b_ada)
    x = x + _L3_cond_ref(x, cond_1024, L3_cond_gate_w, L3_cond_gate_b, L3_cond_time_w, L3_cond_time_b, L3_cond_ew1, L3_cond_eb1, L3_cond_ew2, L3_cond_eb2, L3_cond_sw1, L3_cond_sb1, L3_cond_sw2, L3_cond_sb2)
    return x

_drawn_inputs = setup_inputs


def setup_inputs(seed=0):
    import zlib

    import numpy as np

    out = dict(_drawn_inputs(seed))
    spreads = {'L0_cond_b': (0.0, 0.1),
     'L1_cond_b': (0.0, 0.1),
     'L2_cond_b_q': (0.0, 0.1),
     'L2_cond_b_k': (0.0, 0.1),
     'L2_cond_b_v': (0.0, 0.1),
     'L2_cond_b_o': (0.0, 0.1),
     'L2_cond_b_f1': (0.0, 0.1),
     'L2_cond_b_f2': (0.0, 0.1),
     'L2_cond_b_ada': (0.0, 0.1),
     'L3_cond_gate_b': (0.0, 0.1),
     'L3_cond_time_b': (0.0, 0.1),
     'L3_cond_eb1': (0.0, 0.1),
     'L3_cond_eb2': (0.0, 0.1),
     'L3_cond_sb1': (0.0, 0.1),
     'L3_cond_sb2': (0.0, 0.1)}
    factors = {}
    for name, (base, spread) in spreads.items():
        noise = np.random.default_rng([zlib.crc32(name.encode()), seed]).standard_normal(out[name].shape)
        drawn = base * np.exp(spread * noise) if base else spread * noise
        out[name] = jnp.asarray(drawn.astype(out[name].dtype))
    for name, factor in factors.items():
        out[name] = (out[name] * factor).astype(out[name].dtype)
    return out
```

```python
import concourse.bass as bass
from concourse import mybir
from contextlib import ExitStack

fp32 = mybir.dt.float32
fp16 = mybir.dt.float16
u32 = mybir.dt.uint32
ALU = mybir.AluOpType
ACT = mybir.ActivationFunctionType
AX = mybir.AxisListType

import math
import numpy as np

P = 128
NB, T, D = 8, 512, 256
KC = D // P
GATES = 4 * D // P
CH = 16
NCH = T // CH
H, HD = 16, 16
FF = 1024
FC = FF // P
E, TOPK = 4, 2
NQ = T // P
EPS = 1e-7
MAXT = float(np.float32(1.0 - 1e-5))
ATMAX = math.atanh(MAXT)
beta = lambda a, b: math.exp(math.lgamma(a) + math.lgamma(b) - math.lgamma(a + b))
TO_HEADS = beta(HD / 2, 0.5) / beta(D / 2, 0.5)
FROM_HEADS = 1.0 / TO_HEADS
SEG = T // 3
SEGS = [(0, SEG), (SEG, 2 * SEG), (2 * SEG, T)]
W16_EXP = 14


class Lane:

    def __init__(self, nc, name, eng, sem, events):
        self.name, self.eng, self.sem, self.events = name, eng, sem, events
        self.count, self.seen = 0, {}

    def done(self, ins, event):
        self.count += 1
        ins.then_inc(self.sem, 1)
        self.events[event] = (self.sem, self.count)
        return ins

    def need(self, *events):
        for event in events:
            if event is None:
                continue
            sem, count = self.events[event]
            if self.seen.get(sem.name, 0) < count:
                self.eng.wait_ge(sem, count)
                self.seen[sem.name] = count


class Core:

    def __init__(self, nc, ctx):
        self.nc, self.events = nc, {}
        self.sem = lambda n: ctx.enter_context(nc.semaphore(n))
        mk = lambda n, e: Lane(nc, n, e, self.sem("n_" + n), self.events)
        self.pe, self.act, self.dve = mk("pe", nc.tensor), mk("act", nc.scalar), mk("dve", nc.vector)
        self.pool, self.sp = mk("pool", nc.gpsimd), mk("sp", nc.sync)
        self.lanes = [self.pe, self.act, self.dve, self.pool, self.sp]
        self.dma_sems, self.dma_used = {}, {}
        self.gather = self.sem("gather")
        self.release = {l.name: self.sem("go_" + l.name) for l in self.lanes if l is not self.pool}

    def dma(self, lane, stream, out, in_, event):
        if stream not in self.dma_sems:
            self.dma_sems[stream] = self.sem("dma_" + stream)
            self.dma_used[stream] = 0
        self.dma_used[stream] += 16
        lane.eng.dma_start(out, in_).then_inc(self.dma_sems[stream], 16)
        self.events[event] = (self.dma_sems[stream], self.dma_used[stream])

    def barrier(self):
        pool = self.pool
        for stream, used in self.dma_used.items():
            if used:
                pool.eng.wait_ge(self.dma_sems[stream], used)
        for lane in self.lanes:
            if lane is not pool:
                lane.eng.drain().then_inc(self.gather, 1)
        pool.eng.drain().then_inc(self.gather, 1)
        pool.eng.wait_ge(self.gather, len(self.lanes))
        for lane in self.lanes:
            if lane.count:
                pool.eng.sem_inc(lane.sem, -lane.count)
        for stream, used in self.dma_used.items():
            if used:
                pool.eng.sem_inc(self.dma_sems[stream], -used)
            self.dma_used[stream] = 0
        pool.eng.sem_inc(self.gather, -len(self.lanes))
        for lane in self.lanes:
            if lane is not pool:
                pool.eng.sem_inc(self.release[lane.name], 1)
        for lane in self.lanes:
            if lane is not pool:
                lane.eng.wait_ge(self.release[lane.name], 1)
                lane.eng.sem_inc(self.release[lane.name], -1)
            lane.count, lane.seen = 0, {}
        self.events.clear()


def run(lane, event, needs, issue):
    lane.need(*needs)
    return lane.done(issue(lane.eng), event)


def recurrences(nc, core, ctx, A, XT):
    pe, act, dve, pool, sp = core.pe, core.act, core.dve, core.pool, core.sp
    with ExitStack() as mem:
        sb = lambda n, s, d=fp32: mem.enter_context(nc.sbuf_tensor(n, s, d))
        ps = lambda n: mem.enter_context(nc.psum_tensor(n, [P, 512], fp32))
        wx0 = sb("wx0", [P, KC, D])
        wx1 = sb("wx1", [P, KC, 4 * D])
        wh0 = sb("wh0", [P, KC, D])
        wh1 = sb("wh1", [P, KC, 4 * D])
        wh0p = sb("wh0p", [P, 2, KC, D], fp16)
        wh1p = sb("wh1p", [P, 2, KC, 4 * D], fp16)
        b0 = sb("b0", [P, KC])
        b1 = sb("b1", [1, 4 * D])
        ones = sb("ones", [1, CH * NB])
        ident = sb("ident", [P, P])
        scaled_ident = [sb(f"scaled_ident{l}", [P, P]) for l in range(2)]
        cond = sb("cond", [P, KC, NB])
        xw0 = sb("xw0", [P, KC, T, NB])
        xw1 = sb("xw1", [P, GATES, CH, NB])
        ext = sb("ext", [P, 2, 2])
        mx = sb("mx", [P, 2])
        descale = sb("descale", [P, 2])
        scale = sb("scale", [P, 2])
        hR = sb("hR", [P, KC, CH, NB])
        hL = sb("hL", [P, KC, CH, NB])
        hpR = sb("hpR", [P, KC, 2, NB], fp16)
        hpL = sb("hpL", [P, KC, 2, NB], fp16)
        cell = sb("cell", [P, KC, NB])
        preL = sb("preL", [P, GATES, NB])
        preR = sb("preR", [P, KC, NB])
        sg = sb("sg", [P, GATES, NB])
        u = sb("u", [P, KC, NB])
        w = sb("w", [P, KC, NB])
        tc = sb("tc", [P, KC, NB])
        psL_ifg, psL_o, psR = ps("psL_ifg"), ps("psL_o"), ps("psR")
        psX = [ps(f"psX{i}") for i in range(2)]

        for n, (dst, src) in enumerate([(wh1, "L1_cond_Wh"), (wh0, "L0_cond_Wh"), (wx0, "L0_cond_Wx"), (wx1, "L1_cond_Wx")]):
            core.dma(sp, "w", dst[:, :, :], A[src].rearrange("(k p) n -> p k n", p=P), ("loaded", src))
        core.dma(act, "x", XT[:, :, :, :], A["xT"], "x loaded")
        core.dma(sp, "w", cond[:, :, :], A["condT"], "cond loaded")
        core.dma(sp, "w", b0[:, :], A["b0T"], "b0 loaded")
        core.dma(sp, "w", b1[:, :], A["b1row"], "b1 loaded")
        core.dma(sp, "w", ident[:, :], A["ident"], "small loaded")
        pool.done(pool.eng.memset(ones[:, :], 1.0), "ones")
        pool.done(pool.eng.memset(cell[:, :, :], 0.0), "cell zero")

        g_cols = slice(2 * D, 3 * D)
        dve.need("small loaded")
        for t, name in ((wh1, "wh1"), (wx1, "wx1")):
            dve.done(dve.eng.tensor_scalar(t[:, :, g_cols], t[:, :, g_cols], 2.0, None, ALU.mult), name + " doubled")
        dve.done(dve.eng.tensor_scalar(b1[:, g_cols], b1[:, g_cols], 2.0, None, ALU.mult), "b1 doubled")
        dve.need("wh1 doubled")
        for l, t in enumerate((wh0, wh1)):
            dve.done(dve.eng.tensor_reduce(ext[:, l, 0:1], t[:, :, :], AX.XY, ALU.max), f"max {l}")
            dve.done(dve.eng.tensor_reduce(ext[:, l, 1:2], t[:, :, :], AX.XY, ALU.min), f"min {l}")
        dve.need("min 1")
        dve.done(dve.eng.tensor_scalar(ext[:, :, 1:2], ext[:, :, 1:2], -1.0, None, ALU.mult), "neg min")
        dve.need("neg min")
        dve.done(dve.eng.tensor_reduce(mx[:, :], ext[:, :, :], AX.X, ALU.max), "row max")
        pool.need("row max")
        pool.done(pool.eng.partition_all_reduce(scale[:, :], mx[:, :], P, bass.bass_isa.ReduceOp.max), "max all")
        dve.need("max all")
        dve.done(dve.eng.tensor_scalar(mx[:, :], scale[:, :], 1e-6, None, ALU.max), "clamped")
        dve.need("clamped")
        dve.done(dve.eng.tensor_scalar(descale[:, :].bitcast(u32), mx[:, :].bitcast(u32), 0x7F800000, None, ALU.bitwise_and), "pow2")
        dve.need("pow2")
        dve.done(dve.eng.tensor_scalar(descale[:, :], descale[:, :], 2.0 ** -W16_EXP, None, ALU.mult), "descale")
        dve.need("descale")
        dve.done(dve.eng.reciprocal(scale[:, :], descale[:, :]), "scale")
        dve.need("scale")
        for l, (t, tp) in enumerate(((wh0, wh0p), (wh1, wh1p))):
            s = scale[:, l:l + 1]
            dve.done(dve.eng.tensor_scalar(scaled_ident[l][:, :], ident[:, :], s, None, ALU.mult), f"ident {l}")
            dve.done(dve.eng.tensor_scalar(t[:, :, :], t[:, :, :], s, None, ALU.mult), f"scaled {l}")
            dve.need(f"scaled {l}")
            dve.done(dve.eng.tensor_copy(tp[:, 0], t[:, :, :]), f"hi {l}")
            dve.need(f"hi {l}")
            dve.done(dve.eng.tensor_tensor(tp[:, 1], t[:, :, :], tp[:, 0], ALU.subtract), f"lo {l}")
        dve.need("cond loaded")
        for l, hp in enumerate((hpR, hpL)):
            dve.done(dve.eng.tensor_copy(hp[:, :, 0, :], cond[:, :, :]), f"h0 hi {l}")
            dve.need(f"h0 hi {l}")
            dve.done(dve.eng.tensor_tensor(hp[:, :, 1, :], cond[:, :, :], hp[:, :, 0, :], ALU.subtract), f"h0 lo {l}")
        pe.need("small loaded")
        core.barrier()

        NX = 512 // NB
        with nc.Fori(0, T // NX) as blk:
            for m in range(KC):
                for k in range(KC):
                    last = pe.eng.matmul(psX[m][:, :], wx0[:, k, m * P:(m + 1) * P],
                                         XT[:, k, bass.ds(blk * NX, NX), :], start=k == 0, stop=k == KC - 1)
                pe.done(last, ("xw0", m))
                lane = (act, dve)[m]
                lane.need(("xw0", m))
                dst, src = xw0[:, m, bass.ds(blk * NX, NX), :], psX[m][:, :].rearrange("p (t b) -> p t b", b=NB)
                if m == 0:
                    lane.done(act.eng.activation(dst, src, ACT.Identity, bias=b0[:, m:m + 1]), ("xw0 out", m))
                else:
                    lane.done(dve.eng.tensor_scalar(dst, src, b0[:, m:m + 1], None, ALU.add), ("xw0 out", m))
            core.barrier()

        def parts_view(bank, slots):
            return bank[:, 0:slots * 2 * NB].rearrange("p (g q b) -> p g q b", q=2, b=NB)

        vR, vIFG, vO = parts_view(psR, KC), parts_view(psL_ifg, 6), parts_view(psL_o, 2)

        def inject(v, l, src, event):
            pe.done(pe.eng.matmul(v[:, :, 0, :], scaled_ident[l][:, :], src, start=True, stop=False, skip_group_check=True), event)

        def inject_lstm(s):
            pe.need(("pre ifg", s - 1) if s else None)
            inject(vIFG, 1, xw1[:, 0:6, s, :], ("inject ifg", s))
            pe.need(("pre o", s - 1) if s else None)
            inject(vO, 1, xw1[:, 6:8, s, :], ("inject o", s))

        def inject_rnn(s, i):
            pe.need(("pre R", s - 1) if s else None)
            inject(vR, 0, xw0[:, :, bass.ds(i * CH + s, 1), :], ("inject R", s))

        def products(v, wp, hp, g0, event):
            slots = v.shape[1]
            for g in range(slots):
                for k in range(KC):
                    for q in range(2):
                        last = pe.eng.matmul(v[:, g, :, :], wp[:, q, k, (g0 + g) * P:(g0 + g + 1) * P], hp[:, k, :, :],
                                             start=False, stop=(k == KC - 1 and q == 1), skip_group_check=True)
            pe.done(last, event)

        def add_parts(dst, halves):
            return dve.eng.tensor_reduce(dst, halves.rearrange("p g q b -> p g b q"), AX.X, ALU.add)

        def chunk(i, rnn, lstm, xw):
            ev = core.events
            prev = lambda name, s: (name, s - 1) if s else None
            if lstm:
                inject_lstm(0)
            if rnn:
                inject_rnn(0, i)
            for s in range(CH):
                if lstm:
                    pe.need(prev("hL parts", s))
                    products(vIFG, wh1p, hpL, 0, ("ifg", s))
                    products(vO, wh1p, hpL, 6, ("o", s))
                if rnn:
                    pe.need(prev("hR parts", s))
                    products(vR, wh0p, hpR, 0, ("R", s))
                if xw:
                    g, half = divmod(s, 2)
                    dst = psX[g // 4][:, (g % 4) * CH * NB:(g % 4 + 1) * CH * NB]
                    xs = lambda k: XT[:, k, bass.ds((i - 1) * CH, CH), :]
                    if half == 0:
                        pe.eng.matmul(dst, b1[:, g * P:(g + 1) * P], ones[:, :], start=True, stop=False)
                        last = pe.eng.matmul(dst, wx1[:, 0, g * P:(g + 1) * P], xs(0), start=False, stop=False)
                    else:
                        last = pe.eng.matmul(dst, wx1[:, 1, g * P:(g + 1) * P], xs(1), start=False, stop=True)
                    pe.done(last, ("xw1", s))
                if lstm:
                    dve.need(("ifg", s))
                    if s:
                        dve.need(("sig ifg", s - 1), ("sig o", s - 1))
                    dve.done(add_parts(preL[:, 0:6, :], vIFG), ("pre ifg", s))
                    dve.need(("o", s))
                    dve.done(add_parts(preL[:, 6:8, :], vO), ("pre o", s))
                    if s:
                        act.need(("hL lo", s - 1))
                    act.need(("pre ifg", s))
                    act.done(act.eng.activation(sg[:, 0:6, :], preL[:, 0:6, :], ACT.Sigmoid, scale=descale[:, 1:2]), ("sig ifg", s))
                    act.need(("pre o", s))
                    act.done(act.eng.activation(sg[:, 6:8, :], preL[:, 6:8, :], ACT.Sigmoid, scale=descale[:, 1:2]), ("sig o", s))
                if rnn:
                    dve.need(("R", s))
                    if s:
                        dve.need(("hR", s - 1))
                    dve.done(add_parts(preR[:, :, :], vR), ("pre R", s))
                    act.need(("pre R", s))
                    act.done(act.eng.activation(hR[:, :, s, :], preR[:, :, :], ACT.Tanh, scale=descale[:, 0:1]), ("hR", s))
                if s + 1 < CH:
                    if lstm:
                        inject_lstm(s + 1)
                    if rnn:
                        inject_rnn(s + 1, i)
                if lstm:
                    dve.need(("sig ifg", s))
                    dve.done(dve.eng.scalar_tensor_tensor(u[:, :, :], sg[:, 4:6, :], -0.5, sg[:, 0:2, :], ALU.add, ALU.mult), ("u", s))
                    dve.done(dve.eng.tensor_tensor(w[:, :, :], sg[:, 2:4, :], cell[:, :, :], ALU.mult), ("w", s))
                    dve.need(("w", s))
                    dve.done(dve.eng.scalar_tensor_tensor(cell[:, :, :], u[:, :, :], 2.0, w[:, :, :], ALU.mult, ALU.add), ("c", s))
                    act.need(("c", s))
                    act.done(act.eng.activation(tc[:, :, :], cell[:, :, :], ACT.Tanh), ("tanh c", s))
                if rnn:
                    dve.need(("hR", s), ("R", s))
                    dve.done(dve.eng.tensor_copy(hpR[:, :, 0, :], hR[:, :, s, :]), ("hR hi", s))
                    dve.need(("hR hi", s))
                    dve.done(dve.eng.tensor_tensor(hpR[:, :, 1, :], hR[:, :, s, :], hpR[:, :, 0, :], ALU.subtract), ("hR parts", s))
                if lstm:
                    dve.need(("tanh c", s), ("sig o", s))
                    dve.done(dve.eng.tensor_tensor(hL[:, :, s, :], sg[:, 6:8, :], tc[:, :, :], ALU.mult), ("hL", s))
                    dve.done(dve.eng.tensor_tensor(hpL[:, :, 0, :], sg[:, 6:8, :], tc[:, :, :], ALU.mult), ("hL lo", s))
                    dve.need(("hL lo", s))
                    dve.done(dve.eng.tensor_tensor(hpL[:, :, 1, :], hL[:, :, s, :], hpL[:, :, 0, :], ALU.subtract), ("hL parts", s))
                if s % 4 == 3:
                    for on, h, t0, name in ((rnn, hR, i * CH, "hR"), (lstm, hL, (i - 2) * CH, "hL")):
                        if on:
                            pool.need((name, s))
                            for k in range(KC):
                                xs = XT[:, k, bass.ds(t0 + (s - 3), 4), :]
                                pool.done(pool.eng.tensor_tensor(xs, xs, h[:, k, s - 3:s + 1, :], ALU.add), ("x", name, s, k))
            if xw:
                for n, lane in ((0, act), (1, dve)):
                    if lstm:
                        lane.need(("inject o", CH - 1))
                    lane.need(("xw1", CH - 1))
                    dst = xw1[:, 4 * n:4 * n + 4, :, :].rearrange("p g t b -> p (g t b)")
                    if n == 0:
                        act.done(act.eng.copy(dst, psX[n][:, :]), "xw1 a")
                    else:
                        dve.done(dve.eng.tensor_copy(dst, psX[n][:, :]), "xw1 b")
            core.barrier()

        chunk(0, True, False, False)
        chunk(1, True, False, True)
        with nc.Fori(2, NCH) as i:
            chunk(i, True, True, True)
        chunk(NCH, False, True, True)
        chunk(NCH + 1, False, True, False)



def load_weights(nc, core, ctx, A):
    sp, act = core.sp, core.act
    sb = lambda n, s, d=fp32: ctx.enter_context(nc.sbuf_tensor(n, s, d))
    W = {}
    sem = core.sem("weights")
    n = 0
    for name, shape in (("wqkv", [P, KC, 3 * D]), ("wo", [P, KC, D]), ("wf1", [P, KC, FF]), ("wf2", [P, FC, D]),
                        ("sw1", [P, KC, FF]), ("sw2", [P, FC, D]), ("gate_w", [P, 3 * KC, E]),
                        ("bf1", [P, FC]), ("sb1", [P, FC]), ("eb1", [P, E, FC]), ("segs", [P, 3, NQ]), ("I", [P, P])):
        W[name] = sb("W_" + name, shape)
        sp.eng.dma_start(W[name][tuple([slice(None)] * len(shape))], A[name]).then_inc(sem, 16)
        n += 16
    for name, width in (("bqkv", 3 * D), ("bo", D), ("bf2", D), ("sb2", D)):
        W[name] = sb("W_" + name, [P, width])
        sp.eng.dma_start(W[name][:, :], A[name].partition_broadcast(P)).then_inc(sem, 16)
        n += 16
    core.weights = (sem, n)
    return W


def conditioning(nc, core, A, W, ada_dram, modrow):
    pe, act, dve, pool, sp = core.pe, core.act, core.dve, core.pool, core.sp
    with ExitStack() as mem:
        sb = lambda n, s, d=fp32: mem.enter_context(nc.sbuf_tensor(n, s, d))
        wada = sb("wada", [P, KC, 6 * D])
        cond = sb("cond2", [P, KC, NB])
        silu = sb("silu", [P, KC, NB])
        timew = sb("timew", [P, KC, 2 * E])
        bada = sb("bada", [NB, 6 * D])
        timeb = sb("timeb", [1, 2 * E])
        ada = sb("ada", [NB, 6 * D])
        ps = [mem.enter_context(nc.psum_tensor(f"psA{i}", [P, 512], fp32)) for i in range(4)]
        sp.eng.wait_ge(*core.weights)
        for dst, src in ((wada[:, :, :], A["w_ada"]), (cond[:, :, :], A["condT"]), (timew[:, :, :], A["time_w"]),
                         (bada[:, :], A["b_ada"].partition_broadcast(NB)), (timeb[:, :], A["time_b"])):
            core.dma(sp, "c", dst, src, "cond in")
        pe.need("cond in")
        for j in range(3):
            for k in range(KC):
                last = pe.eng.matmul(ps[j][0:NB, :], cond[:, k, :], wada[:, k, j * 512:(j + 1) * 512], start=k == 0, stop=k == KC - 1)
            pe.done(last, ("ada", j))
            run(dve, ("ada b", j), [("ada", j), "cond in"], lambda e: e.tensor_tensor(
                ada[:, j * 512:(j + 1) * 512], ps[j][0:NB, :], bada[:, j * 512:(j + 1) * 512], ALU.add))
        for j in (1, 4):
            run(dve, ("ada 1", j), [("ada b", 2)], lambda e: e.tensor_scalar(ada[:, j * D:(j + 1) * D], ada[:, j * D:(j + 1) * D], 1.0, None, ALU.add))
        sp.need(("ada 1", 4))
        core.dma(sp, "c", ada_dram, ada[:, :], "ada out")
        act.need("cond in")
        run(act, "sigmoid", [], lambda e: e.activation(silu[:, :, :], cond[:, :, :], ACT.Sigmoid))
        run(dve, "silu", ["sigmoid"], lambda e: e.tensor_tensor(silu[:, :, :], silu[:, :, :], cond[:, :, :], ALU.mult))
        pe.need("silu")
        for b in range(NB):
            for k in range(KC):
                last = pe.eng.matmul(ps[3][0:1, b * 2 * E:(b + 1) * 2 * E], silu[:, k, b:b + 1], timew[:, k, :], start=k == 0, stop=k == KC - 1)
        pe.done(last, "mod")
        run(dve, "mod b", ["mod"], lambda e: e.tensor_tensor(
            modrow[:, :, :], ps[3][0:1, 0:NB * 2 * E].rearrange("p (b e) -> p b e", b=NB),
            timeb[:, :].unsqueeze(1).to_broadcast([1, NB, 2 * E]), ALU.add))
        run(dve, "mod 1", ["mod b"], lambda e: e.tensor_scalar(modrow[:, :, 0:E], modrow[:, :, 0:E], 1.0, None, ALU.add))
        core.barrier()


def transformer_and_experts(nc, core, A, W, XT, ada_dram, modrow, out):
    pe, act, dve, pool, sp = core.pe, core.act, core.dve, core.pool, core.sp
    with ExitStack() as mem:
        sb = lambda n, s, d=fp32: mem.enter_context(nc.sbuf_tensor(n, s, d))
        PS = [mem.enter_context(nc.psum_tensor(f"bank{i}", [P, 2, 512], fp32)) for i in range(4)]
        bank = lambda i: PS[i // 2][:, i % 2, :]
        ada = sb("adab", [P, 6, D])
        ew1 = [sb(f"ew1_{i}", [P, KC, FF]) for i in range(TOPK)]
        eb2 = [sb(f"eb2_{i}", [P, D]) for i in range(TOPK)]
        eb1 = sb("eb1s", [P, TOPK, FC])
        xT = sb("xT", [P, KC, T])
        x = sb("x", [P, NQ, D])
        x1 = sb("x1", [P, NQ, D])
        z = sb("z", [P, NQ, D])
        w = sb("w_", [P, NQ, D])
        zT = sb("zT", [P, KC, T])
        big = sb("big", [P, 2 * 2048])
        qkv = big[:, 0:NQ * 3 * D].rearrange("p (q a h d) -> p q a h d", q=NQ, a=3, h=H)
        spl = sb("spl", [P, 2, NQ, H, 4, HD], fp16)
        splT = sb("splT", [P, 2, H // 2, T], fp16)
        vt = sb("vt", [P, NQ, H, 2 * HD])
        pexp = sb("pexp", [P, 2, 4, 512])
        uT = pexp[:, :, :, :].rearrange("p a b c -> p (a b) c")
        oT = spl[:, 0].rearrange("p q h s d -> p (q h s d)").bitcast(fp32).rearrange("p (g t) -> p g t", g=H // 4)
        O = spl[:, 1].rearrange("p q h s d -> p (q h s d)").bitcast(fp32).rearrange("p (q h d) -> p q h d", q=NQ, h=H)
        ew2 = [splT[:, i].rearrange("p h t -> p (h t)").bitcast(fp32).rearrange("p (m d) -> p m d", m=FC) for i in range(TOPK)]
        pflat = pexp[:, :, :, :].rearrange("p a b c -> p (a b c)")
        st6 = sb("st6", [P, NQ, 6])
        mv = sb("mv", [P, NQ, 2])
        acc = sb("acc", [P, 8, NQ])
        S = sb("S", [P, 24, NQ])
        hs = sb("hs", [P, 4, NQ, 3 * H])
        gin = sb("gin", [P, 3, KC])
        gi = sb("gi", [P, 3, KC])
        gr = sb("gr", [1, 64])
        gidx = sb("gidx", [1, 8], u32)
        g6 = sb("g6", [1, 3 * TOPK])
        b6 = sb("b6", [P, 3 * TOPK])
        wm = sb("wm", [P, TOPK, NQ])
        ones = sb("ones_", [P, P])
        half = sb("half", [P, NQ * 3 * H])
        mhalf = sb("mhalf", [P, NQ])
        I = W["I"]
        f3 = lambda t: t.rearrange("p a b -> p (a b)")

        run(pool, "ones", [], lambda e: e.memset(ones[:, :], 1.0))
        run(pool, "half", [], lambda e: e.memset(half[:, :], 0.5))
        run(pool, "mhalf", [], lambda e: e.memset(mhalf[:, :], -0.5))
        run(pool, "vt 0", [], lambda e: e.memset(vt[:, :, :, :], 0.0))
        run(pool, "vt 1", ["vt 0"], lambda e: e.memset(vt[:, :, :, HD:HD + 1], 1.0))
        core.barrier()

        def norm_clip(tag, out_, ss, needs, halves=None):
            run(pool, tag + " sqrt", needs, lambda e: e.tensor_tensor(out_, ss, half[:, 0:NQ] if halves is None else halves, ALU.pow))
            run(dve, tag, [tag + " sqrt"], lambda e: e.tensor_scalar(out_, out_, EPS, None, ALU.max))

        def clipped_ratio(tag, out_, n, tmp, needs):
            run(dve, tag + " r", needs, lambda e: e.reciprocal(tmp, n))
            run(dve, tag, [tag + " r"], lambda e: e.scalar_tensor_tensor(out_, n, ATMAX, tmp, ALU.min, ALU.mult))

        def to_feature_major(tag, src, dst, banks, needs):
            pe.need(*needs)
            for k in range(KC):
                for q in range(NQ):
                    last = pe.eng.transpose(bank(banks[k])[:, q * P:(q + 1) * P], src[:, q, k * P:(k + 1) * P], I[:, :])
                pe.done(last, (tag, "T", k))
            run(act, (tag, 0), [(tag, "T", 0)], lambda e: e.copy(dst[:, 0, :], bank(banks[0])))
            run(dve, (tag, 1), [(tag, "T", 1)], lambda e: e.tensor_copy(dst[:, 1, :], bank(banks[1])))

        def modulated_norm(tag, xin, j, needs):
            for q in range(NQ):
                run(dve, (tag, "st", q), needs, lambda e: e.bn_stats(st6[:, q, :], xin[:, q, :]))
            for q in range(NQ):
                run(dve, (tag, "mv", q), [(tag, "st", q)], lambda e: e.bn_aggr(mv[:, q, :], st6[:, q, :]))
            mu, var = mv[:, :, 0], mv[:, :, 1]
            X2, n, m, t0, t1, al = (S[:, i, :] for i in (0, 2, 3, 4, 5, 6))
            run(dve, tag + "1", [(tag, "mv", NQ - 1)], lambda e: e.tensor_tensor(t0, mu, mu, ALU.mult))
            run(dve, tag + "2", [tag + "1"], lambda e: e.tensor_tensor(t0, t0, var, ALU.add))
            run(dve, tag + " X2", [tag + "2"], lambda e: e.tensor_scalar(X2, t0, float(D), None, ALU.mult))
            norm_clip(tag + " n", n, X2, [tag + " X2"])
            run(dve, tag + "3", [tag + " n"], lambda e: e.tensor_scalar(m, n, MAXT, None, ALU.min))
            run(dve, tag + "4", [tag + "3"], lambda e: e.tensor_scalar(t0, m, -1.0, 1.0, ALU.mult, ALU.add))
            run(dve, tag + "5", [tag + "4"], lambda e: e.reciprocal(t1, t0))
            run(dve, tag + "6", [tag + "5"], lambda e: e.scalar_tensor_tensor(t0, m, 1.0, t1, ALU.add, ALU.mult))
            run(act, tag + " ln", [tag + "6"], lambda e: e.activation(t1, t0, ACT.Ln))
            run(dve, tag + "7", [tag + " ln"], lambda e: e.reciprocal(t0, n))
            run(dve, tag + " al", [tag + "7"], lambda e: e.scalar_tensor_tensor(al, t1, 0.5, t0, ALU.mult, ALU.mult))
            run(dve, tag + "8", [tag + " al"], lambda e: e.tensor_tensor(t0, al, al, ALU.mult))
            run(dve, tag + "9", [tag + "8"], lambda e: e.tensor_tensor(t0, t0, var, ALU.mult))
            run(dve, tag + "10", [tag + "9"], lambda e: e.tensor_scalar(t0, t0, 1e-6, None, ALU.add))
            run(pool, tag + "11", [tag + "10"], lambda e: e.tensor_tensor(t1, t0, mhalf[:, :], ALU.pow))
            run(dve, tag + " r", [tag + "11"], lambda e: e.tensor_tensor(t1, t1, al, ALU.mult))
            for q in range(NQ):
                run(dve, (tag, "xn", q), [tag + " r"], lambda e: e.tensor_scalar(
                    z[:, q, :], xin[:, q, :], mv[:, q, 0:1], S[:, 5, q:q + 1], ALU.subtract, ALU.mult))
            bc = lambda row: ada[:, row, :].unsqueeze(1).to_broadcast([P, NQ, D])
            run(dve, tag + " sc", [(tag, "xn", NQ - 1), "ada"], lambda e: e.tensor_tensor(z[:, :, :], z[:, :, :], bc(j + 1), ALU.mult))
            run(dve, tag + " z", [tag + " sc"], lambda e: e.tensor_tensor(z[:, :, :], z[:, :, :], bc(j), ALU.add))
            for q in range(NQ):
                run(act, (tag, "zz", q), [tag + " z"], lambda e: e.activation(big[:, q * D:(q + 1) * D], z[:, q, :], ACT.Square, accum_out=acc[:, 0, q:q + 1]))
            norm_clip(tag + " zn", n, acc[:, 0, :], [(tag, "zz", NQ - 1)])
            clipped_ratio(tag + " s", S[:, 1, :], n, t0, [tag + " zn"])

        def mobius_update(tag, banks, bias, j, xin, xout, more, needs):
            a = z
            for q in range(NQ):
                run(dve, (tag, "a", q), needs, lambda e: e.scalar_tensor_tensor(
                    a[:, q, :], bank(banks[q // 2])[:, (q % 2) * D:(q % 2 + 1) * D], S[:, 7, q:q + 1], bias[:, :], ALU.mult, ALU.add))
                run(act, (tag, "aa", q), [(tag, "a", q)], lambda e: e.activation(big[:, q * D:(q + 1) * D], a[:, q, :], ACT.Square, accum_out=acc[:, 1, q:q + 1]))
            run(dve, tag + " w", [(tag, "a", NQ - 1)], lambda e: e.tensor_tensor(
                w[:, :, :], a[:, :, :], ada[:, j, :].unsqueeze(1).to_broadcast([P, NQ, D]), ALU.mult))
            for q in range(NQ):
                run(act, (tag, "ww", q), [tag + " w"], lambda e: e.activation(big[:, (4 + q) * D:(5 + q) * D], w[:, q, :], ACT.Square, accum_out=acc[:, 2, q:q + 1]))
                run(dve, (tag, "xw", q), [tag + " w", ((tag, "xw", q - 1) if q else None)], lambda e: e.tensor_tensor_reduce(
                    out=big[:, 8 * D:9 * D], in0=xin[:, q, :], in1=w[:, q, :], scale=1.0, scalar=0.0, op0=ALU.mult, op1=ALU.add,
                    accum_out=acc[:, 3, q:q + 1]))
            X2, na, ca, t0, n2, th, be, XY, Y2, den, pp, rr, t1 = (S[:, i, :] for i in (0, 8, 9, 10, 11, 12, 13, 14, 15, 16, 17, 18, 19))
            norm_clip(tag + " na", na, acc[:, 1, :], [(tag, "aa", NQ - 1)])
            clipped_ratio(tag + " ca", ca, na, t0, [tag + " na"])
            run(pool, tag + " wn", [(tag, "ww", NQ - 1), tag + " ca"], lambda e: e.tensor_tensor(n2, acc[:, 2, :], half[:, 0:NQ], ALU.pow))
            run(dve, tag + " wc", [tag + " wn"], lambda e: e.tensor_tensor(n2, n2, ca, ALU.mult))
            run(dve, tag + " n2", [tag + " wc"], lambda e: e.tensor_scalar(n2, n2, EPS, None, ALU.max))
            run(act, tag + " th", [tag + " n2"], lambda e: e.activation(th, n2, ACT.Tanh))
            run(dve, tag + " rn", [tag + " n2"], lambda e: e.reciprocal(t0, n2))
            run(dve, tag + " cr", [tag + " rn"], lambda e: e.tensor_tensor(t0, t0, ca, ALU.mult))
            run(dve, tag + " be", [tag + " cr", tag + " th"], lambda e: e.tensor_tensor(be, t0, th, ALU.mult))
            run(dve, tag + " XY", [tag + " be", (tag, "xw", NQ - 1)], lambda e: e.tensor_tensor(XY, be, acc[:, 3, :], ALU.mult))
            run(dve, tag + " bb", [tag + " be"], lambda e: e.tensor_tensor(t0, be, be, ALU.mult))
            run(dve, tag + " Y2", [tag + " bb"], lambda e: e.tensor_tensor(Y2, t0, acc[:, 2, :], ALU.mult))
            run(dve, tag + " 2XY", [tag + " XY"], lambda e: e.tensor_scalar(t1, XY, 2.0, 1.0, ALU.mult, ALU.add))
            run(dve, tag + " X2Y2", [tag + " Y2"], lambda e: e.tensor_tensor(den, X2, Y2, ALU.mult))
            run(dve, tag + " den", [tag + " X2Y2", tag + " 2XY"], lambda e: e.tensor_tensor(den, den, t1, ALU.add))
            run(dve, tag + " denc", [tag + " den"], lambda e: e.tensor_scalar(den, den, EPS, None, ALU.max))
            run(dve, tag + " rden", [tag + " denc"], lambda e: e.reciprocal(t0, den))
            run(dve, tag + " num", [tag + " Y2", tag + " 2XY"], lambda e: e.tensor_tensor(pp, t1, Y2, ALU.add))
            run(dve, tag + " p", [tag + " num", tag + " rden"], lambda e: e.tensor_tensor(pp, pp, t0, ALU.mult))
            run(dve, tag + " 1-X2", [tag + " X2Y2"], lambda e: e.tensor_scalar(rr, X2, -1.0, 1.0, ALU.mult, ALU.add))
            run(dve, tag + " r1", [tag + " 1-X2"], lambda e: e.tensor_tensor(rr, rr, be, ALU.mult))
            run(dve, tag + " r", [tag + " r1", tag + " rden"], lambda e: e.tensor_tensor(rr, rr, t0, ALU.mult))
            for q in range(NQ):
                run(act, (tag, "xp", q), [tag + " p"], lambda e: e.activation(z[:, q, :], xin[:, q, :], ACT.Identity, scale=S[:, 17, q:q + 1]))
            for q in range(NQ):
                run(dve, (tag, "x", q), [(tag, "xp", q), tag + " r"], lambda e: e.scalar_tensor_tensor(
                    xout[:, q, :], w[:, q, :], S[:, 18, q:q + 1], z[:, q, :], ALU.mult, ALU.add))
            if more is not None:
                run(dve, tag + " out", [(tag, "x", NQ - 1)], lambda e: e.tensor_tensor(xout[:, :, :], xout[:, :, :], more[:, :, :], ALU.add))
            else:
                core.events[tag + " out"] = core.events[(tag, "x", NQ - 1)]

        def hidden_layer(tag, w1, w2, src, b1, func, hbanks, ybanks, needs, act_needs):
            pe.need(*needs)

            def second(m):
                pe.need((tag, "h", m))
                for q in range(NQ):
                    last = pe.eng.matmul(bank(ybanks[q // 2])[:, (q % 2) * D:(q % 2 + 1) * D], uT[:, m, q * P:(q + 1) * P], w2[:, m, :],
                                         start=(m == 0 and q % 2 == 0), stop=m == FC - 1, skip_group_check=True)
                pe.done(last, (tag, "y", m))

            for m in range(FC):
                hb = hbanks[m % len(hbanks)]
                if m >= len(hbanks):
                    pe.need((tag, "h", m - len(hbanks)))
                for k in range(KC):
                    last = pe.eng.matmul(bank(hb), w1[:, k, m * P:(m + 1) * P], src[:, k, :], start=k == 0, stop=k == KC - 1)
                pe.done(last, (tag, "up", m))
                run(act, (tag, "h", m), [(tag, "up", m)] + (act_needs if m == 0 else []),
                    lambda e: e.activation(uT[:, m, :], bank(hb), func, bias=b1[:, m:m + 1]))
                if m:
                    second(m - 1)
            second(FC - 1)

        def batch(b):
            core.dma(sp, "ada", ada[:, :, :].rearrange("p j d -> p (j d)"), ada_dram[bass.ds(b, 1), :].rearrange("o n -> (o n)").partition_broadcast(P), "ada")
            for k in range(KC):
                run((pool, act)[k], ("xT", k), [], lambda e: (e.tensor_copy if k == 0 else e.copy)(xT[:, k, :], XT[:, k, :, bass.ds(b, 1)]))
            pe.need(("xT", 0), ("xT", 1))
            for q in range(NQ):
                for k in range(KC):
                    last = pe.eng.transpose(bank(q // 2)[:, (q % 2) * D + k * P:(q % 2) * D + (k + 1) * P], xT[:, k, q * P:(q + 1) * P], I[:, :])
                if q % 2:
                    pe.done(last, ("x T", q // 2))
            run(act, "x 0", [("x T", 0)], lambda e: e.copy(f3(x[:, 0:2, :]), bank(0)))
            run(dve, "x 1", [("x T", 1)], lambda e: e.tensor_copy(f3(x[:, 2:4, :]), bank(1)))
            modulated_norm("ln1", x, 0, ["x 0", "x 1"])
            to_feature_major("zT", z, zT, (2, 3), ["ln1 z"])

            pe.need(("zT", 0), ("zT", 1))
            for q in range(NQ):
                b0, b1_ = (4, 5) if q % 2 == 0 else (6, 7)
                if q >= 2:
                    pe.need(("qkv b", q - 2))
                for (lo, hi), bk in (((0, 512), b0), ((512, 768), b1_)):
                    for k in range(KC):
                        last = pe.eng.matmul(bank(bk)[:, 0:hi - lo], zT[:, k, q * P:(q + 1) * P], W["wqkv"][:, k, lo:hi], start=k == 0, stop=k == KC - 1)
                pe.done(last, ("qkv", q))
                flat = qkv[:, q].rearrange("p a h d -> p (a h d)")
                for (lo, hi), bk, nm in (((0, 512), b0, "qkv a"), ((512, 768), b1_, "qkv b")):
                    run(dve, (nm, q), [("qkv", q), "ln1 s"], lambda e: e.scalar_tensor_tensor(
                        flat[:, lo:hi], bank(bk)[:, 0:hi - lo], S[:, 1, q:q + 1], W["bqkv"][:, lo:hi], ALU.mult, ALU.add))
                run(act, ("qkv sq", q), [("qkv b", q)], lambda e: e.activation(pflat[:, q * 768:(q + 1) * 768], flat, ACT.Square))
                run(dve, ("qkv ss", q), [("qkv sq", q)], lambda e: e.tensor_reduce(
                    hs[:, 0, q, :], pflat[:, q * 768:(q + 1) * 768].rearrange("p (h d) -> p h d", d=HD), AX.X, ALU.add))
            hss, hf, ht = hs[:, 0], hs[:, 1], hs[:, 2]
            tot, tn, tr = acc[:, 4:7, :].rearrange("p a q -> p q a"), S[:, 20:23, :].rearrange("p a q -> p q a"), hs[:, 3, :, 0:3]
            run(dve, "tot", [("qkv ss", NQ - 1)], lambda e: e.tensor_reduce(tot, hss.rearrange("p q (a h) -> p q a h", h=H), AX.X, ALU.add))
            norm_clip("tn", tn, tot, ["tot"], half[:, 0:3 * NQ].rearrange("p (q a) -> p q a", a=3))
            run(dve, "tr", ["tn"], lambda e: e.reciprocal(tr, tn))
            run(dve, "tm", ["tr"], lambda e: e.tensor_scalar(tn, tn, ATMAX, TO_HEADS, ALU.min, ALU.mult))
            run(dve, "cs", ["tm"], lambda e: e.tensor_tensor(tn, tn, tr, ALU.mult))
            csb = tn.unsqueeze(3).to_broadcast([P, NQ, 3, H])
            h4 = lambda t: t.rearrange("p q (a h) -> p q a h", h=H)
            run(pool, "h sqrt", ["tot"], lambda e: e.tensor_tensor(f3(ht), f3(hss), half[:, :], ALU.pow))
            run(dve, "h n", ["h sqrt", "cs"], lambda e: e.tensor_tensor(h4(ht), h4(ht), csb, ALU.mult))
            run(dve, "h nc", ["h n"], lambda e: e.tensor_scalar(f3(ht), f3(ht), EPS, None, ALU.max))
            run(dve, "h r", ["h nc"], lambda e: e.reciprocal(f3(hf), f3(ht)))
            run(dve, "h f", ["h r"], lambda e: e.scalar_tensor_tensor(f3(hf), f3(ht), ATMAX, f3(hf), ALU.min, ALU.mult))
            run(dve, "h F", ["h f"], lambda e: e.tensor_tensor(h4(hf), h4(hf), csb, ALU.mult))
            hf4 = h4(hf)
            for q in range(NQ):
                for a in (0, 1):
                    run(dve, ("qk", q, a), ["h F"], lambda e: e.tensor_tensor(
                        qkv[:, q, a], qkv[:, q, a], hf4[:, q, a, :].unsqueeze(2).to_broadcast([P, H, HD]), ALU.mult))
                run(dve, ("v", q), ["h F"], lambda e: e.tensor_tensor(
                    vt[:, q, :, 0:HD], qkv[:, q, 2], hf4[:, q, 2, :].unsqueeze(2).to_broadcast([P, H, HD]), ALU.mult))
                for a in (0, 1):
                    src = qkv[:, q, a]
                    dst = spl[:, a, q].rearrange("p h (s t) d -> p h s t d", t=2)
                    hi = [dst[:, :, 0, :, :], dst[:, :, :, 0, :]][a]
                    lo = [dst[:, :, 1, :, :], dst[:, :, :, 1, :]][a]
                    srcb = src.unsqueeze(2).to_broadcast([P, H, 2, HD])
                    run(act, ("hi", q, a), [("qk", q, a)], lambda e: e.copy(hi, srcb))
                    run(dve, ("lo", q, a), [("hi", q, a)], lambda e: e.tensor_tensor(lo, srcb, hi, ALU.subtract))
            I16 = I16_t
            for a in (0, 1):
                for hp2 in range(H // 4):
                    bk = 4 * a + hp2
                    v16 = bank(bk).bitcast(fp16)
                    for q in range(NQ):
                        pe.need(("lo", q, a))
                        if q == 0 and bk >= 4:
                            pe.need(("qkv b", NQ - 1))
                        for j in range(2):
                            hp = 2 * hp2 + j
                            src = spl[:, a, q, 2 * hp:2 * hp + 2].rearrange("p h s d -> p (h s d)")
                            last = pe.eng.transpose(v16[:, j * 512 + q * P:j * 512 + (q + 1) * P], src, I16[:, :])
                    pe.done(last, ("splT ps", a, hp2))
                    lane = (act, dve)[hp2 % 2]
                    run(lane, ("splT", a, hp2), [("splT ps", a, hp2)], lambda e: (e.copy if lane is act else e.tensor_copy)(
                        splT[:, a, 2 * hp2:2 * hp2 + 2, :].rearrange("p j t -> p (j t)"), v16[:, :]))

            def scores(g, kc):
                for pr in range(2):
                    if (g, kc) != (0, 0):
                        pe.need(("exp", *prev_unit(g, kc), pr))
                    else:
                        pe.need(("splT", 0, pr * 2), ("splT", 0, pr * 2 + 1), ("splT", 1, 3), ("splT", 1, 2))
                    for j in range(2):
                        hp = 2 * g + pr
                        rows = slice(64 * j, 64 * j + 64)
                        last = pe.eng.matmul(bank(2 * pr + j), splT[rows, 1, hp, kc * P:(kc + 1) * P], splT[rows, 0, hp, :], start=True, stop=True)
                    pe.done(last, ("scores", g, kc, pr))
                    if unit_no(g, kc) >= 2:
                        act.need(("av", *prev_unit(*prev_unit(g, kc))))
                    run(act, ("exp", g, kc, pr), [("scores", g, kc, pr)], lambda e: e.activation(
                        pexp[:, unit_no(g, kc) % 2, 2 * pr:2 * pr + 2, :], PS[pr][:, :, :], ACT.Exp, scale=1.0 / math.sqrt(HD)))

            def values(g, kc):
                pe.need(("exp", g, kc, 1), ("v", kc))
                if kc == 0 and g >= 2:
                    pe.need(("oT", g - 2))
                for j in range(4):
                    last = pe.eng.matmul(bank(4 + g % 2)[32 * j:32 * j + 32, :], vt[:, kc, 4 * g + j, :], pexp[:, unit_no(g, kc) % 2, j, :],
                                         start=kc == 0, stop=kc == NQ - 1, tile_position=(0, 32 * j))
                pe.done(last, ("av", g, kc))
                if kc == NQ - 1:
                    run(dve, ("oT", g), [("av", g, kc)], lambda e: e.tensor_copy(oT[:, g, :], bank(4 + g % 2)))

            def back(g):
                pe.need(("oT", g))
                if g >= 2:
                    pe.need(("O", g - 2))
                bk = 6 + g % 2
                for q in range(NQ):
                    last = pe.eng.transpose(bank(bk)[:, q * P:(q + 1) * P], oT[:, g, q * P:(q + 1) * P], I[:, :])
                pe.done(last, ("O T", g))
                run(dve, ("O", g), [("O T", g)], lambda e: e.tensor_copy(
                    O[:, :, 4 * g:4 * g + 4, :].rearrange("p q h d -> p q (h d)"), bank(bk).rearrange("p (q n) -> p q n", q=NQ)))

            unit_no = lambda g, kc: g * NQ + kc
            prev_unit = lambda g, kc: divmod(unit_no(g, kc) - 1, NQ)
            units = [(g, kc) for g in range(H // 4) for kc in range(NQ)]
            scores(*units[0])
            for n, u in enumerate(units):
                if n + 1 < len(units):
                    scores(*units[n + 1])
                values(*u)
                if u[1] == 1 and u[0] > 0:
                    back(u[0] - 1)
            back(H // 4 - 1)

            o3 = O[:, :, :, 0:HD]
            oss, ond, oh, of, ot = (hs[:, i, :, 0:H] for i in (0, 1, 2, 3, 3))
            sqv = big[:, 0:NQ * D].rearrange("p (q h d) -> p q h d", q=NQ, h=H)
            run(act, "o sq", [("O", 3)], lambda e: e.activation(sqv, o3, ACT.Square))
            run(dve, "o ss", ["o sq"], lambda e: e.tensor_reduce(oss, sqv, AX.X, ALU.add))
            run(dve, "o rd", ["o ss"], lambda e: e.reciprocal(ond, O[:, :, :, HD]))
            run(pool, "o sqrt", ["o ss"], lambda e: e.tensor_tensor(oh, oss, half[:, 0:NQ * H].rearrange("p (q h) -> p q h", q=NQ), ALU.pow))
            run(dve, "o nh", ["o sqrt", "o rd"], lambda e: e.tensor_tensor(oh, oh, ond, ALU.mult))
            run(dve, "o nc", ["o nh"], lambda e: e.tensor_scalar(oh, oh, EPS, None, ALU.max))
            run(dve, "o r", ["o nc"], lambda e: e.reciprocal(of, oh))
            run(dve, "o m", ["o r"], lambda e: e.scalar_tensor_tensor(of, oh, ATMAX, of, ALU.min, ALU.mult))
            run(dve, "o f", ["o m"], lambda e: e.scalar_tensor_tensor(of, of, FROM_HEADS, ond, ALU.mult, ALU.mult))
            run(dve, "o t", ["o f"], lambda e: e.tensor_tensor(
                z[:, :, :].rearrange("p q (h d) -> p q h d", h=H), o3, of.unsqueeze(3).to_broadcast([P, NQ, H, HD]), ALU.mult))
            run(dve, "o ff", ["o f"], lambda e: e.tensor_tensor(oh, of, of, ALU.mult))
            run(dve, "o ffs", ["o ff"], lambda e: e.tensor_tensor(oh, oh, oss, ALU.mult))
            run(dve, "t ss", ["o ffs"], lambda e: e.tensor_reduce(acc[:, 7, :], oh, AX.X, ALU.add))
            norm_clip("t n", S[:, 8, :], acc[:, 7, :], ["t ss"])
            clipped_ratio("t s", S[:, 7, :], S[:, 8, :], S[:, 9, :], ["t n"])
            to_feature_major("tT", z, zT, (0, 1), ["o t", ("exp", 3, 3, 1)])
            pe.need(("tT", 0), ("tT", 1))
            for q in range(NQ):
                for k in range(KC):
                    last = pe.eng.matmul(bank(2 + q // 2)[:, (q % 2) * D:(q % 2 + 1) * D], zT[:, k, q * P:(q + 1) * P], W["wo"][:, k, :], start=k == 0, stop=k == KC - 1)
            pe.done(last, "wo")
            mobius_update("m1", (2, 3), W["bo"], 2, x, x1, None, ["wo", "t s", ("tT", "T", 1)])

            modulated_norm("ln2", x1, 3, ["m1 out"])
            for q in range(NQ):
                run(dve, ("zs", q), ["ln2 s"], lambda e: e.tensor_scalar(z[:, q, :], z[:, q, :], S[:, 1, q:q + 1], None, ALU.mult))
            to_feature_major("zsT", z, zT, (0, 1), [("zs", NQ - 1)])
            hidden_layer("ff", W["wf1"], W["wf2"], zT, W["bf1"], ACT.Identity, (4, 5), (6, 7), [("zsT", 0), ("zsT", 1), ("O", 3)], [])
            run(act, "u sq", [("ff", "h", FC - 1), ("m1", "xw", NQ - 1)], lambda e: e.activation(big[:, :], uT.rearrange("p a b -> p (a b)"), ACT.Square))
            run(dve, "u ss", ["u sq"], lambda e: e.tensor_reduce(xT[:, 0, :], big[:, :].rearrange("p (m t) -> p t m", m=FC), AX.X, ALU.add))
            pe.need("u ss", ("zsT", 0))
            for q in range(NQ):
                last = pe.eng.matmul(bank(2)[:, q:q + 1], xT[:, 0, q * P:(q + 1) * P], ones[:, 0:1], start=q == 0, stop=True, skip_group_check=True)
            pe.done(last, "u tot")
            run(dve, "u out", ["u tot"], lambda e: e.tensor_copy(acc[:, 7, :], bank(2)[:, 0:NQ]))
            norm_clip("u n", S[:, 8, :], acc[:, 7, :], ["u out"])
            clipped_ratio("u s", S[:, 7, :], S[:, 8, :], S[:, 9, :], ["u n"])
            mobius_update("m2", (6, 7), W["bf2"], 5, x1, x1, x, [("ff", "y", FC - 1), "u s", ("zsT", "T", 1)])

            to_feature_major("x3T", x1, xT, (0, 1), ["m2 out", "u tot"])
            for n, (lo, hi) in enumerate(SEGS):
                run(dve, ("seg", n), [("x3T", 0), ("x3T", 1)], lambda e: e.tensor_reduce(gin[:, n, :], xT[:, :, lo:hi], AX.X, ALU.add))
            nhp = T - SEG
            run(dve, "g hp", [("seg", 2)], lambda e: e.tensor_tensor(gi[:, 1, :], gin[:, 0, :], gin[:, 2, :], ALU.add))
            run(dve, "g wp", [("seg", 2)], lambda e: e.tensor_tensor(gi[:, 2, :], gin[:, 1, :], gin[:, 2, :], ALU.add))
            run(dve, "g all", ["g hp"], lambda e: e.tensor_tensor(gi[:, 0, :], gi[:, 1, :], gin[:, 1, :], ALU.add))
            run(dve, "g m0", ["g all"], lambda e: e.tensor_scalar(gi[:, 0, :], gi[:, 0, :], 1.0 / T, None, ALU.mult))
            run(dve, "g m1", ["g all", "g wp"], lambda e: e.tensor_scalar(gi[:, 1:3, :], gi[:, 1:3, :], 1.0 / nhp, None, ALU.mult))
            pe.need("g m1", "u out")
            for n in range(3):
                for k in range(KC):
                    last = pe.eng.matmul(bank(2)[0:1, 0:E], gi[:, n, k:k + 1], W["gate_w"][:, n * KC + k, :], start=(n, k) == (0, 0), stop=(n, k) == (2, KC - 1))
            pe.done(last, "logits")
            G = lambda i, m=8: gr[:, 8 * i:8 * i + m]
            run(dve, "l b", ["logits"], lambda e: e.tensor_tensor(G(0, E), bank(2)[0:1, 0:E], gateb[:, :], ALU.add))
            run(dve, "l s", ["l b"], lambda e: e.tensor_tensor(G(0, E), G(0, E), modrow[:, bass.ds(b, 1), 0:E], ALU.mult))
            run(dve, "l t", ["l s"], lambda e: e.tensor_tensor(G(0, E), G(0, E), modrow[:, bass.ds(b, 1), E:2 * E], ALU.add))
            run(dve, "l max", ["l t"], lambda e: e.tensor_reduce(G(1, 1), G(0, E), AX.X, ALU.max, negate=True))
            run(dve, "pad", [], lambda e: e.memset(G(2), -1.0))
            run(act, "l exp", ["l max", "pad"], lambda e: e.activation(G(2, E), G(0, E), ACT.Exp, bias=G(1, 1)))
            run(dve, "l sum", ["l exp"], lambda e: e.tensor_reduce(G(3, 1), G(2, E), AX.X, ALU.add))
            run(dve, "l rs", ["l sum"], lambda e: e.reciprocal(G(3, 1), G(3, 1)))
            run(dve, "l p", ["l rs"], lambda e: e.tensor_scalar(G(2, E), G(2, E), G(3, 1), None, ALU.mult))
            run(dve, "top", ["l p"], lambda e: e.max(G(4), G(2)))
            run(dve, "idx", ["top"], lambda e: e.max_index(gidx[:, :], G(4), G(2)))
            sp.need("idx")
            for s in range(TOPK):
                ei = sp.eng.value_load(gidx[:, s:s + 1], min_val=0, max_val=E - 1)
                core.dma(sp, f"e{s}", ew1[s][:, :, :], A["ew1"][bass.ds(ei, 1)].rearrange("o p k n -> p (o k) n"), ("ew", s))
                core.dma(sp, f"e{s}", ew2[s][:, :, :], A["ew2"][bass.ds(ei, 1)].rearrange("o p k n -> p (o k) n"), ("ew", s))
                core.dma(sp, f"e{s}", eb2[s][:, :], A["eb2"][bass.ds(ei, 1), :].rearrange("o n -> (o n)").partition_broadcast(P), ("ew", s))
                core.dma(sp, f"e{s}", eb1[:, s, :], A["eb1d"][bass.ds(ei, 1)].rearrange("o p n -> p (o n)"), ("ew", s))
            run(dve, "w sum", ["top"], lambda e: e.tensor_reduce(G(5, 1), G(4, TOPK), AX.X, ALU.add))
            run(dve, "w eps", ["w sum"], lambda e: e.tensor_scalar(G(5, 1), G(5, 1), 1e-8, None, ALU.add))
            run(dve, "w r", ["w eps"], lambda e: e.reciprocal(G(5, 1), G(5, 1)))
            run(dve, "w n", ["w r"], lambda e: e.tensor_scalar(G(4, TOPK), G(4, TOPK), G(5, 1), None, ALU.mult))
            run(dve, "idx f", ["idx"], lambda e: e.tensor_copy(G(6), gidx[:, :]))
            for n, masked in ((0, 2.0), (1, 1.0)):
                run(dve, ("g6", n), ["idx f", "w n"], lambda e: e.scalar_tensor_tensor(
                    g6[:, n * TOPK:(n + 1) * TOPK], G(6, TOPK), masked, G(4, TOPK), ALU.not_equal, ALU.mult))
            run(dve, "g6", ["w n"], lambda e: e.tensor_copy(g6[:, 2 * TOPK:3 * TOPK], G(4, TOPK)))
            run(pe, "b6 ps", ["g6", "l b"], lambda e: e.matmul(bank(2)[:, 0:3 * TOPK], ones[0:1, :], g6[:, :], start=True, stop=True))
            run(dve, "b6", ["b6 ps"], lambda e: e.tensor_copy(b6[:, :], bank(2)[:, 0:3 * TOPK]))
            for s in range(TOPK):
                for n in range(3):
                    seg, fac = W["segs"][:, n, :], b6[:, n * TOPK + s:n * TOPK + s + 1]
                    if n == 0:
                        run(dve, ("wm", s, n), ["b6"], lambda e: e.tensor_scalar(wm[:, s, :], seg, fac, None, ALU.mult))
                    else:
                        run(dve, ("wm", s, n), [("wm", s, n - 1)], lambda e: e.scalar_tensor_tensor(wm[:, s, :], seg, fac, wm[:, s, :], ALU.mult, ALU.add))

            y, yb = x, w
            for n in range(1 + TOPK):
                s = n - 1
                ybanks = (4, 5) if n % 2 == 0 else (6, 7)
                w1, w2, c1, r2 = (W["sw1"], W["sw2"], W["sb1"], W["sb2"]) if n == 0 else (ew1[s], ew2[s], eb1[:, s, :], eb2[s])
                needs = [("x3T", 0), ("x3T", 1), ("m2", "a", NQ - 1)] if n == 0 else [("ew", s), "b6", (f"x{n - 1}", "h", FC - 1)]
                if n == 2:
                    needs += [("yb", 0, NQ - 1)]
                hidden_layer(f"x{n}", w1, w2, xT, c1, ACT.Gelu_apprx_tanh, (0, 1, 2, 3) if n else (0, 1, 3), ybanks, needs,
                             ["u sq", "u tot"] if n == 0 else [("ew", s), (f"x{n - 1}", "y", FC - 1)])
                for q in range(NQ):
                    src = bank(ybanks[q // 2])[:, (q % 2) * D:(q % 2 + 1) * D]
                    run(dve, ("yb", n, q), [(f"x{n}", "y", FC - 1), ("m2", "x", NQ - 1)] + ([("ew", s)] if n else []),
                        lambda e: e.tensor_tensor(yb[:, q, :], src, r2[:, :], ALU.add))
                    if n == 0:
                        run(dve, ("y", n, q), [("yb", n, q)], lambda e: e.tensor_tensor(x1[:, q, :], yb[:, q, :], x1[:, q, :], ALU.add))
                    else:
                        run(dve, ("y", n, q), [("yb", n, q), ("wm", s, 2)], lambda e: e.scalar_tensor_tensor(
                            x1[:, q, :], yb[:, q, :], wm[:, s, q:q + 1], x1[:, q, :], ALU.mult, ALU.add))
            sp.need(("y", TOPK, NQ - 1))
            core.dma(sp, "out", out[bass.ds(b, 1)].rearrange("o (q p) d -> p (o q) d", p=P), x1[:, :, :], "out")
            core.barrier()

        I16_t = sb("I16", [P, P], fp16)
        gateb = sb("gateb", [1, E])
        core.dma(sp, "c", gateb[:, :], A["gate_b"], "gateb")
        run(dve, "I16", [], lambda e: e.tensor_copy(I16_t[:, :], I[:, :]))
        core.barrier()
        with nc.Fori(0, NB) as b:
            batch(b)


def program(nc, A, out):
    with ExitStack() as ctx:
        core = Core(nc, ctx)
        XT = ctx.enter_context(nc.sbuf_tensor("XT", [P, KC, T, NB], fp32))
        modrow = ctx.enter_context(nc.sbuf_tensor("modrow", [1, NB, 2 * E], fp32))
        ada_dram = nc.dram_tensor("ada_scratch", (NB, 6 * D), fp32, kind="Internal").ap()
        W = load_weights(nc, core, ctx, A)
        recurrences(nc, core, ctx, A, XT)
        conditioning(nc, core, A, W, ada_dram, modrow)
        transformer_and_experts(nc, core, A, W, XT, ada_dram, modrow, out)


def kernel(**inputs):
    import numpy as np
    import concourse.bacc as bacc
    from concourse.bass_utils import run_bass_kernel_spmd

    f = {n: np.ascontiguousarray(a) for n, a in inputs.items()}
    L2 = lambda n: f["L2_cond_" + n]
    L3 = lambda n: f["L3_cond_" + n]
    ifgo = lambda a: np.concatenate([a[..., 0:D], a[..., D:2 * D], a[..., 3 * D:], a[..., 2 * D:3 * D]], axis=-1)
    rows = lambda a: a.reshape(-1, P, a.shape[-1]).transpose(1, 0, 2)
    cols = lambda a: a.reshape(-1, P).T
    token = np.arange(T).reshape(NQ, P).T
    arrays = {
        "xT": f["x"].transpose(2, 1, 0).reshape(KC, P, T, NB).transpose(1, 0, 2, 3),
        "condT": rows(f["cond_1024"].T),
        "b0T": cols(f["L0_cond_b"]),
        "b1row": ifgo(f["L1_cond_b"])[None, :],
        "L0_cond_Wx": f["L0_cond_Wx"], "L0_cond_Wh": f["L0_cond_Wh"],
        "L1_cond_Wx": ifgo(f["L1_cond_Wx"]), "L1_cond_Wh": ifgo(f["L1_cond_Wh"]),
        "ident": np.eye(P, dtype=np.float32), "I": np.eye(P, dtype=np.float32),
        "segs": np.stack([(token >= lo) & (token < hi) for lo, hi in SEGS], axis=1).astype(np.float32),
        "wqkv": rows(np.concatenate([L2("w_q"), L2("w_k"), L2("w_v")], axis=1)),
        "bqkv": np.concatenate([L2("b_q"), L2("b_k"), L2("b_v")]),
        "wo": rows(L2("w_o")), "bo": L2("b_o"), "wf1": rows(L2("w_f1")), "bf1": cols(L2("b_f1")),
        "wf2": rows(L2("w_f2")), "bf2": L2("b_f2"), "w_ada": rows(L2("w_ada")), "b_ada": L2("b_ada"),
        "gate_w": rows(L3("gate_w")), "gate_b": L3("gate_b")[None, :], "time_w": rows(L3("time_w")), "time_b": L3("time_b")[None, :],
        "ew1": np.stack([rows(L3("ew1")[e]) for e in range(E)]), "ew2": np.stack([rows(L3("ew2")[e]) for e in range(E)]),
        "eb1": np.stack([cols(L3("eb1")[e]) for e in range(E)], axis=1), "eb1d": np.stack([cols(L3("eb1")[e]) for e in range(E)]),
        "eb2": L3("eb2"),
        "sw1": rows(L3("sw1")), "sb1": cols(L3("sb1")), "sw2": rows(L3("sw2")), "sb2": L3("sb2"),
    }
    arrays = {n: np.ascontiguousarray(a) for n, a in arrays.items()}
    nc = bacc.Bacc("TRN2", target_bir_lowering=False, num_devices=1)
    A = {n: nc.dram_tensor("in_" + n, a.shape, mybir.dt.from_np(a.dtype), kind="ExternalInput").ap() for n, a in arrays.items()}
    out = nc.dram_tensor("out_x", (NB, T, D), fp32, kind="ExternalOutput").ap()
    program(nc, A, out)
    r = run_bass_kernel_spmd(nc, [{"in_" + n: a for n, a in arrays.items()}], core_ids=[0])
    return r.results[0]["out_x"]
```

```python
import concourse.bass as bass
from concourse import mybir
from contextlib import ExitStack

fp32 = mybir.dt.float32
fp16 = mybir.dt.float16
bf16 = mybir.dt.bfloat16
u32 = mybir.dt.uint32
ALU = mybir.AluOpType
ACT = mybir.ActivationFunctionType
AX = mybir.AxisListType

import math
import numpy as np

P = 128
NB, T, D = 8, 512, 256
KC = D // P
GATES = 4 * D // P
CH = 16
NCH = T // CH
H, HD = 16, 16
FF = 1024
FC = FF // P
E, TOPK = 4, 2
NQ = T // P
EPS = 1e-7
MAXT = float(np.float32(1.0 - 1e-5))
ATMAX = math.atanh(MAXT)
beta = lambda a, b: math.exp(math.lgamma(a) + math.lgamma(b) - math.lgamma(a + b))
TO_HEADS = beta(HD / 2, 0.5) / beta(D / 2, 0.5)
FROM_HEADS = 1.0 / TO_HEADS
SEG = T // 3
SEGS = [(0, SEG), (SEG, 2 * SEG), (2 * SEG, T)]
W16_EXP = 14


class Lane:

    def __init__(self, name, eng, sems, core):
        self.name, self.eng, self.sems, self.core = name, eng, sems, core
        self.count, self.seen = [0, 0], {}

    def done(self, ins, event):
        epoch = self.core.epoch
        self.count[epoch] += 1
        ins.then_inc(self.sems[epoch], 1)
        self.core.events[event] = (self.sems[epoch], self.count[epoch])
        return ins

    def need(self, *events):
        for event in events:
            if event is None:
                continue
            sem, count = self.core.events[event]
            if self.seen.get(sem.name, 0) < count:
                self.eng.wait_ge(sem, count)
                self.seen[sem.name] = count


class Core:

    def __init__(self, nc, ctx):
        self.nc, self.events, self.epoch = nc, {}, 0
        self.sem = lambda n: ctx.enter_context(nc.semaphore(n))
        mk = lambda n, e: Lane(n, e, [self.sem(f"n_{n}_{i}") for i in range(2)], self)
        self.pe, self.act, self.dve = mk("pe", nc.tensor), mk("act", nc.scalar), mk("dve", nc.vector)
        self.pool, self.sp = mk("pool", nc.gpsimd), mk("sp", nc.sync)
        self.lanes = [self.pe, self.act, self.dve, self.pool, self.sp]
        self.others = [l for l in self.lanes if l is not self.pool]
        self.dma_sems, self.dma_used = {}, {}
        self.gather = self.sem("gather")
        self.release = {l.name: self.sem("go_" + l.name) for l in self.others}
        self.passed = [self.sem(f"passed_{i}") for i in range(2)]
        self.ready = [{l.name: self.sem(f"ready_{i}_{l.name}") for l in self.others} for i in range(2)]
        self.retired = [False, False]
        self.background = Background()

    def dma(self, lane, stream, out, in_, event):
        if stream not in self.dma_sems:
            self.dma_sems[stream] = self.sem("dma_" + stream)
            self.dma_used[stream] = 0
        self.dma_used[stream] += 16
        lane.eng.dma_start(out, in_).then_inc(self.dma_sems[stream], 16)
        self.events[event] = (self.dma_sems[stream], self.dma_used[stream])

    def zero(self, epoch):
        for lane in self.lanes:
            if lane.count[epoch]:
                self.pool.eng.sem_inc(lane.sems[epoch], -lane.count[epoch])
            lane.count[epoch] = 0

    def retire(self):
        old, pool = 1 - self.epoch, self.pool
        if not any(l.count[old] for l in self.lanes):
            return
        for lane in self.others:
            lane.eng.sem_inc(self.passed[old], 1)
        pool.eng.wait_ge(self.passed[old], len(self.others))
        for lane in self.lanes:
            if lane.count[old]:
                pool.eng.wait_ge(lane.sems[old], lane.count[old])
        self.zero(old)
        pool.eng.sem_inc(self.passed[old], -len(self.others))
        for lane in self.others:
            pool.eng.sem_inc(self.ready[old][lane.name], 1)
        self.retired[old] = True

    def next_epoch(self):
        self.epoch = 1 - self.epoch
        if self.retired[self.epoch]:
            for lane in self.others:
                lane.eng.wait_ge(self.ready[self.epoch][lane.name], 1)
                lane.eng.sem_inc(self.ready[self.epoch][lane.name], -1)
        self.retired[self.epoch] = False
        mine = {l.sems[self.epoch].name for l in self.lanes}
        self.events = {e: v for e, v in self.events.items() if v[0].name not in mine}
        for lane in self.lanes:
            for l in self.lanes:
                lane.seen.pop(l.sems[self.epoch].name, None)

    def barrier(self):
        pool = self.pool
        for stream, used in self.dma_used.items():
            if used:
                pool.eng.wait_ge(self.dma_sems[stream], used)
        for lane in self.lanes:
            lane.eng.drain().then_inc(self.gather, 1)
        pool.eng.wait_ge(self.gather, len(self.lanes))
        for epoch in (0, 1):
            self.zero(epoch)
            if self.retired[epoch]:
                for lane in self.others:
                    pool.eng.sem_inc(self.ready[epoch][lane.name], -1)
                self.retired[epoch] = False
        for stream, used in self.dma_used.items():
            if used:
                pool.eng.sem_inc(self.dma_sems[stream], -used)
            self.dma_used[stream] = 0
        pool.eng.sem_inc(self.gather, -len(self.lanes))
        for lane in self.others:
            pool.eng.sem_inc(self.release[lane.name], 1)
        for lane in self.others:
            lane.eng.wait_ge(self.release[lane.name], 1)
            lane.eng.sem_inc(self.release[lane.name], -1)
        for lane in self.lanes:
            lane.seen = {}
        self.events.clear()


class Background:

    STEP = 0.9

    def __init__(self, steps=()):
        self.steps, self.credit, self.open, self.mark = iter(steps), 0.0, False, None

    def tick(self, us):
        if not self.open:
            return
        self.credit += us
        while self.credit >= self.STEP and not self.mark:
            self.credit -= self.STEP
            self.step()

    def step(self):
        was, self.open = self.open, False
        self.mark = next(self.steps, "end")
        self.open = was

    def run_to(self, mark):
        while self.mark not in (mark, "end"):
            self.step()

    def go_on(self):
        self.open, self.mark, self.credit = True, None, 0.0


TICK = {"dve": 0.2, "act": 0.2, "pool": 1.0, "pe": 0.0}


def run(lane, event, needs, issue, us=None):
    lane.need(*needs)
    ins = lane.done(issue(lane.eng), event)
    lane.core.background.tick(TICK[lane.name] if us is None else us)
    return ins


def recurrences(nc, core, ctx, A, x2_dram):
    pe, act, dve, pool, sp = core.pe, core.act, core.dve, core.pool, core.sp
    with ExitStack() as mem:
        sb = lambda n, s, d=fp32: mem.enter_context(nc.sbuf_tensor(n, s, d))
        ps = lambda n: mem.enter_context(nc.psum_tensor(n, [P, 512], fp32))
        XT = sb("XT", [P, KC, NB, T])
        steps = lambda k, t0, n: XT[:, k, :, bass.ds(t0, n)].rearrange("p b t -> p t b")
        wx0 = sb("wx0", [P, KC, D])
        wx1 = sb("wx1", [P, KC, 4 * D])
        wh0 = sb("wh0", [P, KC, D])
        wh1 = sb("wh1", [P, KC, 4 * D])
        wh0p = sb("wh0p", [P, 2, KC, D], fp16)
        wh1p = sb("wh1p", [P, 2, KC, 4 * D], fp16)
        b0 = sb("b0", [P, KC])
        b1 = sb("b1", [1, 4 * D])
        ones = sb("ones", [1, CH * NB])
        cond = sb("cond", [P, KC, NB])
        xw0p = sb("xw0p", [P, 3, KC, T, NB], bf16)
        xw1p = sb("xw1p", [P, 2, 3, GATES, CH, NB], bf16)
        rest = sb("rest", [P, 2, 512])
        ident = sb("ident", [P, P])
        scaled_ident = [sb(f"scaled_ident{l}", [P, P], bf16) for l in range(2)]
        ext = sb("ext", [P, 2, 2])
        mx = sb("mx", [P, 2])
        descale = sb("descale", [P, 2])
        scale = sb("scale", [P, 2])
        hR = sb("hR", [P, KC, CH, NB])
        hL = sb("hL", [P, KC, CH, NB])
        hpR = sb("hpR", [P, KC, 2, NB], fp16)
        hpL = sb("hpL", [P, KC, 2, NB], fp16)
        cell = sb("cell", [P, KC, NB])
        preL = sb("preL", [P, GATES, NB])
        preR = sb("preR", [P, KC, NB])
        tL = sb("tL", [P, GATES, NB])
        tR = sb("tR", [P, KC, NB])
        sg = sb("sg", [P, GATES, NB])
        u = sb("u", [P, KC, NB])
        w = sb("w", [P, KC, NB])
        tc = sb("tc", [P, KC, NB])
        psL_ifg, psL_o, psR = ps("psL_ifg"), ps("psL_o"), ps("psR")
        psX = [ps(f"psX{i}") for i in range(2)]

        for n, (dst, src) in enumerate([(wh1, "L1_cond_Wh"), (wh0, "L0_cond_Wh"), (wx0, "L0_cond_Wx"), (wx1, "L1_cond_Wx")]):
            core.dma(sp, "w", dst[:, :, :], A[src].rearrange("(k p) n -> p k n", p=P), ("loaded", src))
        core.dma(act, "x", XT[:, :, :, :], A["xT"], "x loaded")
        core.dma(sp, "w", cond[:, :, :], A["condT"], "cond loaded")
        core.dma(sp, "w", b0[:, :], A["b0T"], "b0 loaded")
        core.dma(sp, "w", ident[:, :], A["ident"], "ident loaded")
        core.dma(sp, "w", b1[:, :], A["b1row"], "small loaded")
        pool.done(pool.eng.memset(ones[:, :], 1.0), "ones")
        pool.done(pool.eng.memset(cell[:, :, :], 0.0), "cell zero")

        g_cols = slice(2 * D, 3 * D)
        dve.need("small loaded")
        for t, name in ((wh1, "wh1"), (wx1, "wx1")):
            dve.done(dve.eng.tensor_scalar(t[:, :, g_cols], t[:, :, g_cols], 2.0, None, ALU.mult), name + " doubled")
        dve.done(dve.eng.tensor_scalar(b1[:, g_cols], b1[:, g_cols], 2.0, None, ALU.mult), "b1 doubled")
        dve.need("wh1 doubled")
        for l, t in enumerate((wh0, wh1)):
            dve.done(dve.eng.tensor_reduce(ext[:, l, 0:1], t[:, :, :], AX.XY, ALU.max), f"max {l}")
            dve.done(dve.eng.tensor_reduce(ext[:, l, 1:2], t[:, :, :], AX.XY, ALU.min), f"min {l}")
        dve.need("min 1")
        dve.done(dve.eng.tensor_scalar(ext[:, :, 1:2], ext[:, :, 1:2], -1.0, None, ALU.mult), "neg min")
        dve.need("neg min")
        dve.done(dve.eng.tensor_reduce(mx[:, :], ext[:, :, :], AX.X, ALU.max), "row max")
        pool.need("row max")
        pool.done(pool.eng.partition_all_reduce(scale[:, :], mx[:, :], P, bass.bass_isa.ReduceOp.max), "max all")
        dve.need("max all")
        dve.done(dve.eng.tensor_scalar(mx[:, :], scale[:, :], 1e-6, None, ALU.max), "clamped")
        dve.need("clamped")
        dve.done(dve.eng.tensor_scalar(descale[:, :].bitcast(u32), mx[:, :].bitcast(u32), 0x7F800000, None, ALU.bitwise_and), "pow2")
        dve.need("pow2")
        dve.done(dve.eng.tensor_scalar(descale[:, :], descale[:, :], 2.0 ** -W16_EXP, None, ALU.mult), "descale")
        dve.need("descale")
        dve.done(dve.eng.reciprocal(scale[:, :], descale[:, :]), "scale")
        dve.need("scale")
        for l, (t, tp) in enumerate(((wh0, wh0p), (wh1, wh1p))):
            s = scale[:, l:l + 1]
            dve.done(dve.eng.tensor_scalar(scaled_ident[l][:, :], ident[:, :], s, None, ALU.mult), f"ident {l}")
            dve.done(dve.eng.tensor_scalar(t[:, :, :], t[:, :, :], s, None, ALU.mult), f"scaled {l}")
            dve.need(f"scaled {l}")
            dve.done(dve.eng.tensor_copy(tp[:, 0], t[:, :, :]), f"hi {l}")
            dve.need(f"hi {l}")
            dve.done(dve.eng.tensor_tensor(tp[:, 1], t[:, :, :], tp[:, 0], ALU.subtract), f"lo {l}")
        dve.need("cond loaded")
        for l, hp in enumerate((hpR, hpL)):
            dve.done(dve.eng.tensor_copy(hp[:, :, 0, :], cond[:, :, :]), f"h0 hi {l}")
            dve.need(f"h0 hi {l}")
            dve.done(dve.eng.tensor_tensor(hp[:, :, 1, :], cond[:, :, :], hp[:, :, 0, :], ALU.subtract), f"h0 lo {l}")
        pe.need("small loaded")
        core.barrier()

        NX = 512 // NB
        with nc.Fori(0, T // NX) as blk:
            for m in range(KC):
                for k in range(KC):
                    last = pe.eng.matmul(psX[m][:, :], wx0[:, k, m * P:(m + 1) * P],
                                         steps(k, blk * NX, NX), start=k == 0, stop=k == KC - 1)
                pe.done(last, ("xw0", m))
                full = rest[:, m, :]
                act.need(("xw0", m))
                act.done(act.eng.activation(full, psX[m][:, :], ACT.Identity, bias=b0[:, m:m + 1]), ("xw0 full", m))
                part = lambda q: xw0p[:, q, m, bass.ds(blk * NX, NX), :].rearrange("p t b -> p (t b)")
                dve.need(("xw0 full", m))
                dve.done(dve.eng.tensor_copy(part(0), full), ("p0", m))
                dve.need(("p0", m))
                dve.done(dve.eng.tensor_tensor(full, full, part(0), ALU.subtract), ("r0", m))
                dve.need(("r0", m))
                dve.done(dve.eng.tensor_copy(part(1), full), ("p1", m))
                dve.need(("p1", m))
                dve.done(dve.eng.tensor_tensor(part(2), full, part(1), ALU.subtract), ("p2", m))
            core.barrier()

        def parts_view(bank, slots):
            return bank[:, 0:slots * 2 * NB].rearrange("p (g q b) -> p g q b", q=2, b=NB)

        vR, vIFG, vO = parts_view(psR, KC), parts_view(psL_ifg, 6), parts_view(psL_o, 2)

        def inject(v, l, parts, event):
            for q in range(3):
                last = pe.eng.matmul(v[:, :, 0, :], scaled_ident[l][:, :], parts(q), start=q == 0, stop=False, skip_group_check=True)
            pe.done(last, event)

        def products(v, wp, hp, g0, event):
            slots = v.shape[1]
            for g in range(slots):
                for k in range(KC):
                    for q in range(2):
                        last = pe.eng.matmul(v[:, g, :, :], wp[:, q, k, (g0 + g) * P:(g0 + g + 1) * P], hp[:, k, :, :],
                                             start=False, stop=(k == KC - 1 and q == 1), skip_group_check=True)
            pe.done(last, event)

        def add_halves(dst, halves, name, key):
            dve.need((name, *key))
            dve.done(dve.eng.tensor_reduce(dst, halves.rearrange("p g q b -> p g b q"), AX.X, ALU.add), (name + " pre", *key))

        def chunk(i, par, rnn, lstm, xw):
            has = lambda *events: [e for e in events if e in core.events]
            for s in range(CH):
                key = (par, s)
                before = (par, s - 1) if s else (1 - par, CH - 1)
                prev = lambda name: (name, *before) if (name, *before) in core.events else None
                if s == CH // 2:
                    for lane, name in ((act, "hR"), (dve, "hL")):
                        lane.need(*has(("x", name, 1 - par, CH // 4 - 1, KC - 1)))
                    core.retire()
                if lstm:
                    pe.need(prev("ifg pre"))
                    inject(vIFG, 1, lambda q: xw1p[:, par, q, 0:6, s, :], ("inject ifg", *key))
                    pe.need(prev("o pre"))
                    inject(vO, 1, lambda q: xw1p[:, par, q, 6:8, s, :], ("inject o", *key))
                if rnn:
                    pe.need(prev("R pre"))
                    inject(vR, 0, lambda q: xw0p[:, q, :, bass.ds(i * CH + s, 1), :].squeeze(2), ("inject R", *key))
                if lstm:
                    pe.need(prev("hL parts"))
                    products(vIFG, wh1p, hpL, 0, ("ifg", *key))
                    products(vO, wh1p, hpL, 6, ("o", *key))
                if rnn:
                    pe.need(prev("hR parts"))
                    products(vR, wh0p, hpR, 0, ("R", *key))
                if xw and 1 <= s <= 3 * GATES // 2:
                    if s == 1:
                        pe.need(*has(("x", "hR", 1 - par, CH // 4 - 1, KC - 1)))
                    for n in (2 * s - 2, 2 * s - 1):
                        g, what = divmod(n, 3)
                        dst = psX[g // 4][:, (g % 4) * CH * NB:(g % 4 + 1) * CH * NB]
                        if what == 0:
                            if g % 4 == 0:
                                pe.need(*has(("rest", 1 - par, g // 4)))
                            last = pe.eng.matmul(dst, b1[:, g * P:(g + 1) * P], ones[:, :], start=True, stop=False)
                        else:
                            last = pe.eng.matmul(dst, wx1[:, what - 1, g * P:(g + 1) * P], steps(what - 1, (i - 1) * CH, CH), start=False, stop=what == 2)
                        if what == 2 and g % 4 == 3:
                            pe.done(last, ("xw1", par, g // 4))
                if lstm:
                    dve.need(prev("sig ifg"), prev("sig o"))
                    add_halves(preL[:, 0:6, :], vIFG, "ifg", key)
                    add_halves(preL[:, 6:8, :], vO, "o", key)
                if rnn:
                    dve.need(prev("hR"))
                    add_halves(preR[:, :, :], vR, "R", key)
                if lstm:
                    act.need(prev("hL hi"), ("ifg pre", *key))
                    act.done(act.eng.activation(sg[:, 0:6, :], preL[:, 0:6, :], ACT.Sigmoid, scale=descale[:, 1:2]), ("sig ifg", *key))
                    act.need(("o pre", *key))
                    act.done(act.eng.activation(sg[:, 6:8, :], preL[:, 6:8, :], ACT.Sigmoid, scale=descale[:, 1:2]), ("sig o", *key))
                if rnn:
                    act.need(("R pre", *key))
                    if s % 4 == 0:
                        act.need(*has(("x", "hR", 1 - par, s // 4, 1)))
                    act.done(act.eng.activation(hR[:, :, s, :], preR[:, :, :], ACT.Tanh, scale=descale[:, 0:1]), ("hR", *key))
                if lstm:
                    dve.need(("sig ifg", *key))
                    dve.done(dve.eng.scalar_tensor_tensor(u[:, :, :], sg[:, 4:6, :], -0.5, sg[:, 0:2, :], ALU.add, ALU.mult), ("u", *key))
                    dve.done(dve.eng.tensor_tensor(w[:, :, :], sg[:, 2:4, :], cell[:, :, :], ALU.mult), ("w", *key))
                    dve.need(("w", *key))
                    dve.done(dve.eng.scalar_tensor_tensor(cell[:, :, :], u[:, :, :], 2.0, w[:, :, :], ALU.mult, ALU.add), ("c", *key))
                    act.need(("c", *key))
                    act.done(act.eng.activation(tc[:, :, :], cell[:, :, :], ACT.Tanh), ("tanh c", *key))
                    dve.need(("tanh c", *key), ("sig o", *key))
                    if s % 4 == 0:
                        dve.need(*has(("x", "hL", 1 - par, s // 4, 1)))
                    dve.done(dve.eng.tensor_tensor(hL[:, :, s, :], sg[:, 6:8, :], tc[:, :, :], ALU.mult), ("hL", *key))
                    dve.done(dve.eng.tensor_tensor(hpL[:, :, 0, :], sg[:, 6:8, :], tc[:, :, :], ALU.mult), ("hL hi", *key))
                if rnn:
                    dve.need(("hR", *key), ("R", *key))
                    dve.done(dve.eng.tensor_copy(hpR[:, :, 0, :], hR[:, :, s, :]), ("hR hi", *key))
                if lstm:
                    dve.need(("hL hi", *key))
                    dve.done(dve.eng.tensor_tensor(hpL[:, :, 1, :], hL[:, :, s, :], hpL[:, :, 0, :], ALU.subtract), ("hL parts", *key))
                if rnn:
                    dve.need(("hR hi", *key))
                    dve.done(dve.eng.tensor_tensor(hpR[:, :, 1, :], hR[:, :, s, :], hpR[:, :, 0, :], ALU.subtract), ("hR parts", *key))
                if s % 4 == 3:
                    for on, h, t0, name in ((rnn, hR, i * CH, "hR"), (lstm, hL, (i - 2) * CH, "hL")):
                        if on:
                            pool.need((name, *key))
                            for k in range(KC):
                                xs = steps(k, t0 + (s - 3), 4)
                                pool.done(pool.eng.tensor_tensor(xs, xs, h[:, k, s - 3:s + 1, :], ALU.add), ("x", name, par, s // 4, k))
                if xw:
                    for n, at in ((0, 7), (1, 13)):
                        part = lambda q: xw1p[:, 1 - par, q, 4 * n:4 * n + 4, :, :].rearrange("p g t b -> p (g t b)")
                        if s == at:
                            act.need(("xw1", par, n))
                            act.need(*has(("inject ifg", 1 - par, CH - 1), ("inject o", 1 - par, CH - 1)))
                            act.done(act.eng.copy(part(0), psX[n][:, :]), ("part", par, n, 0))
                            dve.need(("part", par, n, 0))
                            dve.done(dve.eng.tensor_tensor(rest[:, n, :], psX[n][:, :], part(0), ALU.subtract), ("rest", par, n))
                        if s == at + 1:
                            act.need(("rest", par, n))
                            act.done(act.eng.copy(part(1), rest[:, n, :]), ("part", par, n, 1))
                            dve.need(("part", par, n, 1))
                            dve.done(dve.eng.tensor_tensor(part(2), rest[:, n, :], part(1), ALU.subtract), ("part", par, n, 2))
                    if s == CH - 1:
                        pe.need(("part", par, 1, 2))

        def pair(i, rnn, lstm, xw):
            for par in range(2):
                chunk(i + par, par, rnn, lstm, xw[par])
                core.next_epoch()

        pair(0, True, False, (False, True))
        core.barrier()
        pair(2, True, True, (True, True))
        with nc.Fori(2, NCH // 2) as two:
            pair(two * 2, True, True, (True, True))
        pair(NCH, False, True, (True, False))
        core.barrier()
        core.dma(sp, "x2", x2_dram, XT[:, :, :, :], "x2 out")
        core.barrier()



def load_weights(nc, core, ctx, A):
    sp, act = core.sp, core.act
    sb = lambda n, s, d=fp32: ctx.enter_context(nc.sbuf_tensor(n, s, d))
    W = {}
    sem = core.sem("weights")
    n = 0
    for name, shape in (("wqkv", [P, KC, 3 * D]), ("wo", [P, KC, D]), ("wf1", [P, KC, FF]), ("wf2", [P, FC, D]),
                        ("sw1", [P, KC, FF]), ("sw2", [P, FC, D]), ("gate_w", [P, 3 * KC, E]),
                        ("bf1", [P, FC]), ("sb1", [P, FC]), ("eb1", [P, E, FC]), ("segs", [P, 3, NQ]), ("I", [P, P])):
        W[name] = sb("W_" + name, shape)
        sp.eng.dma_start(W[name][tuple([slice(None)] * len(shape))], A[name]).then_inc(sem, 16)
        n += 16
    for name, width in (("bqkv", 3 * D), ("bo", D), ("bf2", D), ("sb2", D)):
        W[name] = sb("W_" + name, [P, width])
        sp.eng.dma_start(W[name][:, :], A[name].partition_broadcast(P)).then_inc(sem, 16)
        n += 16
    core.weights = (sem, n)
    return W


def conditioning(nc, core, A, W, ada_dram, modrow):
    pe, act, dve, pool, sp = core.pe, core.act, core.dve, core.pool, core.sp
    with ExitStack() as mem:
        sb = lambda n, s, d=fp32: mem.enter_context(nc.sbuf_tensor(n, s, d))
        wada = sb("wada", [P, KC, 6 * D])
        cond = sb("cond2", [P, KC, NB])
        silu = sb("silu", [P, KC, NB])
        timew = sb("timew", [P, KC, 2 * E])
        bada = sb("bada", [NB, 6 * D])
        timeb = sb("timeb", [1, 2 * E])
        ada = sb("ada", [NB, 6 * D])
        ps = [mem.enter_context(nc.psum_tensor(f"psA{i}", [P, 512], fp32)) for i in range(4)]
        sp.eng.wait_ge(*core.weights)
        for dst, src in ((wada[:, :, :], A["w_ada"]), (cond[:, :, :], A["condT"]), (timew[:, :, :], A["time_w"]),
                         (bada[:, :], A["b_ada"].partition_broadcast(NB)), (timeb[:, :], A["time_b"])):
            core.dma(sp, "c", dst, src, "cond in")
        pe.need("cond in")
        for j in range(3):
            for k in range(KC):
                last = pe.eng.matmul(ps[j][0:NB, :], cond[:, k, :], wada[:, k, j * 512:(j + 1) * 512], start=k == 0, stop=k == KC - 1)
            pe.done(last, ("ada", j))
            run(dve, ("ada b", j), [("ada", j), "cond in"], lambda e: e.tensor_tensor(
                ada[:, j * 512:(j + 1) * 512], ps[j][0:NB, :], bada[:, j * 512:(j + 1) * 512], ALU.add))
        for j in (1, 4):
            run(dve, ("ada 1", j), [("ada b", 2)], lambda e: e.tensor_scalar(ada[:, j * D:(j + 1) * D], ada[:, j * D:(j + 1) * D], 1.0, None, ALU.add))
        sp.need(("ada 1", 4))
        core.dma(sp, "c", ada_dram, ada[:, :], "ada out")
        act.need("cond in")
        run(act, "sigmoid", [], lambda e: e.activation(silu[:, :, :], cond[:, :, :], ACT.Sigmoid))
        run(dve, "silu", ["sigmoid"], lambda e: e.tensor_tensor(silu[:, :, :], silu[:, :, :], cond[:, :, :], ALU.mult))
        pe.need("silu")
        for b in range(NB):
            for k in range(KC):
                last = pe.eng.matmul(ps[3][0:1, b * 2 * E:(b + 1) * 2 * E], silu[:, k, b:b + 1], timew[:, k, :], start=k == 0, stop=k == KC - 1)
        pe.done(last, "mod")
        run(dve, "mod b", ["mod"], lambda e: e.tensor_tensor(
            modrow[:, :, :], ps[3][0:1, 0:NB * 2 * E].rearrange("p (b e) -> p b e", b=NB),
            timeb[:, :].unsqueeze(1).to_broadcast([1, NB, 2 * E]), ALU.add))
        run(dve, "mod 1", ["mod b"], lambda e: e.tensor_scalar(modrow[:, :, 0:E], modrow[:, :, 0:E], 1.0, None, ALU.add))
        core.barrier()


def transformer_and_experts(nc, core, A, W, x2_dram, ada_dram, modrow, out):
    pe, act, dve, pool, sp = core.pe, core.act, core.dve, core.pool, core.sp
    with ExitStack() as mem:
        sb = lambda n, s, d=fp32: mem.enter_context(nc.sbuf_tensor(n, s, d))
        PS = [mem.enter_context(nc.psum_tensor(f"bank{i}", [P, 2, 512], fp32)) for i in range(4)]
        bank = lambda i: PS[i // 2][:, i % 2, :]
        ada = sb("adab", [P, 6, D])
        ew1 = [sb(f"ew1_{i}", [P, KC, FF]) for i in range(TOPK)]
        ew2 = [sb(f"ew2_{i}", [P, FC, D]) for i in range(TOPK)]
        x3 = sb("x3", [P, NQ, D])
        x3T = sb("x3T", [P, KC, T])
        hidden = sb("hidden", [P, 3, T])
        weighted = sb("weighted", [P, NQ, D])
        expert_wm = sb("expert_wm", [P, TOPK, NQ])
        eb2 = [sb(f"eb2_{i}", [P, D]) for i in range(TOPK)]
        eb1 = sb("eb1s", [P, TOPK, FC])
        xT = sb("xT", [P, KC, T])
        x = sb("x", [P, NQ, D])
        x1 = sb("x1", [P, NQ, D])
        z = sb("z", [P, NQ, D])
        w = sb("w_", [P, NQ, D])
        zT = sb("zT", [P, KC, T])
        big = sb("big", [P, 2 * 2048])
        qkv = big[:, 0:NQ * 3 * D].rearrange("p (q a h d) -> p q a h d", q=NQ, a=3, h=H)
        spl = sb("spl", [P, 2, NQ, H, 4, HD], fp16)
        splT = sb("splT", [P, 2, H // 2, T], fp16)
        vt = sb("vt", [P, NQ, H, 2 * HD])
        pexp = sb("pexp", [P, 2, 4, 512])
        uT = pexp[:, :, :, :].rearrange("p a b c -> p (a b) c")
        oT = spl[:, 0].rearrange("p q h s d -> p (q h s d)").bitcast(fp32).rearrange("p (g t) -> p g t", g=H // 4)
        O = spl[:, 1].rearrange("p q h s d -> p (q h s d)").bitcast(fp32).rearrange("p (q h d) -> p q h d", q=NQ, h=H)
        xin = big[:, 0:KC * T].rearrange("p (k t) -> p k t", k=KC)
        pflat = pexp[:, :, :, :].rearrange("p a b c -> p (a b c)")
        st6 = sb("st6", [P, NQ, 6])
        mv = sb("mv", [P, NQ, 2])
        acc = sb("acc", [P, 8, NQ])
        S = sb("S", [P, 24, NQ])
        hs = sb("hs", [P, 4, NQ, 3 * H])
        gin = sb("gin", [P, 3, KC])
        gi = sb("gi", [P, 3, KC])
        gr = sb("gr", [1, 64])
        gidx = sb("gidx", [1, 8], u32)
        g6 = sb("g6", [1, 3 * TOPK])
        b6 = sb("b6", [P, 3 * TOPK])
        wm = sb("wm", [P, TOPK, NQ])
        ones = sb("ones_", [P, P])
        half = sb("half", [P, NQ * 3])
        mhalf = sb("mhalf", [P, NQ])
        I = W["I"]
        f3 = lambda t: t.rearrange("p a b -> p (a b)")

        run(pool, "ones", [], lambda e: e.memset(ones[:, :], 1.0))
        run(pool, "half", [], lambda e: e.memset(half[:, :], 0.5))
        run(pool, "mhalf", [], lambda e: e.memset(mhalf[:, :], -0.5))
        run(pool, "vt 0", [], lambda e: e.memset(vt[:, :, :, :], 0.0))
        run(pool, "vt 1", ["vt 0"], lambda e: e.memset(vt[:, :, :, HD:HD + 1], 1.0))
        core.barrier()

        def norm_clip(tag, out_, ss, needs, halves=None):
            run(pool, tag + " sqrt", needs, lambda e: e.tensor_tensor(out_, ss, half[:, 0:NQ] if halves is None else halves, ALU.pow))
            run(dve, tag, [tag + " sqrt"], lambda e: e.tensor_scalar(out_, out_, EPS, None, ALU.max))

        def clipped_ratio(tag, out_, n, tmp, needs):
            run(dve, tag + " r", needs, lambda e: e.reciprocal(tmp, n))
            run(dve, tag, [tag + " r"], lambda e: e.scalar_tensor_tensor(out_, n, ATMAX, tmp, ALU.min, ALU.mult))

        def to_feature_major(tag, src, dst, banks, needs):
            pe.need(*needs)
            for k in range(KC):
                for q in range(NQ):
                    last = pe.eng.transpose(bank(banks[k])[:, q * P:(q + 1) * P], src[:, q, k * P:(k + 1) * P], I[:, :])
                pe.done(last, (tag, "T", k))
            run(act, (tag, 0), [(tag, "T", 0)], lambda e: e.copy(dst[:, 0, :], bank(banks[0])), 0)
            run(dve, (tag, 1), [(tag, "T", 1)], lambda e: e.tensor_copy(dst[:, 1, :], bank(banks[1])), 0.9)

        def modulated_norm(tag, xa, j, needs):
            for q in range(NQ):
                run(dve, (tag, "st", q), needs, lambda e: e.bn_stats(st6[:, q, :], xa[:, q, :]), 0.33)
            for q in range(NQ):
                run(dve, (tag, "mv", q), [(tag, "st", q)], lambda e: e.bn_aggr(mv[:, q, :], st6[:, q, :]), 0.08)
            mu, var = mv[:, :, 0], mv[:, :, 1]
            X2, n, m, t0, t1, al = (S[:, i, :] for i in (0, 2, 3, 4, 5, 6))
            run(dve, tag + "1", [(tag, "mv", NQ - 1)], lambda e: e.tensor_tensor(t0, mu, mu, ALU.mult))
            run(dve, tag + "2", [tag + "1"], lambda e: e.tensor_tensor(t0, t0, var, ALU.add))
            run(dve, tag + " X2", [tag + "2"], lambda e: e.tensor_scalar(X2, t0, float(D), None, ALU.mult))
            norm_clip(tag + " n", n, X2, [tag + " X2"])
            run(dve, tag + "3", [tag + " n"], lambda e: e.tensor_scalar(m, n, MAXT, None, ALU.min))
            run(dve, tag + "4", [tag + "3"], lambda e: e.tensor_scalar(t0, m, -1.0, 1.0, ALU.mult, ALU.add))
            run(dve, tag + "5", [tag + "4"], lambda e: e.reciprocal(t1, t0))
            run(dve, tag + "6", [tag + "5"], lambda e: e.scalar_tensor_tensor(t0, m, 1.0, t1, ALU.add, ALU.mult))
            run(act, tag + " ln", [tag + "6"], lambda e: e.activation(t1, t0, ACT.Ln), 1.5)
            run(dve, tag + "7", [tag + " ln"], lambda e: e.reciprocal(t0, n))
            run(dve, tag + " al", [tag + "7"], lambda e: e.scalar_tensor_tensor(al, t1, 0.5, t0, ALU.mult, ALU.mult))
            run(dve, tag + "8", [tag + " al"], lambda e: e.tensor_tensor(t0, al, al, ALU.mult))
            run(dve, tag + "9", [tag + "8"], lambda e: e.tensor_tensor(t0, t0, var, ALU.mult))
            run(dve, tag + "10", [tag + "9"], lambda e: e.tensor_scalar(t0, t0, 1e-6, None, ALU.add))
            run(pool, tag + "11", [tag + "10"], lambda e: e.tensor_tensor(t1, t0, mhalf[:, :], ALU.pow))
            run(dve, tag + " r", [tag + "11"], lambda e: e.tensor_tensor(t1, t1, al, ALU.mult))
            for q in range(NQ):
                run(dve, (tag, "xn", q), [tag + " r"], lambda e: e.tensor_scalar(
                    z[:, q, :], xa[:, q, :], mv[:, q, 0:1], S[:, 5, q:q + 1], ALU.subtract, ALU.mult), 0.33)
            bc = lambda row: ada[:, row, :].unsqueeze(1).to_broadcast([P, NQ, D])
            run(dve, tag + " sc", [(tag, "xn", NQ - 1), "ada"], lambda e: e.tensor_tensor(z[:, :, :], z[:, :, :], bc(j + 1), ALU.mult), 1.2)
            run(dve, tag + " z", [tag + " sc"], lambda e: e.tensor_tensor(z[:, :, :], z[:, :, :], bc(j), ALU.add), 1.2)
            for q in range(NQ):
                run(act, (tag, "zz", q), [tag + " z"], lambda e: e.activation(big[:, q * D:(q + 1) * D], z[:, q, :], ACT.Square, accum_out=acc[:, 0, q:q + 1]), 0.4)
            norm_clip(tag + " zn", n, acc[:, 0, :], [(tag, "zz", NQ - 1)])
            clipped_ratio(tag + " s", S[:, 1, :], n, t0, [tag + " zn"])

        def mobius_update(tag, banks, bias, j, xa, xout, more, needs):
            a = z
            for q in range(NQ):
                run(dve, (tag, "a", q), needs, lambda e: e.scalar_tensor_tensor(
                    a[:, q, :], bank(banks[q // 2])[:, (q % 2) * D:(q % 2 + 1) * D], S[:, 7, q:q + 1], bias[:, :], ALU.mult, ALU.add), 0.4)
                run(act, (tag, "aa", q), [(tag, "a", q)], lambda e: e.activation(big[:, q * D:(q + 1) * D], a[:, q, :], ACT.Square, accum_out=acc[:, 1, q:q + 1]), 0)
            run(dve, tag + " w", [(tag, "a", NQ - 1)], lambda e: e.tensor_tensor(
                w[:, :, :], a[:, :, :], ada[:, j, :].unsqueeze(1).to_broadcast([P, NQ, D]), ALU.mult), 1.15)
            for q in range(NQ):
                run(act, (tag, "ww", q), [tag + " w"], lambda e: e.activation(big[:, (4 + q) * D:(5 + q) * D], w[:, q, :], ACT.Square, accum_out=acc[:, 2, q:q + 1]), 0)
                run(dve, (tag, "xw", q), [tag + " w", ((tag, "xw", q - 1) if q else None)], lambda e: e.tensor_tensor_reduce(
                    out=big[:, 8 * D:9 * D], in0=xa[:, q, :], in1=w[:, q, :], scale=1.0, scalar=0.0, op0=ALU.mult, op1=ALU.add,
                    accum_out=acc[:, 3, q:q + 1]), 0.43)
            X2, na, ca, t0, n2, th, be, XY, Y2, den, pp, rr, t1 = (S[:, i, :] for i in (0, 8, 9, 10, 11, 12, 13, 14, 15, 16, 17, 18, 19))
            norm_clip(tag + " na", na, acc[:, 1, :], [(tag, "aa", NQ - 1)])
            clipped_ratio(tag + " ca", ca, na, t0, [tag + " na"])
            run(pool, tag + " wn", [(tag, "ww", NQ - 1), tag + " ca"], lambda e: e.tensor_tensor(n2, acc[:, 2, :], half[:, 0:NQ], ALU.pow))
            run(dve, tag + " wc", [tag + " wn"], lambda e: e.tensor_tensor(n2, n2, ca, ALU.mult))
            run(dve, tag + " n2", [tag + " wc"], lambda e: e.tensor_scalar(n2, n2, EPS, None, ALU.max))
            run(act, tag + " th", [tag + " n2"], lambda e: e.activation(th, n2, ACT.Tanh))
            run(dve, tag + " rn", [tag + " n2"], lambda e: e.reciprocal(t0, n2))
            run(dve, tag + " cr", [tag + " rn"], lambda e: e.tensor_tensor(t0, t0, ca, ALU.mult))
            run(dve, tag + " be", [tag + " cr", tag + " th"], lambda e: e.tensor_tensor(be, t0, th, ALU.mult))
            run(dve, tag + " XY", [tag + " be", (tag, "xw", NQ - 1)], lambda e: e.tensor_tensor(XY, be, acc[:, 3, :], ALU.mult))
            run(dve, tag + " bb", [tag + " be"], lambda e: e.tensor_tensor(t0, be, be, ALU.mult))
            run(dve, tag + " Y2", [tag + " bb"], lambda e: e.tensor_tensor(Y2, t0, acc[:, 2, :], ALU.mult))
            run(dve, tag + " 2XY", [tag + " XY"], lambda e: e.tensor_scalar(t1, XY, 2.0, 1.0, ALU.mult, ALU.add))
            run(dve, tag + " X2Y2", [tag + " Y2"], lambda e: e.tensor_tensor(den, X2, Y2, ALU.mult))
            run(dve, tag + " den", [tag + " X2Y2", tag + " 2XY"], lambda e: e.tensor_tensor(den, den, t1, ALU.add))
            run(dve, tag + " denc", [tag + " den"], lambda e: e.tensor_scalar(den, den, EPS, None, ALU.max))
            run(dve, tag + " rden", [tag + " denc"], lambda e: e.reciprocal(t0, den))
            run(dve, tag + " num", [tag + " Y2", tag + " 2XY"], lambda e: e.tensor_tensor(pp, t1, Y2, ALU.add))
            run(dve, tag + " p", [tag + " num", tag + " rden"], lambda e: e.tensor_tensor(pp, pp, t0, ALU.mult))
            run(dve, tag + " 1-X2", [tag + " X2Y2"], lambda e: e.tensor_scalar(rr, X2, -1.0, 1.0, ALU.mult, ALU.add))
            run(dve, tag + " r1", [tag + " 1-X2"], lambda e: e.tensor_tensor(rr, rr, be, ALU.mult))
            run(dve, tag + " r", [tag + " r1", tag + " rden"], lambda e: e.tensor_tensor(rr, rr, t0, ALU.mult))
            for q in range(NQ):
                run(act, (tag, "xp", q), [tag + " p"], lambda e: e.activation(z[:, q, :], xa[:, q, :], ACT.Identity, scale=S[:, 17, q:q + 1]), 0.1)
            for q in range(NQ):
                run(dve, (tag, "x", q), [(tag, "xp", q), tag + " r"], lambda e: e.scalar_tensor_tensor(
                    xout[:, q, :], w[:, q, :], S[:, 18, q:q + 1], z[:, q, :], ALU.mult, ALU.add), 0.4)
            if more is not None:
                run(dve, tag + " out", [(tag, "x", NQ - 1)], lambda e: e.tensor_tensor(xout[:, :, :], xout[:, :, :], more[:, :, :], ALU.add), 1.15)
            else:
                core.events[tag + " out"] = core.events[(tag, "x", NQ - 1)]

        def feed_forward(hbanks, ybanks, needs):
            pe.need(*needs)

            def second(m):
                pe.need(("u", m))
                for q in range(NQ):
                    last = pe.eng.matmul(bank(ybanks[q // 2])[:, (q % 2) * D:(q % 2 + 1) * D], uT[:, m, q * P:(q + 1) * P], W["wf2"][:, m, :],
                                         start=(m == 0 and q % 2 == 0), stop=m == FC - 1, skip_group_check=True)
                pe.done(last, ("ff", m))

            for m in range(FC):
                hb = hbanks[m % len(hbanks)]
                if m >= len(hbanks):
                    pe.need(("u", m - len(hbanks)))
                for k in range(KC):
                    last = pe.eng.matmul(bank(hb), W["wf1"][:, k, m * P:(m + 1) * P], zT[:, k, :], start=k == 0, stop=k == KC - 1)
                pe.done(last, ("u ps", m))
                run(act, ("u", m), [("u ps", m)], lambda e: e.activation(uT[:, m, :], bank(hb), ACT.Identity, bias=W["bf1"][:, m:m + 1]))
                run(act, ("u sq", m), [("u", m), ("m1", "xw", NQ - 1)], lambda e: e.activation(big[:, m * T:(m + 1) * T], uT[:, m, :], ACT.Square))
                if m:
                    run(dve, ("u ss", m), [("u sq", m), ("u ss", m - 1) if m > 1 else None], lambda e: e.tensor_tensor(
                        xT[:, 0, :], big[:, 0:T] if m == 1 else xT[:, 0, :], big[:, m * T:(m + 1) * T], ALU.add))
                    second(m - 1)
            second(FC - 1)

        def experts(b):
            for s in range(TOPK):
                ei = sp.eng.value_load(gidx[:, s:s + 1], min_val=0, max_val=E - 1)
                core.dma(sp, f"e{s}", ew1[s][:, :, :], A["ew1"][bass.ds(ei, 1)].rearrange("o p k n -> p (o k) n"), ("ew", s))
                core.dma(sp, f"e{s}", ew2[s][:, :, :], A["ew2"][bass.ds(ei, 1)].rearrange("o p k n -> p (o k) n"), ("ew", s))
                core.dma(sp, f"e{s}", eb2[s][:, :], A["eb2"][bass.ds(ei, 1), :].rearrange("o n -> (o n)").partition_broadcast(P), ("ew", s))
                core.dma(sp, f"e{s}", eb1[:, s, :], A["eb1d"][bass.ds(ei, 1)].rearrange("o p n -> p (o n)"), ("ew", s))
            run(act, "x3T moved", [], lambda e: e.copy(f3(x3T[:, :, :]), f3(xT[:, :, :])))
            run(dve, "x3 moved", [], lambda e: e.tensor_copy(f3(x3[:, :, :]), f3(x1[:, :, :])))
            run(pool, "wm moved", [], lambda e: e.tensor_copy(f3(expert_wm[:, :, :]), f3(wm[:, :, :])))
            yield None
            chunks = [(n, m) for n in range(1 + TOPK) for m in range(FC)]
            half_way = FC + FC // 2
            weights = [(W["sw1"], W["sw2"], W["sb1"], W["sb2"])] + [(ew1[s], ew2[s], eb1[:, s, :], eb2[s]) for s in range(TOPK)]
            pe.need("x3T moved")
            groups = 0
            for lo, hi in ((0, half_way), (half_way, len(chunks))):
                for i in range(lo, hi + 2):
                    if i < hi:
                        n, m = chunks[i]
                        if n:
                            pe.need(("ew", n - 1))
                        if i >= lo + 2:
                            pe.need(("eh", i - 2))
                        for k in range(KC):
                            last = pe.eng.matmul(bank(4 + i % 2), weights[n][0][:, k, m * P:(m + 1) * P], x3T[:, k, :], start=k == 0, stop=k == KC - 1)
                            if k < KC - 1:
                                yield None
                        pe.done(last, ("eup", i))
                        yield None
                    if i < lo + 2:
                        later = None
                    else:
                        later = i - 2
                        n2, m2 = chunks[later]
                        first, end = later == lo or m2 == 0, later == hi - 1 or m2 == FC - 1
                        pe.need(("eh", later), *([("y out", groups - 1, q) for q in range(NQ)] if first and groups else []))
                    for q in range(NQ):
                        if q == NQ // 2:
                            if later is not None:
                                yield None
                            if i < hi:
                                run(act, ("eh", i), [("eup", i), ("esecond", i - 3) if i >= 3 else None, ("ew", n - 1) if n else None],
                                    lambda e: e.activation(hidden[:, i % 3, :], bank(4 + i % 2), ACT.Gelu_apprx_tanh, bias=weights[n][2][:, m:m + 1]))
                        if later is not None:
                            last = pe.eng.matmul(bank(6 + q // 2)[:, (q % 2) * D:(q % 2 + 1) * D], hidden[:, later % 3, q * P:(q + 1) * P], weights[n2][1][:, m2, :],
                                                 start=first and q % 2 == 0, stop=end, skip_group_check=True)
                    if later is None:
                        continue
                    pe.done(last, ("esecond", later))
                    yield None
                    if end:
                        for q in range(NQ):
                            scale = expert_wm[:, n2 - 1, q:q + 1] if n2 else 1.0
                            run(act, ("y out", groups, q), [("esecond", later), "wm moved", ("y", groups - 1, q) if groups else None], lambda e: e.activation(
                                weighted[:, q, :], bank(6 + q // 2)[:, (q % 2) * D:(q % 2 + 1) * D], ACT.Identity, scale=scale))
                        for q in range(NQ):
                            run(pool, ("y", groups, q), [("y out", groups, q), "x3 moved"], lambda e: e.tensor_tensor(x3[:, q, :], x3[:, q, :], weighted[:, q, :], ALU.add))
                        if m2 == FC - 1:
                            for q in range(NQ):
                                row = weights[n2][3][:, :]
                                if n2:
                                    run(pool, ("eb", q), [("ew", n2 - 1), ("y", groups, q)], lambda e: e.tensor_scalar(
                                        weighted[:, q, :], row, expert_wm[:, n2 - 1, q:q + 1], None, ALU.mult))
                                    row = weighted[:, q, :]
                                run(pool, ("y", groups, q), [("y", groups, q), ("eb", q) if n2 else None], lambda e: e.tensor_tensor(
                                    x3[:, q, :], x3[:, q, :], row, ALU.add))
                        groups += 1
                if hi == half_way:
                    core.events["experts' banks free"] = core.events[("y out", groups - 1, NQ - 1)]
                    yield "attention"
                    pe.need(*[e for e in (("O", 3), ("oT", 3)) if e in core.events])
            sp.need(("y", groups - 1, NQ - 1))
            core.dma(sp, "out", out[bass.ds(b, 1)].rearrange("o (q p) d -> p (o q) d", p=P), x3[:, :, :], "out")

        known = lambda *events: [e for e in events if e in core.events]

        def front(b, background):
            core.background = background
            core.dma(sp, "ada", ada[:, :, :].rearrange("p j d -> p (j d)"), ada_dram[bass.ds(b, 1), :].rearrange("o n -> (o n)").partition_broadcast(P), "ada")
            core.dma(sp, "x2", xin, x2_dram[:, :, bass.ds(b, 1), :].rearrange("p k o t -> p k (o t)"), "x2 in")
            background.open = True
            background.tick(6.0)
            pe.need("x2 in")
            for q in range(NQ):
                for k in range(KC):
                    last = pe.eng.transpose(bank(q // 2)[:, (q % 2) * D + k * P:(q % 2) * D + (k + 1) * P], xin[:, k, q * P:(q + 1) * P], I[:, :])
                if q % 2:
                    pe.done(last, ("x T", q // 2))
            run(act, "x 0", [("x T", 0)], lambda e: e.copy(f3(x[:, 0:2, :]), bank(0)))
            run(dve, "x 1", [("x T", 1)], lambda e: e.tensor_copy(f3(x[:, 2:4, :]), bank(1)))
            modulated_norm("ln1", x, 0, ["x 0", "x 1"])
            to_feature_major("zT", z, zT, (2, 3), ["ln1 z"])

            pe.need(("zT", 0), ("zT", 1))
            for q in range(NQ):
                b0, b1_ = (0, 1) if q % 2 == 0 else (2, 3)
                if q >= 2:
                    pe.need(("qkv b", q - 2))
                for (lo, hi), bk in (((0, 512), b0), ((512, 768), b1_)):
                    for k in range(KC):
                        last = pe.eng.matmul(bank(bk)[:, 0:hi - lo], zT[:, k, q * P:(q + 1) * P], W["wqkv"][:, k, lo:hi], start=k == 0, stop=k == KC - 1)
                pe.done(last, ("qkv", q))
                flat = qkv[:, q].rearrange("p a h d -> p (a h d)")
                for (lo, hi), bk, nm in (((0, 512), b0, "qkv a"), ((512, 768), b1_, "qkv b")):
                    run(dve, (nm, q), [("qkv", q), "ln1 s"], lambda e: e.scalar_tensor_tensor(
                        flat[:, lo:hi], bank(bk)[:, 0:hi - lo], S[:, 1, q:q + 1], W["bqkv"][:, lo:hi], ALU.mult, ALU.add), 0)
                run(act, ("qkv sq", q), [("qkv b", q)], lambda e: e.activation(pflat[:, q * 768:(q + 1) * 768], flat, ACT.Square), 0)
                run(dve, ("qkv ss", q), [("qkv sq", q)], lambda e: e.tensor_reduce(
                    hs[:, 0, q, :], pflat[:, q * 768:(q + 1) * 768].rearrange("p (h d) -> p h d", d=HD), AX.X, ALU.add), 4.0 if q == NQ - 1 else 0)
            hss, hf, ht = hs[:, 0], hs[:, 1], hs[:, 2]
            tot, tn, tr = acc[:, 4:7, :].rearrange("p a q -> p q a"), S[:, 20:23, :].rearrange("p a q -> p q a"), hs[:, 3, :, 0:3]
            run(dve, "tot", [("qkv ss", NQ - 1)], lambda e: e.tensor_reduce(tot, hss.rearrange("p q (a h) -> p q a h", h=H), AX.X, ALU.add))
            norm_clip("tn", tn, tot, ["tot"], half[:, 0:3 * NQ].rearrange("p (q a) -> p q a", a=3))
            run(dve, "tr", ["tn"], lambda e: e.reciprocal(tr, tn))
            run(dve, "tm", ["tr"], lambda e: e.tensor_scalar(tn, tn, ATMAX, TO_HEADS, ALU.min, ALU.mult))
            run(dve, "cs", ["tm"], lambda e: e.tensor_tensor(tn, tn, tr, ALU.mult))
            csb = tn.unsqueeze(3).to_broadcast([P, NQ, 3, H])
            h4 = lambda t: t.rearrange("p q (a h) -> p q a h", h=H)
            run(act, "h sqrt", ["tot"], lambda e: e.activation(f3(ht), f3(hss), ACT.Sqrt), 1.5)
            run(dve, "h n", ["h sqrt", "cs"], lambda e: e.tensor_tensor(h4(ht), h4(ht), csb, ALU.mult))
            run(dve, "h nc", ["h n"], lambda e: e.tensor_scalar(f3(ht), f3(ht), EPS, None, ALU.max))
            run(dve, "h r", ["h nc"], lambda e: e.reciprocal(f3(hf), f3(ht)), 1.3)
            run(dve, "h f", ["h r"], lambda e: e.scalar_tensor_tensor(f3(hf), f3(ht), ATMAX, f3(hf), ALU.min, ALU.mult))
            run(dve, "h F", ["h f"], lambda e: e.tensor_tensor(h4(hf), h4(hf), csb, ALU.mult))
            hf4 = h4(hf)
            for q in range(NQ):
                for a in (0, 1):
                    run(dve, ("qk", q, a), ["h F"], lambda e: e.tensor_tensor(
                        qkv[:, q, a], qkv[:, q, a], hf4[:, q, a, :].unsqueeze(2).to_broadcast([P, H, HD]), ALU.mult), 0.33)
                run(dve, ("v", q), ["h F"], lambda e: e.tensor_tensor(
                    vt[:, q, :, 0:HD], qkv[:, q, 2], hf4[:, q, 2, :].unsqueeze(2).to_broadcast([P, H, HD]), ALU.mult), 0.33)
                for a in (0, 1):
                    src = qkv[:, q, a]
                    dst = spl[:, a, q].rearrange("p h (s t) d -> p h s t d", t=2)
                    hi = [dst[:, :, 0, :, :], dst[:, :, :, 0, :]][a]
                    lo = [dst[:, :, 1, :, :], dst[:, :, :, 1, :]][a]
                    srcb = src.unsqueeze(2).to_broadcast([P, H, 2, HD])
                    run(act, ("hi", q, a), [("qk", q, a)], lambda e: e.copy(hi, srcb), 0)
                    run(dve, ("lo", q, a), [("hi", q, a)], lambda e: e.tensor_tensor(lo, srcb, hi, ALU.subtract), 0.6)
            I16 = I16_t
            background.open = False
            background.run_to("attention")
            for a in (0, 1):
                for hp2 in range(H // 4):
                    bk = hp2
                    v16 = bank(bk).bitcast(fp16)
                    for q in range(NQ):
                        pe.need(("lo", q, a))
                        if q == 0:
                            pe.need(("qkv b", NQ - 1) if a == 0 else ("splT", 0, hp2))
                        for j in range(2):
                            hp = 2 * hp2 + j
                            src = spl[:, a, q, 2 * hp:2 * hp + 2].rearrange("p h s d -> p (h s d)")
                            last = pe.eng.transpose(v16[:, j * 512 + q * P:j * 512 + (q + 1) * P], src, I16[:, :])
                    pe.done(last, ("splT ps", a, hp2))
                    lane = (act, dve)[hp2 % 2]
                    run(lane, ("splT", a, hp2), [("splT ps", a, hp2)], lambda e: (e.copy if lane is act else e.tensor_copy)(
                        splT[:, a, 2 * hp2:2 * hp2 + 2, :].rearrange("p j t -> p (j t)"), v16[:, :]))

            def scores(g, kc):
                for pr in range(2):
                    if (g, kc) != (0, 0):
                        pe.need(("exp", *prev_unit(g, kc), pr))
                    else:
                        pe.need(*[("splT", 1, i) for i in range(H // 4)])
                    for j in range(2):
                        hp = 2 * g + pr
                        rows = slice(64 * j, 64 * j + 64)
                        last = pe.eng.matmul(bank(2 * pr + j), splT[rows, 1, hp, kc * P:(kc + 1) * P], splT[rows, 0, hp, :], start=True, stop=True)
                    pe.done(last, ("scores", g, kc, pr))
                    if unit_no(g, kc) >= 2:
                        act.need(("av", *prev_unit(*prev_unit(g, kc))))
                    run(act, ("exp", g, kc, pr), [("scores", g, kc, pr)], lambda e: e.activation(
                        pexp[:, unit_no(g, kc) % 2, 2 * pr:2 * pr + 2, :], PS[pr][:, :, :], ACT.Exp, scale=1.0 / math.sqrt(HD)))

            def values(g, kc):
                pe.need(("exp", g, kc, 1), ("v", kc))
                if unit_no(g, kc) == 0:
                    pe.need(*known("experts' banks free"))
                if kc == 0 and g >= 2:
                    pe.need(("oT", g - 2))
                for j in range(4):
                    last = pe.eng.matmul(bank(4 + g % 2)[32 * j:32 * j + 32, :], vt[:, kc, 4 * g + j, :], pexp[:, unit_no(g, kc) % 2, j, :],
                                         start=kc == 0, stop=kc == NQ - 1, tile_position=(0, 32 * j))
                pe.done(last, ("av", g, kc))
                if kc == NQ - 1:
                    run(dve, ("oT", g), [("av", g, kc)], lambda e: e.tensor_copy(oT[:, g, :], bank(4 + g % 2)))

            def back(g):
                pe.need(("oT", g))
                if g >= 2:
                    pe.need(("O", g - 2))
                bk = 6 + g % 2
                for q in range(NQ):
                    last = pe.eng.transpose(bank(bk)[:, q * P:(q + 1) * P], oT[:, g, q * P:(q + 1) * P], I[:, :])
                pe.done(last, ("O T", g))
                run(dve, ("O", g), [("O T", g)], lambda e: e.tensor_copy(
                    O[:, :, 4 * g:4 * g + 4, :].rearrange("p q h d -> p q (h d)"), bank(bk).rearrange("p (q n) -> p q n", q=NQ)))

            unit_no = lambda g, kc: g * NQ + kc
            prev_unit = lambda g, kc: divmod(unit_no(g, kc) - 1, NQ)
            units = [(g, kc) for g in range(H // 4) for kc in range(NQ)]
            scores(*units[0])
            for n, u in enumerate(units):
                if n + 1 < len(units):
                    scores(*units[n + 1])
                values(*u)
                if u[1] == 1 and u[0] > 0:
                    back(u[0] - 1)
            back(H // 4 - 1)
            background.go_on()

            o3 = O[:, :, :, 0:HD]
            oss, ond, oh, of, ot = (hs[:, i, :, 0:H] for i in (0, 1, 2, 3, 3))
            sqv = big[:, 0:NQ * D].rearrange("p (q h d) -> p q h d", q=NQ, h=H)
            run(act, "o sq", [("O", 3)], lambda e: e.activation(sqv, o3, ACT.Square), 1.0)
            run(dve, "o ss", ["o sq"], lambda e: e.tensor_reduce(oss, sqv, AX.X, ALU.add), 1.2)
            run(dve, "o rd", ["o ss"], lambda e: e.reciprocal(ond, O[:, :, :, HD]))
            run(act, "o sqrt", ["o ss"], lambda e: e.activation(oh, oss, ACT.Sqrt), 1.0)
            run(dve, "o nh", ["o sqrt", "o rd"], lambda e: e.tensor_tensor(oh, oh, ond, ALU.mult))
            run(dve, "o nc", ["o nh"], lambda e: e.tensor_scalar(oh, oh, EPS, None, ALU.max))
            run(dve, "o r", ["o nc"], lambda e: e.reciprocal(of, oh))
            run(dve, "o m", ["o r"], lambda e: e.scalar_tensor_tensor(of, oh, ATMAX, of, ALU.min, ALU.mult))
            run(dve, "o f", ["o m"], lambda e: e.scalar_tensor_tensor(of, of, FROM_HEADS, ond, ALU.mult, ALU.mult))
            run(dve, "o t", ["o f"], lambda e: e.tensor_tensor(
                z[:, :, :].rearrange("p q (h d) -> p q h d", h=H), o3, of.unsqueeze(3).to_broadcast([P, NQ, H, HD]), ALU.mult), 1.2)
            run(dve, "o ff", ["o f"], lambda e: e.tensor_tensor(oh, of, of, ALU.mult))
            run(dve, "o ffs", ["o ff"], lambda e: e.tensor_tensor(oh, oh, oss, ALU.mult))
            run(dve, "t ss", ["o ffs"], lambda e: e.tensor_reduce(acc[:, 7, :], oh, AX.X, ALU.add))
            norm_clip("t n", S[:, 8, :], acc[:, 7, :], ["t ss"])
            clipped_ratio("t s", S[:, 7, :], S[:, 8, :], S[:, 9, :], ["t n"])
            to_feature_major("tT", z, zT, (0, 1), ["o t", ("exp", 3, 3, 1)])
            pe.need(("tT", 0), ("tT", 1))
            for q in range(NQ):
                for k in range(KC):
                    last = pe.eng.matmul(bank(2 + q // 2)[:, (q % 2) * D:(q % 2 + 1) * D], zT[:, k, q * P:(q + 1) * P], W["wo"][:, k, :], start=k == 0, stop=k == KC - 1)
            pe.done(last, "wo")
            mobius_update("m1", (2, 3), W["bo"], 2, x, x1, None, ["wo", "t s", ("tT", "T", 1)])

            modulated_norm("ln2", x1, 3, ["m1 out"])
            for q in range(NQ):
                run(dve, ("zs", q), ["ln2 s"], lambda e: e.tensor_scalar(z[:, q, :], z[:, q, :], S[:, 1, q:q + 1], None, ALU.mult), 0.27)
            to_feature_major("zsT", z, zT, (0, 1), [("zs", NQ - 1)])
            background.open = False
            feed_forward((0, 1), (2, 3), [("zsT", 0), ("zsT", 1)])
            background.open = True
            pe.need(("u ss", FC - 1))
            for q in range(NQ):
                last = pe.eng.matmul(bank(0)[:, q:q + 1], xT[:, 0, q * P:(q + 1) * P], ones[:, 0:1], start=q == 0, stop=True, skip_group_check=True)
            pe.done(last, "u tot")
            run(dve, "u out", ["u tot"], lambda e: e.tensor_copy(acc[:, 7, :], bank(0)[:, 0:NQ]))
            norm_clip("u n", S[:, 8, :], acc[:, 7, :], ["u out"])
            clipped_ratio("u s", S[:, 7, :], S[:, 8, :], S[:, 9, :], ["u n"])
            mobius_update("m2", (2, 3), W["bf2"], 5, x1, x1, x, [("ff", FC - 1), "u s", ("zsT", "T", 1)])

            to_feature_major("x3T", x1, xT, (0, 1), ["m2 out", "u tot"])
            for n, (lo, hi) in enumerate(SEGS):
                run(dve, ("seg", n), [("x3T", 0), ("x3T", 1)], lambda e: e.tensor_reduce(gin[:, n, :], xT[:, :, lo:hi], AX.X, ALU.add), 0.43)
            nhp = T - SEG
            run(dve, "g hp", [("seg", 2)], lambda e: e.tensor_tensor(gi[:, 1, :], gin[:, 0, :], gin[:, 2, :], ALU.add))
            run(dve, "g wp", [("seg", 2)], lambda e: e.tensor_tensor(gi[:, 2, :], gin[:, 1, :], gin[:, 2, :], ALU.add))
            run(dve, "g all", ["g hp"], lambda e: e.tensor_tensor(gi[:, 0, :], gi[:, 1, :], gin[:, 1, :], ALU.add))
            run(dve, "g m0", ["g all"], lambda e: e.tensor_scalar(gi[:, 0, :], gi[:, 0, :], 1.0 / T, None, ALU.mult))
            run(dve, "g m1", ["g all", "g wp"], lambda e: e.tensor_scalar(gi[:, 1:3, :], gi[:, 1:3, :], 1.0 / nhp, None, ALU.mult))
            pe.need("g m1", "u out")
            for n in range(3):
                for k in range(KC):
                    last = pe.eng.matmul(bank(2)[0:1, 0:E], gi[:, n, k:k + 1], W["gate_w"][:, n * KC + k, :], start=(n, k) == (0, 0), stop=(n, k) == (2, KC - 1))
            pe.done(last, "logits")
            G = lambda i, m=8: gr[:, 8 * i:8 * i + m]
            run(dve, "l b", ["logits"], lambda e: e.tensor_tensor(G(0, E), bank(2)[0:1, 0:E], gateb[:, :], ALU.add))
            run(dve, "l s", ["l b"], lambda e: e.tensor_tensor(G(0, E), G(0, E), modrow[:, bass.ds(b, 1), 0:E], ALU.mult))
            run(dve, "l t", ["l s"], lambda e: e.tensor_tensor(G(0, E), G(0, E), modrow[:, bass.ds(b, 1), E:2 * E], ALU.add))
            run(dve, "l max", ["l t"], lambda e: e.tensor_reduce(G(1, 1), G(0, E), AX.X, ALU.max, negate=True))
            run(dve, "pad", [], lambda e: e.memset(G(2), -1.0))
            run(act, "l exp", ["l max", "pad"], lambda e: e.activation(G(2, E), G(0, E), ACT.Exp, bias=G(1, 1)))
            run(dve, "l sum", ["l exp"], lambda e: e.tensor_reduce(G(3, 1), G(2, E), AX.X, ALU.add))
            run(dve, "l rs", ["l sum"], lambda e: e.reciprocal(G(3, 1), G(3, 1)))
            run(dve, "l p", ["l rs"], lambda e: e.tensor_scalar(G(2, E), G(2, E), G(3, 1), None, ALU.mult))
            run(dve, "top", ["l p"], lambda e: e.max(G(4), G(2)))
            run(dve, "idx", ["top", *known(("ew", 0), ("ew", 1))], lambda e: e.max_index(gidx[:, :], G(4), G(2)))
            run(dve, "w sum", ["top"], lambda e: e.tensor_reduce(G(5, 1), G(4, TOPK), AX.X, ALU.add))
            run(dve, "w eps", ["w sum"], lambda e: e.tensor_scalar(G(5, 1), G(5, 1), 1e-8, None, ALU.add))
            run(dve, "w r", ["w eps"], lambda e: e.reciprocal(G(5, 1), G(5, 1)))
            run(dve, "w n", ["w r"], lambda e: e.tensor_scalar(G(4, TOPK), G(4, TOPK), G(5, 1), None, ALU.mult))
            run(dve, "idx f", ["idx"], lambda e: e.tensor_copy(G(6), gidx[:, :]))
            for n, masked in ((0, 2.0), (1, 1.0)):
                run(dve, ("g6", n), ["idx f", "w n"], lambda e: e.scalar_tensor_tensor(
                    g6[:, n * TOPK:(n + 1) * TOPK], G(6, TOPK), masked, G(4, TOPK), ALU.not_equal, ALU.mult))
            run(dve, "g6", ["w n"], lambda e: e.tensor_copy(g6[:, 2 * TOPK:3 * TOPK], G(4, TOPK)))
            run(pe, "b6 ps", ["g6", "l b"], lambda e: e.matmul(bank(2)[:, 0:3 * TOPK], ones[0:1, :], g6[:, :], start=True, stop=True))
            run(dve, "b6", ["b6 ps"], lambda e: e.tensor_copy(b6[:, :], bank(2)[:, 0:3 * TOPK]))
            for s in range(TOPK):
                for n in range(3):
                    seg, fac = W["segs"][:, n, :], b6[:, n * TOPK + s:n * TOPK + s + 1]
                    if n == 0:
                        run(dve, ("wm", s, n), ["b6"], lambda e: e.tensor_scalar(wm[:, s, :], seg, fac, None, ALU.mult))
                    else:
                        run(dve, ("wm", s, n), [("wm", s, n - 1)], lambda e: e.scalar_tensor_tensor(wm[:, s, :], seg, fac, wm[:, s, :], ALU.mult, ALU.add))

            background.open = False
            background.run_to("end")
            core.barrier()

        I16_t = sb("I16", [P, P], fp16)
        gateb = sb("gateb", [1, E])
        core.dma(sp, "c", gateb[:, :], A["gate_b"], "gateb")
        run(dve, "I16", [], lambda e: e.tensor_copy(I16_t[:, :], I[:, :]))
        core.barrier()
        front(0, Background())
        with nc.Fori(1, NB) as b:
            front(b, Background(experts(b - 1)))
        Background(experts(NB - 1)).run_to("end")
        core.barrier()


def program(nc, A, out):
    with ExitStack() as ctx:
        core = Core(nc, ctx)
        modrow = ctx.enter_context(nc.sbuf_tensor("modrow", [1, NB, 2 * E], fp32))
        ada_dram = nc.dram_tensor("ada_scratch", (NB, 6 * D), fp32, kind="Internal").ap()
        x2_dram = nc.dram_tensor("x2_scratch", (P, KC, NB, T), fp32, kind="Internal").ap()
        W = load_weights(nc, core, ctx, A)
        recurrences(nc, core, ctx, A, x2_dram)
        conditioning(nc, core, A, W, ada_dram, modrow)
        transformer_and_experts(nc, core, A, W, x2_dram, ada_dram, modrow, out)


def kernel(**inputs):
    import numpy as np
    import concourse.bacc as bacc
    from concourse.bass_utils import run_bass_kernel_spmd

    f = {n: np.ascontiguousarray(a) for n, a in inputs.items()}
    L2 = lambda n: f["L2_cond_" + n]
    L3 = lambda n: f["L3_cond_" + n]
    ifgo = lambda a: np.concatenate([a[..., 0:D], a[..., D:2 * D], a[..., 3 * D:], a[..., 2 * D:3 * D]], axis=-1)
    rows = lambda a: a.reshape(-1, P, a.shape[-1]).transpose(1, 0, 2)
    cols = lambda a: a.reshape(-1, P).T
    token = np.arange(T).reshape(NQ, P).T
    arrays = {
        "xT": f["x"].transpose(2, 0, 1).reshape(KC, P, NB, T).transpose(1, 0, 2, 3),
        "condT": rows(f["cond_1024"].T),
        "b0T": cols(f["L0_cond_b"]),
        "b1row": ifgo(f["L1_cond_b"])[None, :],
        "L0_cond_Wx": f["L0_cond_Wx"], "L0_cond_Wh": f["L0_cond_Wh"],
        "L1_cond_Wx": ifgo(f["L1_cond_Wx"]), "L1_cond_Wh": ifgo(f["L1_cond_Wh"]),
        "ident": np.eye(P, dtype=np.float32), "I": np.eye(P, dtype=np.float32),
        "segs": np.stack([(token >= lo) & (token < hi) for lo, hi in SEGS], axis=1).astype(np.float32),
        "wqkv": rows(np.concatenate([L2("w_q"), L2("w_k"), L2("w_v")], axis=1)),
        "bqkv": np.concatenate([L2("b_q"), L2("b_k"), L2("b_v")]),
        "wo": rows(L2("w_o")), "bo": L2("b_o"), "wf1": rows(L2("w_f1")), "bf1": cols(L2("b_f1")),
        "wf2": rows(L2("w_f2")), "bf2": L2("b_f2"), "w_ada": rows(L2("w_ada")), "b_ada": L2("b_ada"),
        "gate_w": rows(L3("gate_w")), "gate_b": L3("gate_b")[None, :], "time_w": rows(L3("time_w")), "time_b": L3("time_b")[None, :],
        "ew1": np.stack([rows(L3("ew1")[e]) for e in range(E)]), "ew2": np.stack([rows(L3("ew2")[e]) for e in range(E)]),
        "eb1": np.stack([cols(L3("eb1")[e]) for e in range(E)], axis=1), "eb1d": np.stack([cols(L3("eb1")[e]) for e in range(E)]),
        "eb2": L3("eb2"),
        "sw1": rows(L3("sw1")), "sb1": cols(L3("sb1")), "sw2": rows(L3("sw2")), "sb2": L3("sb2"),
    }
    arrays = {n: np.ascontiguousarray(a) for n, a in arrays.items()}
    nc = bacc.Bacc("TRN2", target_bir_lowering=False, num_devices=1)
    A = {n: nc.dram_tensor("in_" + n, a.shape, mybir.dt.from_np(a.dtype), kind="ExternalInput").ap() for n, a in arrays.items()}
    out = nc.dram_tensor("out_x", (NB, T, D), fp32, kind="ExternalOutput").ap()
    program(nc, A, out)
    r = run_bass_kernel_spmd(nc, [{"in_" + n: a for n, a in arrays.items()}], core_ids=[0])
    return r.results[0]["out_x"]
```

```python
import math
from contextlib import ExitStack

import numpy as np

import concourse.bass as bass
from concourse import mybir

fp32 = mybir.dt.float32
fp16 = mybir.dt.float16
bf16 = mybir.dt.bfloat16
u32 = mybir.dt.uint32
ALU = mybir.AluOpType
ACT = mybir.ActivationFunctionType
AX = mybir.AxisListType

P = 128
NB, T, D = 8, 512, 256
KC = D // P
GATES = 4 * D // P
CH = 16
NCH = T // CH
H, HD = 16, 16
FF = 1024
FC = FF // P
E, TOPK = 4, 2
NQ = T // P
EPS = 1e-7
MAXT = float(np.float32(1.0 - 1e-5))
ATMAX = math.atanh(MAXT)
beta = lambda a, b: math.exp(math.lgamma(a) + math.lgamma(b) - math.lgamma(a + b))
TO_HEADS = beta(HD / 2, 0.5) / beta(D / 2, 0.5)
FROM_HEADS = 1.0 / TO_HEADS
SEG = T // 3
SEGS = [(0, SEG), (SEG, 2 * SEG), (2 * SEG, T)]
W16_EXP = 14


class Lane:

    def __init__(self, name, eng, sems, core):
        self.name, self.eng, self.sems, self.core = name, eng, sems, core
        self.count, self.seen = [0, 0], {}

    def done(self, ins, event):
        epoch = self.core.epoch
        self.count[epoch] += 1
        ins.then_inc(self.sems[epoch], 1)
        self.core.events[event] = (self.sems[epoch], self.count[epoch])
        return ins

    def need(self, *events):
        for event in events:
            if event is None:
                continue
            sem, count = self.core.events[event]
            if self.seen.get(sem.name, 0) < count:
                self.eng.wait_ge(sem, count)
                self.seen[sem.name] = count


class Core:

    def __init__(self, nc, ctx):
        self.nc, self.events, self.epoch = nc, {}, 0
        self.sem = lambda n: ctx.enter_context(nc.semaphore(n))
        mk = lambda n, e: Lane(n, e, [self.sem(f"n_{n}_{i}") for i in range(2)], self)
        self.pe, self.act, self.dve = mk("pe", nc.tensor), mk("act", nc.scalar), mk("dve", nc.vector)
        self.pool, self.sp = mk("pool", nc.gpsimd), mk("sp", nc.sync)
        self.lanes = [self.pe, self.act, self.dve, self.pool, self.sp]
        self.others = [l for l in self.lanes if l is not self.pool]
        self.dma_sems, self.dma_used = {}, {}
        self.gather = self.sem("gather")
        self.release = {l.name: self.sem("go_" + l.name) for l in self.others}
        self.passed = [self.sem(f"passed_{i}") for i in range(2)]
        self.ready = [{l.name: self.sem(f"ready_{i}_{l.name}") for l in self.others} for i in range(2)]
        self.retired = [False, False]
        self.background = Background()

    def dma(self, lane, stream, out, in_, event):
        if stream not in self.dma_sems:
            self.dma_sems[stream] = self.sem("dma_" + stream)
            self.dma_used[stream] = 0
        self.dma_used[stream] += 16
        lane.eng.dma_start(out, in_).then_inc(self.dma_sems[stream], 16)
        self.events[event] = (self.dma_sems[stream], self.dma_used[stream])

    def zero(self, epoch):
        for lane in self.lanes:
            if lane.count[epoch]:
                self.pool.eng.sem_inc(lane.sems[epoch], -lane.count[epoch])
            lane.count[epoch] = 0

    def retire(self):
        old, pool = 1 - self.epoch, self.pool
        if not any(l.count[old] for l in self.lanes):
            return
        for lane in self.others:
            lane.eng.sem_inc(self.passed[old], 1)
        pool.eng.wait_ge(self.passed[old], len(self.others))
        for lane in self.lanes:
            if lane.count[old]:
                pool.eng.wait_ge(lane.sems[old], lane.count[old])
        self.zero(old)
        pool.eng.sem_inc(self.passed[old], -len(self.others))
        for lane in self.others:
            pool.eng.sem_inc(self.ready[old][lane.name], 1)
        self.retired[old] = True

    def next_epoch(self):
        self.epoch = 1 - self.epoch
        if self.retired[self.epoch]:
            for lane in self.others:
                lane.eng.wait_ge(self.ready[self.epoch][lane.name], 1)
                lane.eng.sem_inc(self.ready[self.epoch][lane.name], -1)
        self.retired[self.epoch] = False
        mine = {l.sems[self.epoch].name for l in self.lanes}
        self.events = {e: v for e, v in self.events.items() if v[0].name not in mine}
        for lane in self.lanes:
            for l in self.lanes:
                lane.seen.pop(l.sems[self.epoch].name, None)

    def barrier(self):
        pool = self.pool
        for stream, used in self.dma_used.items():
            if used:
                pool.eng.wait_ge(self.dma_sems[stream], used)
        for lane in self.lanes:
            lane.eng.drain().then_inc(self.gather, 1)
        pool.eng.wait_ge(self.gather, len(self.lanes))
        for epoch in (0, 1):
            self.zero(epoch)
            if self.retired[epoch]:
                for lane in self.others:
                    pool.eng.sem_inc(self.ready[epoch][lane.name], -1)
                self.retired[epoch] = False
        for stream, used in self.dma_used.items():
            if used:
                pool.eng.sem_inc(self.dma_sems[stream], -used)
            self.dma_used[stream] = 0
        pool.eng.sem_inc(self.gather, -len(self.lanes))
        for lane in self.others:
            pool.eng.sem_inc(self.release[lane.name], 1)
        for lane in self.others:
            lane.eng.wait_ge(self.release[lane.name], 1)
            lane.eng.sem_inc(self.release[lane.name], -1)
        for lane in self.lanes:
            lane.seen = {}
        self.events.clear()


class Background:

    AT_ONCE = 2

    def __init__(self, steps=(), side=()):
        self.side = iter(side)
        self.steps, self.credit, self.open, self.mark = iter(steps), 0.0, False, None
        self.pace = 0.9

    def tick(self, us):
        if not self.open:
            return
        self.credit += us
        while self.credit >= self.pace and not self.mark:
            self.credit -= self.pace
            self.step()

    def step(self):
        was, self.open = self.open, False
        self.mark = next(self.steps, "end")
        for _ in range(self.AT_ONCE):
            next(self.side, None)
        self.open = was

    def run(self, steps):
        for _ in range(steps):
            if self.mark != "end":
                self.step()

    def finish_side(self):
        was, self.open = self.open, False
        for _ in self.side:
            pass
        self.open = was

    def run_to(self, mark):
        while self.mark not in (mark, "end"):
            self.step()

    def go_on(self, pace):
        self.open, self.mark, self.credit, self.pace = True, None, 0.0, pace


TICK = {"dve": 0.2, "act": 0.2, "pool": 1.0, "pe": 0.0}


def run(lane, event, needs, issue, us=None):
    lane.need(*needs)
    ins = lane.done(issue(lane.eng), event)
    lane.core.background.tick(TICK[lane.name] if us is None else us)
    return ins


def recurrences(nc, core, ctx, A, x2_dram, prefetch):
    pe, act, dve, pool, sp = core.pe, core.act, core.dve, core.pool, core.sp
    with ExitStack() as mem:
        sb = lambda n, s, d=fp32: mem.enter_context(nc.sbuf_tensor(n, s, d))
        ps = lambda n: mem.enter_context(nc.psum_tensor(n, [P, 512], fp32))
        XT = sb("XT", [P, KC, NB, T])
        steps = lambda k, t0, n: XT[:, k, :, bass.ds(t0, n)].rearrange("p b t -> p t b")
        wx0 = sb("wx0", [P, KC, D])
        wx1 = sb("wx1", [P, KC, 4 * D])
        wh0 = sb("wh0", [P, KC, D])
        wh1 = sb("wh1", [P, KC, 4 * D])
        wh0p = sb("wh0p", [P, 2, KC, D], fp16)
        wh1p = sb("wh1p", [P, 2, KC, 4 * D], fp16)
        b0 = sb("b0", [P, KC])
        b1 = sb("b1", [1, 4 * D])
        ones = sb("ones", [1, CH * NB])
        cond = sb("cond", [P, KC, NB])
        xw0p = sb("xw0p", [P, 3, KC, T, NB], bf16)
        xw1p = sb("xw1p", [P, 2, 3, GATES, CH, NB], bf16)
        rest = sb("rest", [P, 2 * KC, 512])
        ident = sb("ident", [P, P])
        scaled_ident = [sb(f"scaled_ident{l}", [P, P], bf16) for l in range(2)]
        ext = sb("ext", [P, 2, 2])
        mx = sb("mx", [P, 2])
        descale = sb("descale", [P, 2])
        scale = sb("scale", [P, 2])
        hR = sb("hR", [P, KC, CH, NB])
        hL = sb("hL", [P, KC, CH, NB])
        hpR = sb("hpR", [P, KC, 2, NB], fp16)
        hpL = sb("hpL", [P, KC, 2, NB], fp16)
        cell = sb("cell", [P, KC, NB])
        preL = sb("preL", [P, GATES, NB])
        preR = sb("preR", [P, KC, NB])
        tL = sb("tL", [P, GATES, NB])
        tR = sb("tR", [P, KC, NB])
        sg = sb("sg", [P, GATES, NB])
        u = sb("u", [P, KC, NB])
        w = sb("w", [P, KC, NB])
        tc = sb("tc", [P, KC, NB])
        psL_ifg, psL_o, psR = ps("psL_ifg"), ps("psL_o"), ps("psR")
        psX = [ps(f"psX{i}") for i in range(2)]

        for n, (dst, src) in enumerate([(wh1, "L1_cond_Wh"), (wh0, "L0_cond_Wh"), (wx0, "L0_cond_Wx"), (wx1, "L1_cond_Wx")]):
            core.dma(sp, "w", dst[:, :, :], A[src].rearrange("(k p) n -> p k n", p=P), ("loaded", src))
        core.dma(act, "x", XT[:, :, :, :], A["xT"], "x loaded")
        core.dma(sp, "w", cond[:, :, :], A["condT"], "cond loaded")
        core.dma(sp, "w", b0[:, :], A["b0T"], "b0 loaded")
        core.dma(sp, "w", ident[:, :], A["ident"], "ident loaded")
        core.dma(sp, "w", b1[:, :], A["b1row"], "small loaded")
        prefetch.start()
        pool.done(pool.eng.memset(ones[:, :], 1.0), "ones")
        pool.done(pool.eng.memset(cell[:, :, :], 0.0), "cell zero")

        g_cols = slice(2 * D, 3 * D)
        dve.need("small loaded")
        for t, name in ((wh1, "wh1"), (wx1, "wx1")):
            dve.done(dve.eng.tensor_scalar(t[:, :, g_cols], t[:, :, g_cols], 2.0, None, ALU.mult), name + " doubled")
        dve.done(dve.eng.tensor_scalar(b1[:, g_cols], b1[:, g_cols], 2.0, None, ALU.mult), "b1 doubled")
        dve.need("wh1 doubled")
        for l, t in enumerate((wh0, wh1)):
            dve.done(dve.eng.tensor_reduce(ext[:, l, 0:1], t[:, :, :], AX.XY, ALU.max), f"max {l}")
            dve.done(dve.eng.tensor_reduce(ext[:, l, 1:2], t[:, :, :], AX.XY, ALU.min), f"min {l}")
        dve.need("min 1")
        dve.done(dve.eng.tensor_scalar(ext[:, :, 1:2], ext[:, :, 1:2], -1.0, None, ALU.mult), "neg min")
        dve.need("neg min")
        dve.done(dve.eng.tensor_reduce(mx[:, :], ext[:, :, :], AX.X, ALU.max), "row max")
        pool.need("row max")
        pool.done(pool.eng.partition_all_reduce(scale[:, :], mx[:, :], P, bass.bass_isa.ReduceOp.max), "max all")
        dve.need("max all")
        dve.done(dve.eng.tensor_scalar(mx[:, :], scale[:, :], 1e-6, None, ALU.max), "clamped")
        dve.need("clamped")
        dve.done(dve.eng.tensor_scalar(descale[:, :].bitcast(u32), mx[:, :].bitcast(u32), 0x7F800000, None, ALU.bitwise_and), "pow2")
        dve.need("pow2")
        dve.done(dve.eng.tensor_scalar(descale[:, :], descale[:, :], 2.0 ** -W16_EXP, None, ALU.mult), "descale")
        dve.need("descale")
        dve.done(dve.eng.reciprocal(scale[:, :], descale[:, :]), "scale")
        dve.need("scale")
        for l, (t, tp) in enumerate(((wh0, wh0p), (wh1, wh1p))):
            s = scale[:, l:l + 1]
            dve.done(dve.eng.tensor_scalar(scaled_ident[l][:, :], ident[:, :], s, None, ALU.mult), f"ident {l}")
            dve.done(dve.eng.tensor_scalar(t[:, :, :], t[:, :, :], s, None, ALU.mult), f"scaled {l}")
            dve.need(f"scaled {l}")
            dve.done(dve.eng.tensor_copy(tp[:, 0], t[:, :, :]), f"hi {l}")
            dve.need(f"hi {l}")
            dve.done(dve.eng.tensor_tensor(tp[:, 1], t[:, :, :], tp[:, 0], ALU.subtract), f"lo {l}")
        dve.need("cond loaded")
        for l, hp in enumerate((hpR, hpL)):
            dve.done(dve.eng.tensor_copy(hp[:, :, 0, :], cond[:, :, :]), f"h0 hi {l}")
            dve.need(f"h0 hi {l}")
            dve.done(dve.eng.tensor_tensor(hp[:, :, 1, :], cond[:, :, :], hp[:, :, 0, :], ALU.subtract), f"h0 lo {l}")
        pe.need("small loaded")
        core.barrier()

        NX, BLOCKS = 512 // NB, 4
        with nc.Fori(0, T // NX // BLOCKS) as turn:
            for n in range(BLOCKS):
                t0 = (turn * BLOCKS + n) * NX
                part = lambda q, m: xw0p[:, q, m, bass.ds(t0, NX), :].rearrange("p t b -> p (t b)")
                full = lambda m: rest[:, n % 2 * KC + m, :]
                for m in range(KC):
                    bank = (psX, (psR, psL_ifg))[n % 2][m]
                    pe.need(("xw0 full", n - 2, m) if n >= 2 else None)
                    for k in range(KC):
                        last = pe.eng.matmul(bank[:, :], wx0[:, k, m * P:(m + 1) * P], steps(k, t0, NX), start=k == 0, stop=k == KC - 1)
                    pe.done(last, ("xw0", n, m))
                    act.need(("xw0", n, m), ("p2", n - 2, m) if n >= 2 else None)
                    act.done(act.eng.activation(full(m), bank[:, :], ACT.Identity, bias=b0[:, m:m + 1]), ("xw0 full", n, m))
                for m in range(KC):
                    dve.need(("xw0 full", n, m))
                    dve.done(dve.eng.tensor_copy(part(0, m), full(m)), ("p0", n, m))
                for m in range(KC):
                    dve.need(("p0", n, m))
                    dve.done(dve.eng.tensor_tensor(full(m), full(m), part(0, m), ALU.subtract), ("r0", n, m))
                    act.need(("r0", n, m))
                    act.done(act.eng.copy(part(1, m), full(m)), ("p1", n, m))
                for m in range(KC):
                    dve.need(("p1", n, m))
                    dve.done(dve.eng.tensor_tensor(part(2, m), full(m), part(1, m), ALU.subtract), ("p2", n, m))
            core.barrier()

        def parts_view(bank, slots):
            return bank[:, 0:slots * 2 * NB].rearrange("p (g q b) -> p g q b", q=2, b=NB)

        vR, vIFG, vO = parts_view(psR, KC), parts_view(psL_ifg, 6), parts_view(psL_o, 2)

        def inject(v, l, parts, event):
            for q in range(3):
                last = pe.eng.matmul(v[:, :, 0, :], scaled_ident[l][:, :], parts(q), start=q == 0, stop=False, skip_group_check=True)
            pe.done(last, event)

        def products(v, wp, hp, g0, event):
            slots = v.shape[1]
            for g in range(slots):
                for k in range(KC):
                    for q in range(2):
                        last = pe.eng.matmul(v[:, g, :, :], wp[:, q, k, (g0 + g) * P:(g0 + g + 1) * P], hp[:, k, :, :],
                                             start=False, stop=(k == KC - 1 and q == 1), skip_group_check=True)
            pe.done(last, event)

        def add_halves(dst, halves, name, key):
            dve.need((name, *key))
            dve.done(dve.eng.tensor_reduce(dst, halves.rearrange("p g q b -> p g b q"), AX.X, ALU.add), (name + " pre", *key))

        def chunk(i, par, rnn, lstm, xw):
            has = lambda *events: [e for e in events if e in core.events]
            for s in range(CH):
                key = (par, s)
                before = (par, s - 1) if s else (1 - par, CH - 1)
                prev = lambda name: (name, *before) if (name, *before) in core.events else None
                if s == CH // 2:
                    for lane, name in ((act, "hR"), (dve, "hL")):
                        lane.need(*has(("x", name, 1 - par, CH // 4 - 1, KC - 1)))
                    core.retire()
                if lstm:
                    pe.need(prev("ifg pre"))
                    inject(vIFG, 1, lambda q: xw1p[:, par, q, 0:6, s, :], ("inject ifg", *key))
                    pe.need(prev("o pre"))
                    inject(vO, 1, lambda q: xw1p[:, par, q, 6:8, s, :], ("inject o", *key))
                if rnn:
                    pe.need(prev("R pre"))
                    inject(vR, 0, lambda q: xw0p[:, q, :, bass.ds(i * CH + s, 1), :].squeeze(2), ("inject R", *key))
                if lstm:
                    pe.need(prev("hL parts"))
                    products(vIFG, wh1p, hpL, 0, ("ifg", *key))
                    products(vO, wh1p, hpL, 6, ("o", *key))
                if rnn:
                    pe.need(prev("hR parts"))
                    products(vR, wh0p, hpR, 0, ("R", *key))
                if xw and 1 <= s <= 3 * GATES // 2:
                    if s == 1:
                        pe.need(*has(("x", "hR", 1 - par, CH // 4 - 1, KC - 1)))
                    for n in (2 * s - 2, 2 * s - 1):
                        g, what = divmod(n, 3)
                        dst = psX[g // 4][:, (g % 4) * CH * NB:(g % 4 + 1) * CH * NB]
                        if what == 0:
                            if g % 4 == 0:
                                pe.need(*has(("rest", 1 - par, g // 4)))
                            last = pe.eng.matmul(dst, b1[:, g * P:(g + 1) * P], ones[:, :], start=True, stop=False)
                        else:
                            last = pe.eng.matmul(dst, wx1[:, what - 1, g * P:(g + 1) * P], steps(what - 1, (i - 1) * CH, CH), start=False, stop=what == 2)
                        if what == 2 and g % 4 == 3:
                            pe.done(last, ("xw1", par, g // 4))
                if lstm:
                    dve.need(prev("sig ifg"), prev("sig o"))
                    add_halves(preL[:, 0:6, :], vIFG, "ifg", key)
                    add_halves(preL[:, 6:8, :], vO, "o", key)
                if rnn:
                    dve.need(prev("hR"))
                    add_halves(preR[:, :, :], vR, "R", key)
                if lstm:
                    act.need(prev("hL hi"), ("ifg pre", *key))
                    act.done(act.eng.activation(sg[:, 0:6, :], preL[:, 0:6, :], ACT.Sigmoid, scale=descale[:, 1:2]), ("sig ifg", *key))
                    act.need(("o pre", *key))
                    act.done(act.eng.activation(sg[:, 6:8, :], preL[:, 6:8, :], ACT.Sigmoid, scale=descale[:, 1:2]), ("sig o", *key))
                if rnn:
                    act.need(("R pre", *key))
                    if s % 4 == 0:
                        act.need(*has(("x", "hR", 1 - par, s // 4, 1)))
                    act.done(act.eng.activation(hR[:, :, s, :], preR[:, :, :], ACT.Tanh, scale=descale[:, 0:1]), ("hR", *key))
                if lstm:
                    dve.need(("sig ifg", *key))
                    dve.done(dve.eng.scalar_tensor_tensor(u[:, :, :], sg[:, 4:6, :], -0.5, sg[:, 0:2, :], ALU.add, ALU.mult), ("u", *key))
                    dve.done(dve.eng.tensor_tensor(w[:, :, :], sg[:, 2:4, :], cell[:, :, :], ALU.mult), ("w", *key))
                    dve.need(("w", *key))
                    dve.done(dve.eng.scalar_tensor_tensor(cell[:, :, :], u[:, :, :], 2.0, w[:, :, :], ALU.mult, ALU.add), ("c", *key))
                    act.need(("c", *key))
                    act.done(act.eng.activation(tc[:, :, :], cell[:, :, :], ACT.Tanh), ("tanh c", *key))
                    dve.need(("tanh c", *key), ("sig o", *key))
                    if s % 4 == 0:
                        dve.need(*has(("x", "hL", 1 - par, s // 4, 1)))
                    dve.done(dve.eng.tensor_tensor(hL[:, :, s, :], sg[:, 6:8, :], tc[:, :, :], ALU.mult), ("hL", *key))
                    dve.done(dve.eng.tensor_tensor(hpL[:, :, 0, :], sg[:, 6:8, :], tc[:, :, :], ALU.mult), ("hL hi", *key))
                if rnn:
                    dve.need(("hR", *key), ("R", *key))
                    dve.done(dve.eng.tensor_copy(hpR[:, :, 0, :], hR[:, :, s, :]), ("hR hi", *key))
                if lstm:
                    dve.need(("hL hi", *key))
                    dve.done(dve.eng.tensor_tensor(hpL[:, :, 1, :], hL[:, :, s, :], hpL[:, :, 0, :], ALU.subtract), ("hL parts", *key))
                if rnn:
                    dve.need(("hR hi", *key))
                    dve.done(dve.eng.tensor_tensor(hpR[:, :, 1, :], hR[:, :, s, :], hpR[:, :, 0, :], ALU.subtract), ("hR parts", *key))
                if s % 4 == 3:
                    for on, h, t0, name in ((rnn, hR, i * CH, "hR"), (lstm, hL, (i - 2) * CH, "hL")):
                        if on:
                            pool.need((name, *key))
                            for k in range(KC):
                                xs = steps(k, t0 + (s - 3), 4)
                                pool.done(pool.eng.tensor_tensor(xs, xs, h[:, k, s - 3:s + 1, :], ALU.add), ("x", name, par, s // 4, k))
                if xw:
                    for n, at in ((0, 7), (1, 13)):
                        part = lambda q: xw1p[:, 1 - par, q, 4 * n:4 * n + 4, :, :].rearrange("p g t b -> p (g t b)")
                        if s == at:
                            act.need(("xw1", par, n))
                            act.need(*has(("inject ifg", 1 - par, CH - 1), ("inject o", 1 - par, CH - 1)))
                            act.done(act.eng.copy(part(0), psX[n][:, :]), ("part", par, n, 0))
                            dve.need(("part", par, n, 0))
                            dve.done(dve.eng.tensor_tensor(rest[:, n, :], psX[n][:, :], part(0), ALU.subtract), ("rest", par, n))
                        if s == at + 1:
                            act.need(("rest", par, n))
                            act.done(act.eng.copy(part(1), rest[:, n, :]), ("part", par, n, 1))
                            dve.need(("part", par, n, 1))
                            dve.done(dve.eng.tensor_tensor(part(2), rest[:, n, :], part(1), ALU.subtract), ("part", par, n, 2))
                    if s == CH - 1:
                        pe.need(("part", par, 1, 2))

        def pair(i, rnn, lstm, xw):
            for par in range(2):
                chunk(i + par, par, rnn, lstm, xw[par])
                core.next_epoch()

        pair(0, True, False, (False, True))
        core.barrier()
        pair(2, True, True, (True, True))
        with nc.Fori(2, NCH // 2) as two:
            pair(two * 2, True, True, (True, True))
        pair(NCH, False, True, (True, False))
        prefetch.arrived()
        core.barrier()
        core.dma(sp, "x2", x2_dram, XT[:, :, :, :], "x2 out")



class Prefetch:

    def __init__(self, core, name):
        self.lane, self.sem, self.pairs = core.sp, core.sem(name), []

    def add(self, dst, src):
        self.pairs.append((dst, src))

    def start(self):
        for dst, src in self.pairs:
            self.lane.eng.dma_start(dst, src).then_inc(self.sem, 16)

    def arrived(self):
        self.lane.eng.wait_ge(self.sem, 16 * len(self.pairs))


def shared_weights(nc, ctx, A, prefetch):
    sb = lambda n, s, d=fp32: ctx.enter_context(nc.sbuf_tensor(n, s, d))
    W = {}
    for name, shape in (("wqkv", [P, KC, 3 * D]), ("wo", [P, KC, D]), ("wf1", [P, KC, FF]), ("wf2", [P, FC, D]),
                        ("sw1", [P, KC, FF]), ("sw2", [P, FC, D]), ("gate_w", [P, 3 * KC, E]),
                        ("bf1", [P, FC]), ("sb1", [P, FC]), ("eb1", [P, E, FC]), ("segs", [P, 3, NQ]), ("I", [P, P])):
        W[name] = sb("W_" + name, shape)
        prefetch.add(W[name][tuple([slice(None)] * len(shape))], A[name])
    for name, width in (("bqkv", 3 * D), ("bo", D), ("bf2", D), ("sb2", D)):
        W[name] = sb("W_" + name, [P, width])
        prefetch.add(W[name][:, :], A[name].partition_broadcast(P))
    return W


def conditioning_weights(nc, ctx, A, prefetch):
    sb = lambda n, s, d=fp32: ctx.enter_context(nc.sbuf_tensor(n, s, d))
    C = {"wada": sb("wada", [P, KC, 6 * D]), "cond": sb("cond2", [P, KC, NB]), "timew": sb("timew", [P, KC, 2 * E]),
         "bada": sb("bada", [NB, 6 * D]), "silu": sb("silu", [P, KC, NB]), "timeb": sb("timeb", [1, 2 * E])}
    for dst, src in ((C["wada"][:, :, :], A["w_ada"]), (C["cond"][:, :, :], A["condT"]), (C["timew"][:, :, :], A["time_w"]),
                     (C["bada"][:, :], A["b_ada"].partition_broadcast(NB)), (C["timeb"][:, :], A["time_b"])):
        prefetch.add(dst, src)
    return C


def conditioning(nc, core, C, ada_dram, modrow):
    pe, act, dve, pool, sp = core.pe, core.act, core.dve, core.pool, core.sp
    with ExitStack() as mem:
        sb = lambda n, s, d=fp32: mem.enter_context(nc.sbuf_tensor(n, s, d))
        wada, cond, timew, bada, timeb = (C[n] for n in ("wada", "cond", "timew", "bada", "timeb"))
        ada = bada
        silu = C["silu"]
        ps = [mem.enter_context(nc.psum_tensor(f"psA{i}", [P, 512], fp32)) for i in range(4)]
        for j in range(3):
            for k in range(KC):
                last = pe.eng.matmul(ps[j][0:NB, :], cond[:, k, :], wada[:, k, j * 512:(j + 1) * 512], start=k == 0, stop=k == KC - 1)
            pe.done(last, ("ada", j))
            run(dve, ("ada b", j), [("ada", j)], lambda e: e.tensor_tensor(
                ada[:, j * 512:(j + 1) * 512], ps[j][0:NB, :], bada[:, j * 512:(j + 1) * 512], ALU.add))
        for j in (1, 4):
            run(dve, ("ada 1", j), [("ada b", 2)], lambda e: e.tensor_scalar(ada[:, j * D:(j + 1) * D], ada[:, j * D:(j + 1) * D], 1.0, None, ALU.add))
        sp.need(("ada 1", 4))
        core.dma(sp, "c", ada_dram, ada[:, :], "ada out")
        run(act, "sigmoid", [], lambda e: e.activation(silu[:, :, :], cond[:, :, :], ACT.Sigmoid))
        run(dve, "silu", ["sigmoid"], lambda e: e.tensor_tensor(silu[:, :, :], silu[:, :, :], cond[:, :, :], ALU.mult))
        pe.need("silu")
        for b in range(NB):
            for k in range(KC):
                last = pe.eng.matmul(ps[3][0:1, b * 2 * E:(b + 1) * 2 * E], silu[:, k, b:b + 1], timew[:, k, :], start=k == 0, stop=k == KC - 1)
        pe.done(last, "mod")
        run(dve, "mod b", ["mod"], lambda e: e.tensor_tensor(
            modrow[:, :, :], ps[3][0:1, 0:NB * 2 * E].rearrange("p (b e) -> p b e", b=NB),
            timeb[:, :].unsqueeze(1).to_broadcast([1, NB, 2 * E]), ALU.add))
        run(dve, "mod 1", ["mod b"], lambda e: e.tensor_scalar(modrow[:, :, 0:E], modrow[:, :, 0:E], 1.0, None, ALU.add))
        core.barrier()


def transformer_and_experts(nc, core, A, W, x2_dram, ada_dram, modrow, out):
    pe, act, dve, pool, sp = core.pe, core.act, core.dve, core.pool, core.sp
    with ExitStack() as mem:
        sb = lambda n, s, d=fp32: mem.enter_context(nc.sbuf_tensor(n, s, d))
        PS = [mem.enter_context(nc.psum_tensor(f"bank{i}", [P, 2, 512], fp32)) for i in range(4)]
        bank = lambda i: PS[i // 2][:, i % 2, :]
        ada = sb("adab", [P, 6, D])
        ew1 = [sb(f"ew1_{i}", [P, KC, FF]) for i in range(TOPK)]
        ew2 = [sb(f"ew2_{i}", [P, FC, D]) for i in range(TOPK)]
        x3 = sb("x3", [P, NQ, D])
        x3T = sb("x3T", [P, KC, T])
        exp_scratch = sb("exp_scratch", [P, 1])
        hidden = sb("hidden", [P, 3, T])
        weighted = sb("weighted", [P, NQ, D])
        eb2 = [sb(f"eb2_{i}", [P, D]) for i in range(TOPK)]
        eb1 = sb("eb1s", [P, TOPK, FC])
        xT = sb("xT", [P, KC, T])
        x = sb("x", [P, NQ, D])
        x1 = sb("x1", [P, NQ, D])
        z = sb("z", [P, NQ, D])
        w = sb("w_", [P, NQ, D])
        zT = sb("zT", [P, KC, T])
        big = sb("big", [P, 2 * 2048])
        qkv = big[:, 0:NQ * 3 * D].rearrange("p (q a h d) -> p q a h d", q=NQ, a=3, h=H)
        spl = sb("spl", [P, 2, NQ, H, 4, HD], fp16)
        splT = sb("splT", [P, 2, H // 2, T], fp16)
        vt = sb("vt", [P, NQ, H, 2 * HD])
        pexp = sb("pexp", [P, 2, 4, 512])
        uT = pexp[:, :, :, :].rearrange("p a b c -> p (a b) c")
        oT = spl[:, 0].rearrange("p q h s d -> p (q h s d)").bitcast(fp32).rearrange("p (g t) -> p g t", g=H // 4)
        O = spl[:, 1].rearrange("p q h s d -> p (q h s d)").bitcast(fp32).rearrange("p (q h d) -> p q h d", q=NQ, h=H)
        xin = big[:, 0:KC * T].rearrange("p (k t) -> p k t", k=KC)
        pflat = pexp[:, :, :, :].rearrange("p a b c -> p (a b c)")
        st6 = sb("st6", [P, NQ, 6])
        mv = sb("mv", [P, NQ, 2])
        acc = sb("acc", [P, 8, NQ])
        S = sb("S", [P, 24, NQ])
        hs = sb("hs", [P, 4, NQ, 3 * H])
        gin = sb("gin", [P, 3, KC])
        gi = sb("gi", [P, 3, KC])
        gr = sb("gr", [1, 64])
        gidx = sb("gidx", [1, 8], u32)
        g6 = sb("g6", [1, 3 * TOPK])
        b6 = sb("b6", [P, 3 * TOPK])
        wm = sb("wm", [P, TOPK, NQ])
        ones = sb("ones_", [P, P])
        half = sb("half", [P, NQ * 3])
        mhalf = sb("mhalf", [P, NQ])
        I = W["I"]
        f3 = lambda t: t.rearrange("p a b -> p (a b)")

        run(pool, "ones", [], lambda e: e.memset(ones[:, :], 1.0))
        run(pool, "half", [], lambda e: e.memset(half[:, :], 0.5))
        run(pool, "mhalf", [], lambda e: e.memset(mhalf[:, :], -0.5))
        run(pool, "vt 0", [], lambda e: e.memset(vt[:, :, :, :], 0.0))
        run(pool, "vt 1", ["vt 0"], lambda e: e.memset(vt[:, :, :, HD:HD + 1], 1.0))
        core.barrier()

        known = lambda *events: [e for e in events if e in core.events]

        def norm_clip(tag, out_, ss, needs, halves=None):
            run(pool, tag + " sqrt", needs, lambda e: e.tensor_tensor(out_, ss, half[:, 0:NQ] if halves is None else halves, ALU.pow))
            run(dve, tag, [tag + " sqrt"], lambda e: e.tensor_scalar(out_, out_, EPS, None, ALU.max))

        def clipped_ratio(tag, out_, n, tmp, needs):
            run(dve, tag + " r", needs, lambda e: e.reciprocal(tmp, n))
            run(dve, tag, [tag + " r"], lambda e: e.scalar_tensor_tensor(out_, n, ATMAX, tmp, ALU.min, ALU.mult))

        def to_feature_major(tag, src, dst, banks, needs):
            pe.need(*needs)
            for k in range(KC):
                for q in range(NQ):
                    last = pe.eng.transpose(bank(banks[k])[:, q * P:(q + 1) * P], src[:, q, k * P:(k + 1) * P], I[:, :])
                pe.done(last, (tag, "T", k))
            run(act, (tag, 0), [(tag, "T", 0)], lambda e: e.copy(dst[:, 0, :], bank(banks[0])), 0)
            run(dve, (tag, 1), [(tag, "T", 1)], lambda e: e.tensor_copy(dst[:, 1, :], bank(banks[1])), 0.9)

        def modulated_norm(tag, xa, j, needs):
            for q in range(NQ):
                run(dve, (tag, "st", q), needs, lambda e: e.bn_stats(st6[:, q, :], xa[:, q, :]), 0.33)
            for q in range(NQ):
                run(dve, (tag, "mv", q), [(tag, "st", q)], lambda e: e.bn_aggr(mv[:, q, :], st6[:, q, :]), 0.08)
            mu, var = mv[:, :, 0], mv[:, :, 1]
            X2, n, m, t0, t1, al = (S[:, i, :] for i in (0, 2, 3, 4, 5, 6))
            run(dve, tag + "1", [(tag, "mv", NQ - 1)], lambda e: e.tensor_tensor(t0, mu, mu, ALU.mult))
            run(dve, tag + "2", [tag + "1"], lambda e: e.tensor_tensor(t0, t0, var, ALU.add))
            run(dve, tag + " X2", [tag + "2"], lambda e: e.tensor_scalar(X2, t0, float(D), None, ALU.mult))
            norm_clip(tag + " n", n, X2, [tag + " X2"])
            run(dve, tag + "3", [tag + " n"], lambda e: e.tensor_scalar(m, n, MAXT, None, ALU.min))
            run(dve, tag + "4", [tag + "3"], lambda e: e.tensor_scalar(t0, m, -1.0, 1.0, ALU.mult, ALU.add))
            run(dve, tag + "5", [tag + "4"], lambda e: e.reciprocal(t1, t0))
            run(dve, tag + "6", [tag + "5"], lambda e: e.scalar_tensor_tensor(t0, m, 1.0, t1, ALU.add, ALU.mult))
            run(act, tag + " ln", [tag + "6"], lambda e: e.activation(t1, t0, ACT.Ln), 1.5)
            run(dve, tag + "7", [tag + " ln"], lambda e: e.reciprocal(t0, n))
            run(dve, tag + " al", [tag + "7"], lambda e: e.scalar_tensor_tensor(al, t1, 0.5, t0, ALU.mult, ALU.mult))
            run(dve, tag + "8", [tag + " al"], lambda e: e.tensor_tensor(t0, al, al, ALU.mult))
            run(dve, tag + "9", [tag + "8"], lambda e: e.tensor_tensor(t0, t0, var, ALU.mult))
            run(dve, tag + "10", [tag + "9"], lambda e: e.tensor_scalar(t0, t0, 1e-6, None, ALU.add))
            run(pool, tag + "11", [tag + "10"], lambda e: e.tensor_tensor(t1, t0, mhalf[:, :], ALU.pow))
            run(dve, tag + " r", [tag + "11"], lambda e: e.tensor_tensor(t1, t1, al, ALU.mult))
            for q in range(NQ):
                run(dve, (tag, "xn", q), [tag + " r"], lambda e: e.tensor_scalar(
                    z[:, q, :], xa[:, q, :], mv[:, q, 0:1], S[:, 5, q:q + 1], ALU.subtract, ALU.mult), 0.33)
            bc = lambda row: ada[:, row, :].unsqueeze(1).to_broadcast([P, NQ, D])
            run(dve, tag + " sc", [(tag, "xn", NQ - 1), "ada"], lambda e: e.tensor_tensor(z[:, :, :], z[:, :, :], bc(j + 1), ALU.mult), 1.2)
            run(dve, tag + " z", [tag + " sc"], lambda e: e.tensor_tensor(z[:, :, :], z[:, :, :], bc(j), ALU.add), 1.2)
            for q in range(NQ):
                run(act, (tag, "zz", q), [tag + " z"], lambda e: e.activation(big[:, q * D:(q + 1) * D], z[:, q, :], ACT.Square, accum_out=acc[:, 0, q:q + 1]), 0.4)
            norm_clip(tag + " zn", n, acc[:, 0, :], [(tag, "zz", NQ - 1)])
            clipped_ratio(tag + " s", S[:, 1, :], n, t0, [tag + " zn"])

        def mobius_update(tag, banks, bias, j, xa, xout, more, needs):
            a = z
            for q in range(NQ):
                run(dve, (tag, "a", q), needs, lambda e: e.scalar_tensor_tensor(
                    a[:, q, :], bank(banks[q // 2])[:, (q % 2) * D:(q % 2 + 1) * D], S[:, 7, q:q + 1], bias[:, :], ALU.mult, ALU.add), 0.4)
                run(act, (tag, "aa", q), [(tag, "a", q)], lambda e: e.activation(big[:, q * D:(q + 1) * D], a[:, q, :], ACT.Square, accum_out=acc[:, 1, q:q + 1]), 0)
            run(dve, tag + " w", [(tag, "a", NQ - 1)], lambda e: e.tensor_tensor(
                w[:, :, :], a[:, :, :], ada[:, j, :].unsqueeze(1).to_broadcast([P, NQ, D]), ALU.mult), 1.15)
            for q in range(NQ):
                run(act, (tag, "ww", q), [tag + " w"], lambda e: e.activation(big[:, (4 + q) * D:(5 + q) * D], w[:, q, :], ACT.Square, accum_out=acc[:, 2, q:q + 1]), 0)
                run(dve, (tag, "xw", q), [tag + " w", ((tag, "xw", q - 1) if q else None)], lambda e: e.tensor_tensor_reduce(
                    out=big[:, 8 * D:9 * D], in0=xa[:, q, :], in1=w[:, q, :], scale=1.0, scalar=0.0, op0=ALU.mult, op1=ALU.add,
                    accum_out=acc[:, 3, q:q + 1]), 0.43)
            X2, na, ca, t0, n2, th, be, XY, Y2, den, pp, rr, t1 = (S[:, i, :] for i in (0, 8, 9, 10, 11, 12, 13, 14, 15, 16, 17, 18, 19))
            norms = S[:, 22:24, :]
            run(pool, tag + " norms", [(tag, "aa", NQ - 1), (tag, "ww", NQ - 1)], lambda e: e.tensor_tensor(
                norms, acc[:, 1:3, :], half[:, 0:2 * NQ].rearrange("p (a q) -> p a q", a=2), ALU.pow))
            run(dve, tag + " na", [tag + " norms"], lambda e: e.tensor_scalar(na, norms[:, 0, :], EPS, None, ALU.max))
            clipped_ratio(tag + " ca", ca, na, t0, [tag + " na"])
            run(dve, tag + " wc", [tag + " ca"], lambda e: e.tensor_tensor(n2, norms[:, 1, :], ca, ALU.mult))
            run(dve, tag + " n2", [tag + " wc"], lambda e: e.tensor_scalar(n2, n2, EPS, None, ALU.max))
            run(act, tag + " th", [tag + " n2"], lambda e: e.activation(th, n2, ACT.Tanh))
            run(dve, tag + " rn", [tag + " n2"], lambda e: e.reciprocal(t0, n2))
            run(dve, tag + " cr", [tag + " rn"], lambda e: e.tensor_tensor(t0, t0, ca, ALU.mult))
            run(dve, tag + " be", [tag + " cr", tag + " th"], lambda e: e.tensor_tensor(be, t0, th, ALU.mult))
            run(dve, tag + " XY", [tag + " be", (tag, "xw", NQ - 1)], lambda e: e.tensor_tensor(XY, be, acc[:, 3, :], ALU.mult))
            run(dve, tag + " bb", [tag + " be"], lambda e: e.tensor_tensor(t0, be, be, ALU.mult))
            run(dve, tag + " Y2", [tag + " bb"], lambda e: e.tensor_tensor(Y2, t0, acc[:, 2, :], ALU.mult))
            run(dve, tag + " 2XY", [tag + " XY"], lambda e: e.tensor_scalar(t1, XY, 2.0, 1.0, ALU.mult, ALU.add))
            run(dve, tag + " X2Y2", [tag + " Y2"], lambda e: e.tensor_tensor(den, X2, Y2, ALU.mult))
            run(dve, tag + " den", [tag + " X2Y2", tag + " 2XY"], lambda e: e.tensor_tensor(den, den, t1, ALU.add))
            run(dve, tag + " denc", [tag + " den"], lambda e: e.tensor_scalar(den, den, EPS, None, ALU.max))
            run(dve, tag + " rden", [tag + " denc"], lambda e: e.reciprocal(t0, den))
            run(dve, tag + " num", [tag + " Y2", tag + " 2XY"], lambda e: e.tensor_tensor(pp, t1, Y2, ALU.add))
            run(dve, tag + " p", [tag + " num", tag + " rden"], lambda e: e.tensor_tensor(pp, pp, t0, ALU.mult))
            run(dve, tag + " 1-X2", [tag + " X2Y2"], lambda e: e.tensor_scalar(rr, X2, -1.0, 1.0, ALU.mult, ALU.add))
            run(dve, tag + " r1", [tag + " 1-X2"], lambda e: e.tensor_tensor(rr, rr, be, ALU.mult))
            run(dve, tag + " r", [tag + " r1", tag + " rden"], lambda e: e.tensor_tensor(rr, rr, t0, ALU.mult))
            for q in range(NQ):
                run(act, (tag, "xp", q), [tag + " p"], lambda e: e.activation(z[:, q, :], xa[:, q, :], ACT.Identity, scale=S[:, 17, q:q + 1]), 0.1)
            for q in range(NQ):
                run(dve, (tag, "x", q), [(tag, "xp", q), tag + " r"], lambda e: e.scalar_tensor_tensor(
                    xout[:, q, :], w[:, q, :], S[:, 18, q:q + 1], z[:, q, :], ALU.mult, ALU.add), 0.4)
            if more is not None:
                run(dve, tag + " out", [(tag, "x", NQ - 1)], lambda e: e.tensor_tensor(xout[:, :, :], xout[:, :, :], more[:, :, :], ALU.add), 1.15)
            else:
                core.events[tag + " out"] = core.events[(tag, "x", NQ - 1)]

        def feed_forward(hbanks, ybanks, needs):
            pe.need(*needs)

            def second(m):
                pe.need(("u", m))
                for q in range(NQ):
                    last = pe.eng.matmul(bank(ybanks[q // 2])[:, (q % 2) * D:(q % 2 + 1) * D], uT[:, m, q * P:(q + 1) * P], W["wf2"][:, m, :],
                                         start=(m == 0 and q % 2 == 0), stop=m == FC - 1, skip_group_check=True)
                pe.done(last, ("ff", m))

            for m in range(FC):
                hb = hbanks[m % len(hbanks)]
                if m >= len(hbanks):
                    pe.need(("u", m - len(hbanks)))
                for k in range(KC):
                    last = pe.eng.matmul(bank(hb), W["wf1"][:, k, m * P:(m + 1) * P], zT[:, k, :], start=k == 0, stop=k == KC - 1)
                pe.done(last, ("u ps", m))
                run(act, ("u", m), [("u ps", m)], lambda e: e.activation(uT[:, m, :], bank(hb), ACT.Identity, bias=W["bf1"][:, m:m + 1]))
                run(act, ("u sq", m), [("u", m), ("m1", "xw", NQ - 1)], lambda e: e.activation(big[:, m * T:(m + 1) * T], uT[:, m, :], ACT.Square))
                if m:
                    run(dve, ("u ss", m), [("u sq", m), ("u ss", m - 1) if m > 1 else None], lambda e: e.tensor_tensor(
                        xT[:, 0, :], big[:, 0:T] if m == 1 else xT[:, 0, :], big[:, m * T:(m + 1) * T], ALU.add))
                    second(m - 1)
            second(FC - 1)

        def gate(b):
            for n, (lo, hi) in enumerate(SEGS):
                run(dve, ("seg", n), [], lambda e: e.tensor_reduce(gin[:, n, :], x3T[:, :, lo:hi], AX.X, ALU.add), 0.43)
                yield
            nhp = T - SEG
            run(dve, "g hp", [("seg", 2)], lambda e: e.tensor_tensor(gi[:, 1, :], gin[:, 0, :], gin[:, 2, :], ALU.add))
            yield
            run(dve, "g wp", [("seg", 2)], lambda e: e.tensor_tensor(gi[:, 2, :], gin[:, 1, :], gin[:, 2, :], ALU.add))
            yield
            run(dve, "g all", ["g hp"], lambda e: e.tensor_tensor(gi[:, 0, :], gi[:, 1, :], gin[:, 1, :], ALU.add))
            yield
            run(dve, "g m0", ["g all"], lambda e: e.tensor_scalar(gi[:, 0, :], gi[:, 0, :], 1.0 / T, None, ALU.mult))
            yield
            run(dve, "g m1", ["g all", "g wp"], lambda e: e.tensor_scalar(gi[:, 1:3, :], gi[:, 1:3, :], 1.0 / nhp, None, ALU.mult))
            yield
            pe.need("g m1")
            for n in range(3):
                for k in range(KC):
                    last = pe.eng.matmul(bank(2)[0:1, 0:E], gi[:, n, k:k + 1], W["gate_w"][:, n * KC + k, :], start=(n, k) == (0, 0), stop=(n, k) == (2, KC - 1))
            pe.done(last, "logits")
            G = lambda i, m=8: gr[:, 8 * i:8 * i + m]
            run(dve, "l b", ["logits"], lambda e: e.tensor_tensor(G(0, E), bank(2)[0:1, 0:E], gateb[:, :], ALU.add))
            yield
            run(dve, "l s", ["l b"], lambda e: e.tensor_tensor(G(0, E), G(0, E), modrow[:, bass.ds(b, 1), 0:E], ALU.mult))
            yield
            run(dve, "l t", ["l s"], lambda e: e.tensor_tensor(G(0, E), G(0, E), modrow[:, bass.ds(b, 1), E:2 * E], ALU.add))
            yield
            run(dve, "l max", ["l t"], lambda e: e.tensor_reduce(G(1, 1), G(0, E), AX.X, ALU.max, negate=True))
            yield
            run(dve, "pad", [], lambda e: e.memset(G(2), -1.0))
            yield
            run(act, "l exp", ["l max", "pad"], lambda e: e.activation(G(2, E), G(0, E), ACT.Exp, bias=G(1, 1)))
            yield
            run(dve, "l sum", ["l exp"], lambda e: e.tensor_reduce(G(3, 1), G(2, E), AX.X, ALU.add))
            yield
            run(dve, "l rs", ["l sum"], lambda e: e.reciprocal(G(3, 1), G(3, 1)))
            yield
            run(dve, "l p", ["l rs"], lambda e: e.tensor_scalar(G(2, E), G(2, E), G(3, 1), None, ALU.mult))
            yield
            run(dve, "top", ["l p"], lambda e: e.max(G(4), G(2)))
            yield
            run(dve, "idx", ["top"], lambda e: e.max_index(gidx[:, :], G(4), G(2)))
            yield
            sp.need("idx")
            index = [sp.eng.value_load(gidx[:, s:s + 1], min_val=0, max_val=E - 1) for s in range(TOPK)]
            for s, ei in enumerate(index):
                core.dma(sp, f"b{s}", eb2[s][:, :], A["eb2"][bass.ds(ei, 1), :].rearrange("o n -> (o n)").partition_broadcast(P), ("eb", s))
                core.dma(sp, f"b{s}", eb1[:, s, :], A["eb1d"][bass.ds(ei, 1)].rearrange("o p n -> p (o n)"), ("eb", s))
            for s, ei in enumerate(index):
                core.dma(sp, f"e{s}", ew1[s][:, :, :], A["ew1"][bass.ds(ei, 1)].rearrange("o p k n -> p (o k) n"), ("ew1", s))
                core.dma(sp, f"f{s}", ew2[s][:, :, :], A["ew2"][bass.ds(ei, 1)].rearrange("o p k n -> p (o k) n"), ("ew2", s))
            run(dve, "w sum", ["top"], lambda e: e.tensor_reduce(G(5, 1), G(4, TOPK), AX.X, ALU.add))
            yield
            run(dve, "w eps", ["w sum"], lambda e: e.tensor_scalar(G(5, 1), G(5, 1), 1e-8, None, ALU.add))
            yield
            run(dve, "w r", ["w eps"], lambda e: e.reciprocal(G(5, 1), G(5, 1)))
            yield
            run(dve, "w n", ["w r"], lambda e: e.tensor_scalar(G(4, TOPK), G(4, TOPK), G(5, 1), None, ALU.mult))
            yield
            run(dve, "idx f", ["idx"], lambda e: e.tensor_copy(G(6), gidx[:, :]))
            yield
            for n, masked in ((0, 2.0), (1, 1.0)):
                run(dve, ("g6", n), ["idx f", "w n"], lambda e: e.scalar_tensor_tensor(
                    g6[:, n * TOPK:(n + 1) * TOPK], G(6, TOPK), masked, G(4, TOPK), ALU.not_equal, ALU.mult))
                yield
            run(dve, "g6", ["w n"], lambda e: e.tensor_copy(g6[:, 2 * TOPK:3 * TOPK], G(4, TOPK)))
            yield
            run(pe, "b6 ps", ["g6", "l b"], lambda e: e.matmul(bank(2)[:, 0:3 * TOPK], ones[0:1, :], g6[:, :], start=True, stop=True))
            yield
            run(dve, "b6", ["b6 ps"], lambda e: e.tensor_copy(b6[:, :], bank(2)[:, 0:3 * TOPK]))
            yield
            for s in range(TOPK):
                for n in range(3):
                    seg, fac = W["segs"][:, n, :], b6[:, n * TOPK + s:n * TOPK + s + 1]
                    if n == 0:
                        run(dve, ("wm", s, n), ["b6"], lambda e: e.tensor_scalar(wm[:, s, :], seg, fac, None, ALU.mult))
                        yield
                    else:
                        run(dve, ("wm", s, n), [("wm", s, n - 1)], lambda e: e.scalar_tensor_tensor(wm[:, s, :], seg, fac, wm[:, s, :], ALU.mult, ALU.add))
                        yield

            for s in range(TOPK):
                for q in range(NQ):
                    run(dve, ("x3 bias", s, q), [("eb", s), ("wm", s, 2), ("x3 bias", s - 1, q) if s else "x3 moved"], lambda e: e.scalar_tensor_tensor(
                        x3[:, q, :], eb2[s][:, :], wm[:, s, q:q + 1], x3[:, q, :], ALU.mult, ALU.add))
                    yield

        def experts(b):
            run(dve, "x3 moved", [], lambda e: e.tensor_tensor(x3[:, :, :], x1[:, :, :], W["sb2"][:, :].unsqueeze(1).to_broadcast([P, NQ, D]), ALU.add))
            yield None
            chunks = [(n, m) for n in range(1 + TOPK) for m in range(FC)]
            half_way = FC + 3
            weights = [(W["sw1"], W["sw2"], W["sb1"], W["sb2"])] + [(ew1[s], ew2[s], eb1[:, s, :], eb2[s]) for s in range(TOPK)]
            groups = 0
            for lo, hi in ((0, half_way), (half_way, len(chunks))):
                for i in range(lo, hi + 2):
                    if i == hi == half_way:
                        yield "last hidden chunk"
                    if i < hi:
                        n, m = chunks[i]
                        if n:
                            core.background.finish_side()
                            pe.need(("ew1", n - 1))
                        if i >= lo + 2:
                            pe.need(("eh", i - 2))
                        for k in range(KC):
                            last = pe.eng.matmul(bank(4 + i % 2), weights[n][0][:, k, m * P:(m + 1) * P], x3T[:, k, :], start=k == 0, stop=k == KC - 1)
                            if k < KC - 1:
                                yield None
                        pe.done(last, ("eup", i))
                        yield None
                    if i < lo + 2:
                        later = None
                    else:
                        later = i - 2
                        n2, m2 = chunks[later]
                        first, end = later == lo or m2 == 0, later == hi - 1 or m2 == FC - 1
                        pe.need(("eh", later), ("ew2", n2 - 1) if n2 else None, *([("y out", groups - 1, q) for q in range(NQ)] if first and groups else []))
                    for q in range(NQ):
                        if q == NQ // 2:
                            if later is not None:
                                yield None
                            if i < hi:
                                run(act, ("eh", i), [("eup", i), ("esecond", i - 3) if i >= 3 else None, ("eb", n - 1) if n else None],
                                    lambda e: e.activation(hidden[:, i % 3, :], bank(4 + i % 2), ACT.Gelu_apprx_tanh, bias=weights[n][2][:, m:m + 1]))
                        if later is not None:
                            last = pe.eng.matmul(bank(6 + q // 2)[:, (q % 2) * D:(q % 2 + 1) * D], hidden[:, later % 3, q * P:(q + 1) * P], weights[n2][1][:, m2, :],
                                                 start=first and q % 2 == 0, stop=end, skip_group_check=True)
                    if later is None:
                        continue
                    pe.done(last, ("esecond", later))
                    yield None
                    if end:
                        core.background.finish_side()
                        for q in range(NQ):
                            scale = wm[:, n2 - 1, q:q + 1] if n2 else 1.0
                            y, needs = bank(6 + q // 2)[:, (q % 2) * D:(q % 2 + 1) * D], [("esecond", later), *known(("wm", 1, 2)), ("y", groups - 1, q) if groups else None]
                            if hi == half_way and later == hi - 1:
                                run(dve, ("y out", groups, q), needs, lambda e: e.tensor_scalar(weighted[:, q, :], y, scale, None, ALU.mult))
                            else:
                                run(act, ("y out", groups, q), needs, lambda e: e.activation(weighted[:, q, :], y, ACT.Identity, scale=scale))
                        for q in range(NQ):
                            run(pool, ("y", groups, q), [("y out", groups, q), ("x3 bias", TOPK - 1, q)], lambda e: e.tensor_tensor(x3[:, q, :], x3[:, q, :], weighted[:, q, :], ALU.add))
                        groups += 1
                if hi == half_way:
                    core.events["experts' banks free"] = core.events[("y out", groups - 1, NQ - 1)]
                    yield "attention"
                    pe.need(*known(("O", 3), ("oT", 3)))
            sp.need(("y", groups - 1, NQ - 1))
            core.dma(sp, "out", out[bass.ds(b, 1)].rearrange("o (q p) d -> p (o q) d", p=P), x3[:, :, :], "out")

        def front(b, background):
            core.background = background
            core.dma(sp, "ada", ada[:, :, :].rearrange("p j d -> p (j d)"), ada_dram[bass.ds(b, 1), :].rearrange("o n -> (o n)").partition_broadcast(P), "ada")
            core.dma(sp, "x2", xin, x2_dram[:, :, bass.ds(b, 1), :].rearrange("p k o t -> p k (o t)"), "x2 in")
            background.open = True
            background.tick(6.0)
            pe.need("x2 in")
            for q in range(NQ):
                for k in range(KC):
                    last = pe.eng.transpose(bank(q // 2)[:, (q % 2) * D + k * P:(q % 2) * D + (k + 1) * P], xin[:, k, q * P:(q + 1) * P], I[:, :])
                if q % 2:
                    pe.done(last, ("x T", q // 2))
            run(act, "x 0", [("x T", 0)], lambda e: e.copy(f3(x[:, 0:2, :]), bank(0)))
            run(dve, "x 1", [("x T", 1)], lambda e: e.tensor_copy(f3(x[:, 2:4, :]), bank(1)))
            modulated_norm("ln1", x, 0, ["x 0", "x 1"])
            background.finish_side()
            pe.need(*known("b6"))
            to_feature_major("zT", z, zT, (2, 3), ["ln1 z"])

            pe.need(("zT", 0), ("zT", 1))
            for q in range(NQ):
                b0, b1_ = (0, 1) if q % 2 == 0 else (2, 3)
                if q >= 2:
                    pe.need(("qkv b", q - 2))
                for (lo, hi), bk in (((0, 512), b0), ((512, 768), b1_)):
                    for k in range(KC):
                        last = pe.eng.matmul(bank(bk)[:, 0:hi - lo], zT[:, k, q * P:(q + 1) * P], W["wqkv"][:, k, lo:hi], start=k == 0, stop=k == KC - 1)
                pe.done(last, ("qkv", q))
                flat = qkv[:, q].rearrange("p a h d -> p (a h d)")
                for (lo, hi), bk, nm in (((0, 512), b0, "qkv a"), ((512, 768), b1_, "qkv b")):
                    run(dve, (nm, q), [("qkv", q), "ln1 s"], lambda e: e.scalar_tensor_tensor(
                        flat[:, lo:hi], bank(bk)[:, 0:hi - lo], S[:, 1, q:q + 1], W["bqkv"][:, lo:hi], ALU.mult, ALU.add), 0)
                run(act, ("qkv sq", q), [("qkv b", q)], lambda e: e.activation(pflat[:, q * 768:(q + 1) * 768], flat, ACT.Square), 0)
                run(dve, ("qkv ss", q), [("qkv sq", q)], lambda e: e.tensor_reduce(
                    hs[:, 0, q, :], pflat[:, q * 768:(q + 1) * 768].rearrange("p (h d) -> p h d", d=HD), AX.X, ALU.add), 4.0 if q == NQ - 1 else 0)
            hss, hf, ht = hs[:, 0], hs[:, 1], hs[:, 2]
            tot, tn, tr = acc[:, 4:7, :].rearrange("p a q -> p q a"), S[:, 20:23, :].rearrange("p a q -> p q a"), hs[:, 3, :, 0:3]
            run(dve, "tot", [("qkv ss", NQ - 1)], lambda e: e.tensor_reduce(tot, hss.rearrange("p q (a h) -> p q a h", h=H), AX.X, ALU.add))
            norm_clip("tn", tn, tot, ["tot"], half[:, 0:3 * NQ].rearrange("p (q a) -> p q a", a=3))
            run(dve, "tr", ["tn"], lambda e: e.reciprocal(tr, tn))
            run(dve, "tm", ["tr"], lambda e: e.tensor_scalar(tn, tn, ATMAX, TO_HEADS, ALU.min, ALU.mult))
            run(dve, "cs", ["tm"], lambda e: e.tensor_tensor(tn, tn, tr, ALU.mult))
            csb = tn.unsqueeze(3).to_broadcast([P, NQ, 3, H])
            h4 = lambda t: t.rearrange("p q (a h) -> p q a h", h=H)
            run(act, "h sqrt", ["tot"], lambda e: e.activation(f3(ht), f3(hss), ACT.Sqrt), 1.5)
            run(dve, "h n", ["h sqrt", "cs"], lambda e: e.tensor_tensor(h4(ht), h4(ht), csb, ALU.mult))
            run(dve, "h nc", ["h n"], lambda e: e.tensor_scalar(f3(ht), f3(ht), EPS, None, ALU.max))
            run(dve, "h r", ["h nc"], lambda e: e.reciprocal(f3(hf), f3(ht)), 1.3)
            run(dve, "h f", ["h r"], lambda e: e.scalar_tensor_tensor(f3(hf), f3(ht), ATMAX, f3(hf), ALU.min, ALU.mult))
            run(dve, "h F", ["h f"], lambda e: e.tensor_tensor(h4(hf), h4(hf), csb, ALU.mult))
            hf4 = h4(hf)
            for q in range(NQ):
                for a in (0, 1):
                    run(dve, ("qk", q, a), ["h F"], lambda e: e.tensor_tensor(
                        qkv[:, q, a], qkv[:, q, a], hf4[:, q, a, :].unsqueeze(2).to_broadcast([P, H, HD]), ALU.mult), 0.33)
                run(dve, ("v", q), ["h F"], lambda e: e.tensor_tensor(
                    vt[:, q, :, 0:HD], qkv[:, q, 2], hf4[:, q, 2, :].unsqueeze(2).to_broadcast([P, H, HD]), ALU.mult), 0.33)
                for a in (0, 1):
                    src = qkv[:, q, a]
                    dst = spl[:, a, q].rearrange("p h (s t) d -> p h s t d", t=2)
                    hi = [dst[:, :, 0, :, :], dst[:, :, :, 0, :]][a]
                    lo = [dst[:, :, 1, :, :], dst[:, :, :, 1, :]][a]
                    srcb = src.unsqueeze(2).to_broadcast([P, H, 2, HD])
                    run(act, ("hi", q, a), [("qk", q, a)], lambda e: e.copy(hi, srcb), 0)
                    run(dve, ("lo", q, a), [("hi", q, a)], lambda e: e.tensor_tensor(lo, srcb, hi, ALU.subtract), 0.6)
            background.open = False
            background.run_to("last hidden chunk")
            run(act, "exp table", [], lambda e: e.activation(exp_scratch[:, :], mhalf[:, 0:1], ACT.Exp))
            for a in (0, 1):
                if a:
                    background.run(2)
                for hp2 in range(H // 4):
                    bk = hp2
                    v16 = bank(bk).bitcast(fp16)
                    for q in range(NQ):
                        pe.need(("lo", q, a))
                        if q == 0:
                            pe.need(("qkv b", NQ - 1) if a == 0 else ("splT", 0, hp2))
                        for j in range(2):
                            hp = 2 * hp2 + j
                            src = spl[:, a, q, 2 * hp:2 * hp + 2].rearrange("p h s d -> p (h s d)")
                            last = pe.eng.transpose(v16[:, j * 512 + q * P:j * 512 + (q + 1) * P], src, I16_t[:, :])
                    pe.done(last, ("splT ps", a, hp2))
                    lane = act if hp2 in ((0, 2), (0,))[a] else dve
                    run(lane, ("splT", a, hp2), [("splT ps", a, hp2)], lambda e: (e.copy if lane is act else e.tensor_copy)(
                        splT[:, a, 2 * hp2:2 * hp2 + 2, :].rearrange("p j t -> p (j t)"), v16[:, :]))

            background.run_to("attention")

            def scores(g, kc):
                for pr in range(2):
                    if (g, kc) != (0, 0):
                        pe.need(("exp", *prev_unit(g, kc), pr))
                    else:
                        pe.need(*[("splT", a, i) for a in (0, 1) for i in range(H // 4)])
                    for j in range(2):
                        hp = 2 * g + pr
                        rows = slice(64 * j, 64 * j + 64)
                        last = pe.eng.matmul(bank(2 * pr + j), splT[rows, 1, hp, kc * P:(kc + 1) * P], splT[rows, 0, hp, :], start=True, stop=True)
                    pe.done(last, ("scores", g, kc, pr))
                    if unit_no(g, kc) >= 2:
                        act.need(("av", *prev_unit(*prev_unit(g, kc))))
                    run(act, ("exp", g, kc, pr), [("scores", g, kc, pr)], lambda e: e.activation(
                        pexp[:, unit_no(g, kc) % 2, 2 * pr:2 * pr + 2, :], PS[pr][:, :, :], ACT.Exp, scale=1.0 / math.sqrt(HD)))

            def values(g, kc):
                pe.need(("exp", g, kc, 1), ("v", kc))
                if kc == 0 and g >= 2:
                    pe.need(("oT", g - 2))
                for j in range(4):
                    last = pe.eng.matmul(bank(4 + g % 2)[32 * j:32 * j + 32, :], vt[:, kc, 4 * g + j, :], pexp[:, unit_no(g, kc) % 2, j, :],
                                         start=kc == 0, stop=kc == NQ - 1, tile_position=(0, 32 * j))
                pe.done(last, ("av", g, kc))
                if kc == NQ - 1:
                    run(dve, ("oT", g), [("av", g, kc)], lambda e: e.tensor_copy(oT[:, g, :], bank(4 + g % 2)))

            def back(g):
                pe.need(*known("experts' banks free"))
                pe.need(("oT", g))
                if g >= 2:
                    pe.need(("O", g - 2))
                bk = 6 + g % 2
                for q in range(NQ):
                    last = pe.eng.transpose(bank(bk)[:, q * P:(q + 1) * P], oT[:, g, q * P:(q + 1) * P], I[:, :])
                pe.done(last, ("O T", g))
                run(dve, ("O", g), [("O T", g)], lambda e: e.tensor_copy(
                    O[:, :, 4 * g:4 * g + 4, :].rearrange("p q h d -> p q (h d)"), bank(bk).rearrange("p (q n) -> p q n", q=NQ)))

            unit_no = lambda g, kc: g * NQ + kc
            prev_unit = lambda g, kc: divmod(unit_no(g, kc) - 1, NQ)
            units = [(g, kc) for g in range(H // 4) for kc in range(NQ)]
            scores(*units[0])
            for n, u in enumerate(units):
                if n + 1 < len(units):
                    scores(*units[n + 1])
                values(*u)
                if u[1] == 1 and u[0] > 0:
                    back(u[0] - 1)
            back(H // 4 - 1)
            background.go_on(0.85)

            o3 = O[:, :, :, 0:HD]
            oss, ond, oh, of, ot = (hs[:, i, :, 0:H] for i in (0, 1, 2, 3, 3))
            sqv = big[:, 0:NQ * D].rearrange("p (q h d) -> p q h d", q=NQ, h=H)
            run(act, "o sq", [("O", 3)], lambda e: e.activation(sqv, o3, ACT.Square), 1.0)
            run(dve, "o ss", ["o sq"], lambda e: e.tensor_reduce(oss, sqv, AX.X, ALU.add), 1.2)
            run(dve, "o rd", ["o ss"], lambda e: e.reciprocal(ond, O[:, :, :, HD]))
            run(act, "o sqrt", ["o ss"], lambda e: e.activation(oh, oss, ACT.Sqrt), 1.0)
            run(dve, "o nh", ["o sqrt", "o rd"], lambda e: e.tensor_tensor(oh, oh, ond, ALU.mult))
            run(dve, "o nc", ["o nh"], lambda e: e.tensor_scalar(oh, oh, EPS, None, ALU.max))
            run(dve, "o r", ["o nc"], lambda e: e.reciprocal(of, oh))
            run(dve, "o m", ["o r"], lambda e: e.scalar_tensor_tensor(of, oh, ATMAX, of, ALU.min, ALU.mult))
            run(dve, "o f", ["o m"], lambda e: e.scalar_tensor_tensor(of, of, FROM_HEADS, ond, ALU.mult, ALU.mult))
            run(dve, "o t", ["o f"], lambda e: e.tensor_tensor(
                z[:, :, :].rearrange("p q (h d) -> p q h d", h=H), o3, of.unsqueeze(3).to_broadcast([P, NQ, H, HD]), ALU.mult), 1.2)
            run(dve, "o ff", ["o f"], lambda e: e.tensor_tensor(oh, of, of, ALU.mult))
            run(dve, "o ffs", ["o ff"], lambda e: e.tensor_tensor(oh, oh, oss, ALU.mult))
            run(dve, "t ss", ["o ffs"], lambda e: e.tensor_reduce(acc[:, 7, :], oh, AX.X, ALU.add))
            norm_clip("t n", S[:, 8, :], acc[:, 7, :], ["t ss"])
            clipped_ratio("t s", S[:, 7, :], S[:, 8, :], S[:, 9, :], ["t n"])
            to_feature_major("tT", z, zT, (0, 1), ["o t", ("exp", 3, 3, 1)])
            pe.need(("tT", 0), ("tT", 1))
            for q in range(NQ):
                for k in range(KC):
                    last = pe.eng.matmul(bank(2 + q // 2)[:, (q % 2) * D:(q % 2 + 1) * D], zT[:, k, q * P:(q + 1) * P], W["wo"][:, k, :], start=k == 0, stop=k == KC - 1)
            pe.done(last, "wo")
            mobius_update("m1", (2, 3), W["bo"], 2, x, x1, None, ["wo", "t s", ("tT", "T", 1)])

            modulated_norm("ln2", x1, 3, ["m1 out"])
            for q in range(NQ):
                run(dve, ("zs", q), ["ln2 s"], lambda e: e.tensor_scalar(z[:, q, :], z[:, q, :], S[:, 1, q:q + 1], None, ALU.mult), 0.27)
            to_feature_major("zsT", z, zT, (0, 1), [("zs", NQ - 1)])
            background.open = False
            feed_forward((0, 1), (2, 3), [("zsT", 0), ("zsT", 1)])
            background.open = True
            pe.need(("u ss", FC - 1))
            for q in range(NQ):
                last = pe.eng.matmul(bank(0)[:, q:q + 1], xT[:, 0, q * P:(q + 1) * P], ones[:, 0:1], start=q == 0, stop=True, skip_group_check=True)
            pe.done(last, "u tot")
            run(dve, "u out", ["u tot"], lambda e: e.tensor_copy(acc[:, 7, :], bank(0)[:, 0:NQ]))
            norm_clip("u n", S[:, 8, :], acc[:, 7, :], ["u out"])
            clipped_ratio("u s", S[:, 7, :], S[:, 8, :], S[:, 9, :], ["u n"])
            mobius_update("m2", (2, 3), W["bf2"], 5, x1, x1, x, [("ff", FC - 1), "u s", ("zsT", "T", 1)])

            background.open = False
            background.run_to("end")
            to_feature_major("x3T", x1, x3T, (0, 1), ["m2 out", "u out", *known(("eup", 3 * FC - 1))])
            core.barrier()

        I16_t = sb("I16", [P, P], fp16)
        gateb = sb("gateb", [1, E])
        core.dma(sp, "c", gateb[:, :], A["gate_b"], "gateb")
        run(dve, "I16", [], lambda e: e.tensor_copy(I16_t[:, :], I[:, :]))
        core.barrier()
        front(0, Background())
        with nc.Fori(1, NB) as b:
            front(b, Background(experts(b - 1), gate(b - 1)))
        core.background = Background(experts(NB - 1), gate(NB - 1))
        core.background.run_to("end")
        core.barrier()


def program(nc, A, out):
    with ExitStack() as ctx:
        core = Core(nc, ctx)
        modrow = ctx.enter_context(nc.sbuf_tensor("modrow", [1, NB, 2 * E], fp32))
        ada_dram = nc.dram_tensor("ada_scratch", (NB, 6 * D), fp32, kind="Internal").ap()
        x2_dram = nc.dram_tensor("x2_scratch", (P, KC, NB, T), fp32, kind="Internal").ap()
        prefetch = Prefetch(core, "prefetch")
        W = shared_weights(nc, ctx, A, prefetch)
        with ExitStack() as early:
            C = conditioning_weights(nc, early, A, prefetch)
            recurrences(nc, core, ctx, A, x2_dram, prefetch)
            conditioning(nc, core, C, ada_dram, modrow)
        transformer_and_experts(nc, core, A, W, x2_dram, ada_dram, modrow, out)


def kernel(**inputs):
    import numpy as np
    import concourse.bacc as bacc
    from concourse.bass_utils import run_bass_kernel_spmd

    f = {n: np.ascontiguousarray(a) for n, a in inputs.items()}
    L2 = lambda n: f["L2_cond_" + n]
    L3 = lambda n: f["L3_cond_" + n]
    ifgo = lambda a: np.concatenate([a[..., 0:D], a[..., D:2 * D], a[..., 3 * D:], a[..., 2 * D:3 * D]], axis=-1)
    rows = lambda a: a.reshape(-1, P, a.shape[-1]).transpose(1, 0, 2)
    cols = lambda a: a.reshape(-1, P).T
    token = np.arange(T).reshape(NQ, P).T
    arrays = {
        "xT": f["x"].transpose(2, 0, 1).reshape(KC, P, NB, T).transpose(1, 0, 2, 3),
        "condT": rows(f["cond_1024"].T),
        "b0T": cols(f["L0_cond_b"]),
        "b1row": ifgo(f["L1_cond_b"])[None, :],
        "L0_cond_Wx": f["L0_cond_Wx"], "L0_cond_Wh": f["L0_cond_Wh"],
        "L1_cond_Wx": ifgo(f["L1_cond_Wx"]), "L1_cond_Wh": ifgo(f["L1_cond_Wh"]),
        "ident": np.eye(P, dtype=np.float32), "I": np.eye(P, dtype=np.float32),
        "segs": np.stack([(token >= lo) & (token < hi) for lo, hi in SEGS], axis=1).astype(np.float32),
        "wqkv": rows(np.concatenate([L2("w_q"), L2("w_k"), L2("w_v")], axis=1)),
        "bqkv": np.concatenate([L2("b_q"), L2("b_k"), L2("b_v")]),
        "wo": rows(L2("w_o")), "bo": L2("b_o"), "wf1": rows(L2("w_f1")), "bf1": cols(L2("b_f1")),
        "wf2": rows(L2("w_f2")), "bf2": L2("b_f2"), "w_ada": rows(L2("w_ada")), "b_ada": L2("b_ada"),
        "gate_w": rows(L3("gate_w")), "gate_b": L3("gate_b")[None, :], "time_w": rows(L3("time_w")), "time_b": L3("time_b")[None, :],
        "ew1": np.stack([rows(L3("ew1")[e]) for e in range(E)]), "ew2": np.stack([rows(L3("ew2")[e]) for e in range(E)]),
        "eb1": np.stack([cols(L3("eb1")[e]) for e in range(E)], axis=1), "eb1d": np.stack([cols(L3("eb1")[e]) for e in range(E)]),
        "eb2": L3("eb2"),
        "sw1": rows(L3("sw1")), "sb1": cols(L3("sb1")), "sw2": rows(L3("sw2")), "sb2": L3("sb2"),
    }
    arrays = {n: np.ascontiguousarray(a) for n, a in arrays.items()}
    nc = bacc.Bacc("TRN2", target_bir_lowering=False, num_devices=1)
    A = {n: nc.dram_tensor("in_" + n, a.shape, mybir.dt.from_np(a.dtype), kind="ExternalInput").ap() for n, a in arrays.items()}
    out = nc.dram_tensor("out_x", (NB, T, D), fp32, kind="ExternalOutput").ap()
    program(nc, A, out)
    r = run_bass_kernel_spmd(nc, [{"in_" + n: a for n, a in arrays.items()}], core_ids=[0])
    return r.results[0]["out_x"]
```
